# Optimizing a Trainium2 kernel written in Bass

```python
import numpy as np
import jax
import jax.numpy as jnp

def _softmax(x, axis=-1):
    return jax.nn.softmax(x, axis=axis)

def _gelu(x):
    return jax.nn.gelu(x, approximate=True)

def _silu(x):
    return jax.nn.silu(x)

def _sigmoid(x):
    return jax.nn.sigmoid(x)

def _layernorm(x, axis=-1, eps=1e-05):
    m = jnp.mean(x, axis=axis, keepdims=True)
    v = jnp.var(x, axis=axis, keepdims=True)
    return (x - m) / jnp.sqrt(v + eps)

def _scatter_add(tgt, idx, src, axis=0):
    return tgt.at[idx].add(src)

def _segment_sum(src, seg, n):
    return jax.ops.segment_sum(src, seg, n)
kernel_name = 'mk_gps_d2_gnn_r16_7c32ef'

def setup_inputs(seed: int=0):
    np.random.seed(seed)
    _w = jnp.asarray

    def _rec_inputs():
        import jax
        import jax.numpy as jnp
        _gk = jax.random.key(seed)
        x = -0.0002117 + 1 * jax.random.normal(jax.random.fold_in(_gk, 1), (6250, 256), jnp.float32)
        src = jax.random.randint(jax.random.fold_in(_gk, 2), (100000,), 0, 6250, jnp.int32)
        dst = jax.random.randint(jax.random.fold_in(_gk, 3), (100000,), 0, 6250, jnp.int32)
        _o = jnp.argsort(dst, stable=True)
        src = src[_o]
        dst = dst[_o]
        edge_weight = jax.random.uniform(jax.random.fold_in(_gk, 13), (100000,), jnp.float32, 0.0, 1)
        return (x, src, dst, edge_weight)
    x, src, dst, edge_weight = _rec_inputs()

    def _L0_gnn_setup():
        import jax, jax.numpy as jnp
        import numpy as np
        N_NODES = 6250
        N_EDGES = 200000
        IN_DIM = 256
        OUT_DIM = 256
        key = jax.random.key(seed)
        k1, k2, k3, k4, k5 = jax.random.split(key, 5)
        input_feature = jax.random.normal(k1, (N_NODES, IN_DIM), dtype=jnp.float32)
        edge_src = jax.random.randint(k2, (N_EDGES,), 0, N_NODES, dtype=jnp.int32)
        edge_dst = jax.random.randint(k3, (N_EDGES,), 0, N_NODES, dtype=jnp.int32)
        edge_weight = jax.random.uniform(k4, (N_EDGES,), dtype=jnp.float32)
        bound = float(np.sqrt(6.0 / IN_DIM))
        weight = jax.random.uniform(k5, (IN_DIM, OUT_DIM), dtype=jnp.float32, minval=-bound, maxval=bound)
        bias = jnp.zeros((OUT_DIM,), dtype=jnp.float32)
        return {'input_feature': input_feature, 'edge_src': edge_src, 'edge_dst': edge_dst, 'edge_weight': edge_weight, 'weight': weight, 'bias': bias}
    _L0_gnn_all = _L0_gnn_setup()
    _L0_gnn_in = {k: v for k, v in _L0_gnn_all.items() if k in ('weight', 'bias')}
    del _L0_gnn_all

    def _L0_mix_setup():
        import jax, jax.numpy as jnp
        import numpy as np
        D_MODEL = 256
        NHEAD = 8
        D_HEAD = D_MODEL // NHEAD
        DIM_FF = 1024
        B, L = (4, 1024)
        LN_EPS = 1e-05

        def _layernorm(x, g, b):
            mu = jnp.mean(x, axis=-1, keepdims=True)
            var = jnp.mean((x - mu) ** 2, axis=-1, keepdims=True)
            return (x - mu) * jax.lax.rsqrt(var + LN_EPS) * g + b

        def _phi(x):
            return jnp.where(x > 0, x + 1.0, jnp.exp(x))
        key = jax.random.key(seed)
        ks = jax.random.split(key, 16)
        s_in = 1.0 / np.sqrt(D_MODEL)
        s_ff = 1.0 / np.sqrt(DIM_FF)
        inp = {'x': jax.random.normal(ks[0], (B, L, D_MODEL), dtype=jnp.float32), 'Wq': jax.random.normal(ks[1], (D_MODEL, D_MODEL), dtype=jnp.float32) * s_in, 'bq': jnp.zeros((D_MODEL,), jnp.float32), 'Wk': jax.random.normal(ks[2], (D_MODEL, D_MODEL), dtype=jnp.float32) * s_in, 'bk': jnp.zeros((D_MODEL,), jnp.float32), 'Wv': jax.random.normal(ks[3], (D_MODEL, D_MODEL), dtype=jnp.float32) * s_in, 'bv': jnp.zeros((D_MODEL,), jnp.float32), 'Wo': jax.random.normal(ks[4], (D_MODEL, D_MODEL), dtype=jnp.float32) * s_in, 'bo': jnp.zeros((D_MODEL,), jnp.float32), 'W1': jax.random.normal(ks[5], (D_MODEL, DIM_FF), dtype=jnp.float32) * s_in, 'b1': jnp.zeros((DIM_FF,), jnp.float32), 'W2': jax.random.normal(ks[6], (DIM_FF, D_MODEL), dtype=jnp.float32) * s_ff, 'b2': jnp.zeros((D_MODEL,), jnp.float32), 'ln1_g': jnp.ones((D_MODEL,), jnp.float32), 'ln1_b': jnp.zeros((D_MODEL,), jnp.float32), 'ln2_g': jnp.ones((D_MODEL,), jnp.float32), 'ln2_b': jnp.zeros((D_MODEL,), jnp.float32)}
        return inp
    _L0_mix_all = _L0_mix_setup()
    _L0_mix_in = {k: v for k, v in _L0_mix_all.items() if k in ('Wq', 'bq', 'Wk', 'bk', 'Wv', 'bv', 'Wo', 'bo', 'W1', 'b1', 'W2', 'b2', 'ln1_g', 'ln1_b', 'ln2_g', 'ln2_b')}
    del _L0_mix_all

    def _L0_ffn_setup():
        import jax, jax.numpy as jnp
        import numpy as np
        E = 8
        K = 2
        D = 256
        H = 512
        DOUT = 256
        EPS = 1e-05
        key = jax.random.key(seed)
        ks = jax.random.split(key, 9)
        s = 0.02
        return {'x': jax.random.normal(ks[0], (4, 512, D), jnp.float32), 'gamma': 1.0 + 0.05 * jax.random.normal(ks[1], (D,), jnp.float32), 'beta': 0.05 * jax.random.normal(ks[2], (D,), jnp.float32), 'Wr': 0.01 * jax.random.normal(ks[3], (D, E), jnp.float32), 'br': jnp.zeros((E,), jnp.float32), 'W1': s * jax.random.normal(ks[4], (E, D, H), jnp.float32), 'b1': s * jax.random.normal(ks[5], (E, H), jnp.float32), 'W2': s * jax.random.normal(ks[6], (E, H, DOUT), jnp.float32), 'b2': s * jax.random.normal(ks[7], (E, DOUT), jnp.float32)}
    _L0_ffn_all = _L0_ffn_setup()
    _L0_ffn_in = {k: v for k, v in _L0_ffn_all.items() if k in ('gamma', 'beta', 'Wr', 'br', 'W1', 'b1', 'W2', 'b2')}
    del _L0_ffn_all

    def _L1_gnn_setup():
        import jax, jax.numpy as jnp
        import numpy as np
        N = 6250
        E = 100000
        IN = 256
        H = 4
        C = 64
        key = jax.random.key(seed)
        k1, k2, k3, k4, k5, k6 = jax.random.split(key, 6)
        x = jax.random.normal(k1, (N, IN), dtype=jnp.float32)
        edge_index = jax.random.randint(k2, (2, E), 0, N, dtype=jnp.int64)
        W = jax.random.normal(k3, (IN, H * C), dtype=jnp.float32) * (1.0 / np.sqrt(IN))
        att_src = jax.random.normal(k4, (H, C), dtype=jnp.float32) * 0.1
        att_dst = jax.random.normal(k5, (H, C), dtype=jnp.float32) * 0.1
        bias = jax.random.normal(k6, (H * C,), dtype=jnp.float32) * 0.01
        return {'x': x, 'edge_index': edge_index, 'W': W, 'att_src': att_src, 'att_dst': att_dst, 'bias': bias}
    _L1_gnn_all = _L1_gnn_setup()
    _L1_gnn_in = {k: v for k, v in _L1_gnn_all.items() if k in ('W', 'att_src', 'att_dst', 'bias')}
    del _L1_gnn_all

    def _L1_mix_setup():
        import jax, jax.numpy as jnp
        import numpy as np
        C_CURV = 1.0
        MIN_NORM = 1e-15
        BALL_EPS = 1e-05
        ATT_EPS = 1e-15
        DIM = 32

        def _norm(x):
            return jnp.clip(jnp.linalg.norm(x, axis=-1, keepdims=True), MIN_NORM)

        def proj(x, c):
            maxnorm = (1.0 - BALL_EPS) / jnp.sqrt(c)
            n = _norm(x)
            return jnp.where(n > maxnorm, x / n * maxnorm, x)

        def expmap0(u, c):
            sc = jnp.sqrt(c)
            n = _norm(u)
            return jnp.tanh(sc * n) * u / (sc * n)

        def logmap0(p, c):
            sc = jnp.sqrt(c)
            n = _norm(p)
            return jnp.arctanh(jnp.clip(sc * n, -1.0 + 1e-07, 1.0 - 1e-07)) * p / (sc * n)

        def mobius_add(x, y, c):
            x2 = jnp.sum(x * x, -1, keepdims=True)
            y2 = jnp.sum(y * y, -1, keepdims=True)
            xy = jnp.sum(x * y, -1, keepdims=True)
            num = (1 + 2 * c * xy + c * y2) * x + (1 - c * x2) * y
            den = 1 + 2 * c * xy + c * c * x2 * y2
            return num / jnp.clip(den, MIN_NORM)

        def conv1d(x, w, pad, groups=1):
            return jax.lax.conv_general_dilated(x, w, (1,), [(pad, pad)], dimension_numbers=('NCH', 'OIH', 'NCH'), feature_group_count=groups)

        def batchnorm(x, gamma, beta):
            mean = jnp.mean(x, axis=(0, 2), keepdims=True)
            var = jnp.var(x, axis=(0, 2), keepdims=True)
            xn = (x - mean) * jax.lax.rsqrt(var + 1e-05)
            return gamma[None, :, None] * xn + beta[None, :, None]

        def _reference_tuple_inner(x, w_qkv, bn_gamma, bn_beta, w_dw, w_pw, w_res, b_res):
            c = C_CURV
            h = logmap0(proj(x, c), c)
            h = jnp.transpose(h, (1, 2, 0))
            h = conv1d(h, w_qkv, pad=2)
            h = batchnorm(h, bn_gamma, bn_beta)
            h = jax.nn.relu(jnp.transpose(h, (2, 0, 1)))
            qkv = proj(expmap0(h, c), c)
            t = jnp.transpose(logmap0(proj(qkv, c), c), (1, 2, 0))
            s = conv1d(t, w_dw, pad=2, groups=t.shape[1])
            s = conv1d(s, w_pw, pad=0, groups=t.shape[1] // DIM)
            cat = jnp.concatenate([t, s], axis=1)
            ai = proj(expmap0(jnp.transpose(cat, (2, 0, 1)), c), c)
            t2 = logmap0(proj(ai, c), c)
            L, N, C2 = t2.shape
            g = C2 // (3 * DIM)
            qkv3 = jnp.transpose(t2, (1, 2, 0)).reshape(N, g, 3 * DIM, L)
            q, k, v = jnp.split(qkv3, 3, axis=2)
            q = jax.nn.relu(q)
            k = jax.nn.relu(k)
            vk = jnp.einsum('ngdl,ngel->ngde', v, k)
            out = jnp.einsum('ngde,ngdl->ngdl', vk, q)
            out = out / (jnp.sum(v, -1, keepdims=True) + ATT_EPS)
            out = jnp.transpose(out.reshape(N, g * DIM, L), (2, 0, 1))
            fx_h = proj(expmap0(out, c), c)
            ft = jnp.transpose(logmap0(proj(fx_h, c), c), (1, 2, 0))
            ft = conv1d(ft, w_res, pad=0) + b_res[None, :, None]
            fx = proj(expmap0(jnp.transpose(ft, (2, 0, 1)), c), c)
            residual = mobius_add(fx, x, c)
            return (fx, residual)
        key = jax.random.key(seed)
        ks = jax.random.split(key, 6)
        L, N, C, TD = (128, 16, 256, 256)
        x = jax.random.normal(ks[0], (L, N, C), jnp.float32) * 0.05
        w_qkv = jax.random.normal(ks[1], (3 * TD, C, 5), jnp.float32) / np.sqrt(C * 5)
        bn_gamma = jnp.ones((3 * TD,), jnp.float32)
        bn_beta = jnp.zeros((3 * TD,), jnp.float32)
        w_dw = jax.random.normal(ks[2], (3 * TD, 1, 5), jnp.float32) / np.sqrt(5.0)
        w_pw = jax.random.normal(ks[3], (3 * TD, DIM, 1), jnp.float32) / np.sqrt(DIM)
        w_res = jax.random.normal(ks[4], (C, 2 * TD, 1), jnp.float32) / np.sqrt(2 * TD)
        b_res = jnp.zeros((C,), jnp.float32)
        return {'x': x, 'w_qkv': w_qkv, 'bn_gamma': bn_gamma, 'bn_beta': bn_beta, 'w_dw': w_dw, 'w_pw': w_pw, 'w_res': w_res, 'b_res': b_res}
    _L1_mix_all = _L1_mix_setup()
    _L1_mix_in = {k: v for k, v in _L1_mix_all.items() if k in ('w_qkv', 'bn_gamma', 'bn_beta', 'w_dw', 'w_pw', 'w_res', 'b_res')}
    del _L1_mix_all

    def _L1_ffn_setup():
        import jax, jax.numpy as jnp
        import numpy as np
        B, A = (256, 8)
        IN, OUT = (256, 256)
        SH1, SH2 = (256, 128)
        EH1, EH2 = (128, 64)
        E, TOPK = (4, 2)

        def _shared_mlp(x, W1, b1, W2, b2, W3, b3):
            h = jax.nn.relu(x @ W1 + b1)
            h = jax.nn.relu(h @ W2 + b2)
            return h @ W3 + b3

        def _experts_mlp(x, eW1, eb1, eW2, eb2, eW3, eb3):
            h = jax.nn.relu(jnp.einsum('baf,efh->ebah', x, eW1) + eb1[:, None, None, :])
            h = jax.nn.relu(jnp.einsum('ebah,ehg->ebag', h, eW2) + eb2[:, None, None, :])
            o = jnp.einsum('ebag,ego->ebao', h, eW3) + eb3[:, None, None, :]
            return jnp.moveaxis(o, 0, -1)
        key = jax.random.key(seed)
        ks = jax.random.split(key, 16)
        s = 0.05
        return {'x': jax.random.normal(ks[0], (B, A, IN), jnp.float32), 'sW1': jax.random.normal(ks[1], (IN, SH1), jnp.float32) * s, 'sb1': jnp.zeros((SH1,), jnp.float32), 'sW2': jax.random.normal(ks[2], (SH1, SH2), jnp.float32) * s, 'sb2': jnp.zeros((SH2,), jnp.float32), 'sW3': jax.random.normal(ks[3], (SH2, OUT), jnp.float32) * s, 'sb3': jnp.zeros((OUT,), jnp.float32), 'eW1': jax.random.normal(ks[4], (E, IN, EH1), jnp.float32) * s, 'eb1': jnp.zeros((E, EH1), jnp.float32), 'eW2': jax.random.normal(ks[5], (E, EH1, EH2), jnp.float32) * s, 'eb2': jnp.zeros((E, EH2), jnp.float32), 'eW3': jax.random.normal(ks[6], (E, EH2, OUT), jnp.float32) * s, 'eb3': jnp.zeros((E, OUT), jnp.float32), 'gW': jax.random.normal(ks[7], (IN, E), jnp.float32) * s, 'gb': jnp.zeros((E,), jnp.float32)}
    _L1_ffn_all = _L1_ffn_setup()
    _L1_ffn_in = {k: v for k, v in _L1_ffn_all.items() if k in ('sW1', 'sb1', 'sW2', 'sb2', 'sW3', 'sb3', 'eW1', 'eb1', 'eW2', 'eb2', 'eW3', 'eb3', 'gW', 'gb')}
    del _L1_ffn_all
    return {'x': x, 'src': src, 'dst': dst, 'edge_weight': edge_weight, 'L0_gnn_weight': _L0_gnn_in['weight'], 'L0_gnn_bias': _L0_gnn_in['bias'], 'L0_mix_Wq': _L0_mix_in['Wq'], 'L0_mix_bq': _L0_mix_in['bq'], 'L0_mix_Wk': _L0_mix_in['Wk'], 'L0_mix_bk': _L0_mix_in['bk'], 'L0_mix_Wv': _L0_mix_in['Wv'], 'L0_mix_bv': _L0_mix_in['bv'], 'L0_mix_Wo': _L0_mix_in['Wo'], 'L0_mix_bo': _L0_mix_in['bo'], 'L0_mix_W1': _L0_mix_in['W1'], 'L0_mix_b1': _L0_mix_in['b1'], 'L0_mix_W2': _L0_mix_in['W2'], 'L0_mix_b2': _L0_mix_in['b2'], 'L0_mix_ln1_g': _L0_mix_in['ln1_g'], 'L0_mix_ln1_b': _L0_mix_in['ln1_b'], 'L0_mix_ln2_g': _L0_mix_in['ln2_g'], 'L0_mix_ln2_b': _L0_mix_in['ln2_b'], 'L0_ffn_gamma': _L0_ffn_in['gamma'], 'L0_ffn_beta': _L0_ffn_in['beta'], 'L0_ffn_Wr': _L0_ffn_in['Wr'], 'L0_ffn_br': _L0_ffn_in['br'], 'L0_ffn_W1': _L0_ffn_in['W1'], 'L0_ffn_b1': _L0_ffn_in['b1'], 'L0_ffn_W2': _L0_ffn_in['W2'], 'L0_ffn_b2': _L0_ffn_in['b2'], 'L1_gnn_W': _L1_gnn_in['W'], 'L1_gnn_att_src': _L1_gnn_in['att_src'], 'L1_gnn_att_dst': _L1_gnn_in['att_dst'], 'L1_gnn_bias': _L1_gnn_in['bias'], 'L1_mix_w_qkv': _L1_mix_in['w_qkv'], 'L1_mix_bn_gamma': _L1_mix_in['bn_gamma'], 'L1_mix_bn_beta': _L1_mix_in['bn_beta'], 'L1_mix_w_dw': _L1_mix_in['w_dw'], 'L1_mix_w_pw': _L1_mix_in['w_pw'], 'L1_mix_w_res': _L1_mix_in['w_res'], 'L1_mix_b_res': _L1_mix_in['b_res'], 'L1_ffn_sW1': _L1_ffn_in['sW1'], 'L1_ffn_sb1': _L1_ffn_in['sb1'], 'L1_ffn_sW2': _L1_ffn_in['sW2'], 'L1_ffn_sb2': _L1_ffn_in['sb2'], 'L1_ffn_sW3': _L1_ffn_in['sW3'], 'L1_ffn_sb3': _L1_ffn_in['sb3'], 'L1_ffn_eW1': _L1_ffn_in['eW1'], 'L1_ffn_eb1': _L1_ffn_in['eb1'], 'L1_ffn_eW2': _L1_ffn_in['eW2'], 'L1_ffn_eb2': _L1_ffn_in['eb2'], 'L1_ffn_eW3': _L1_ffn_in['eW3'], 'L1_ffn_eb3': _L1_ffn_in['eb3'], 'L1_ffn_gW': _L1_ffn_in['gW'], 'L1_ffn_gb': _L1_ffn_in['gb']}

def reference(x, src, dst, edge_weight, L0_gnn_weight, L0_gnn_bias, L0_mix_Wq, L0_mix_bq, L0_mix_Wk, L0_mix_bk, L0_mix_Wv, L0_mix_bv, L0_mix_Wo, L0_mix_bo, L0_mix_W1, L0_mix_b1, L0_mix_W2, L0_mix_b2, L0_mix_ln1_g, L0_mix_ln1_b, L0_mix_ln2_g, L0_mix_ln2_b, L0_ffn_gamma, L0_ffn_beta, L0_ffn_Wr, L0_ffn_br, L0_ffn_W1, L0_ffn_b1, L0_ffn_W2, L0_ffn_b2, L1_gnn_W, L1_gnn_att_src, L1_gnn_att_dst, L1_gnn_bias, L1_mix_w_qkv, L1_mix_bn_gamma, L1_mix_bn_beta, L1_mix_w_dw, L1_mix_w_pw, L1_mix_w_res, L1_mix_b_res, L1_ffn_sW1, L1_ffn_sb1, L1_ffn_sW2, L1_ffn_sb2, L1_ffn_sW3, L1_ffn_sb3, L1_ffn_eW1, L1_ffn_eb1, L1_ffn_eW2, L1_ffn_eb2, L1_ffn_eW3, L1_ffn_eb3, L1_ffn_gW, L1_ffn_gb):
    import jax
    import jax.numpy as jnp

    def _L0_gnn_ref(input_feature, edge_src, edge_dst, edge_weight, weight, bias):
        import jax, jax.numpy as jnp
        import numpy as np
        N_NODES = 6250
        N_EDGES = 200000
        IN_DIM = 256
        OUT_DIM = 256
        support = input_feature @ weight
        msgs = support[edge_src] * edge_weight[:, None]
        output = jax.ops.segment_sum(msgs, edge_dst, num_segments=N_NODES)
        output = output + bias
        return output

    def _L0_mix_ref(x, Wq, bq, Wk, bk, Wv, bv, Wo, bo, W1, b1, W2, b2, ln1_g, ln1_b, ln2_g, ln2_b):
        import jax, jax.numpy as jnp
        import numpy as np
        D_MODEL = 256
        NHEAD = 8
        D_HEAD = D_MODEL // NHEAD
        DIM_FF = 1024
        B, L = (4, 1024)
        LN_EPS = 1e-05

        def _layernorm(x, g, b):
            mu = jnp.mean(x, axis=-1, keepdims=True)
            var = jnp.mean((x - mu) ** 2, axis=-1, keepdims=True)
            return (x - mu) * jax.lax.rsqrt(var + LN_EPS) * g + b

        def _phi(x):
            return jnp.where(x > 0, x + 1.0, jnp.exp(x))
        Bq, Lq, _ = x.shape
        q = (x @ Wq + bq).reshape(Bq, Lq, NHEAD, D_HEAD)
        k = (x @ Wk + bk).reshape(Bq, Lq, NHEAD, D_HEAD)
        v = (x @ Wv + bv).reshape(Bq, Lq, NHEAD, D_HEAD)
        q_phi = _phi(q)
        k_phi = _phi(k)
        kv = jnp.einsum('blhd,blhe->bhde', k_phi, v)
        k_sum = k_phi.sum(axis=1)
        z = 1.0 / (jnp.einsum('blhd,bhd->blh', q_phi, k_sum) + 1e-06)
        out = jnp.einsum('blhd,bhde,blh->blhe', q_phi, kv, z)
        out = out.reshape(Bq, Lq, D_MODEL) @ Wo + bo
        x = _layernorm(x + out, ln1_g, ln1_b)
        ff = jax.nn.relu(x @ W1 + b1) @ W2 + b2
        x = _layernorm(x + ff, ln2_g, ln2_b)
        return x

    def _L0_ffn_ref(x, gamma, beta, Wr, br, W1, b1, W2, b2):
        import jax, jax.numpy as jnp
        import numpy as np
        E = 8
        K = 2
        D = 256
        H = 512
        DOUT = 256
        EPS = 1e-05
        mu = jnp.mean(x, axis=-1, keepdims=True)
        var = jnp.mean(jnp.square(x - mu), axis=-1, keepdims=True)
        xn = (x - mu) * jax.lax.rsqrt(var + EPS) * gamma + beta
        logits = jnp.einsum('bsd,de->bse', xn, Wr) + br
        top_vals, top_idx = jax.lax.top_k(logits, K)
        w = jax.nn.softmax(top_vals, axis=-1)
        w_full = jnp.einsum('bsk,bske->bse', w, jax.nn.one_hot(top_idx, E, dtype=w.dtype))
        y = jnp.zeros(x.shape[:-1] + (DOUT,), x.dtype)
        for e in range(E):
            h = jax.nn.gelu(jnp.einsum('bsd,dh->bsh', xn, W1[e]) + b1[e], approximate=False)
            y_e = jnp.einsum('bsh,hd->bsd', h, W2[e]) + b2[e]
            y = y + y_e * w_full[..., e, None]
        return y

    def _L1_gnn_ref(x, edge_index, W, att_src, att_dst, bias):
        import jax, jax.numpy as jnp
        import numpy as np
        N = 6250
        E = 100000
        IN = 256
        H = 4
        C = 64
        n = x.shape[0]
        loops = jnp.arange(n, dtype=edge_index.dtype)
        src = jnp.concatenate([edge_index[0], loops])
        dst = jnp.concatenate([edge_index[1], loops])
        xp = (x @ W).reshape(n, H, C)
        a_src = jnp.einsum('nhc,hc->nh', xp, att_src)
        a_dst = jnp.einsum('nhc,hc->nh', xp, att_dst)
        alpha = jax.nn.leaky_relu(a_src[src] + a_dst[dst], negative_slope=0.2)
        amax = jax.ops.segment_max(alpha, dst, num_segments=n)
        amax = jnp.where(jnp.isfinite(amax), amax, 0.0)
        ex = jnp.exp(alpha - amax[dst])
        denom = jax.ops.segment_sum(ex, dst, num_segments=n)
        w = ex / denom[dst]
        msg = xp[src] * w[..., None]
        agg = jax.ops.segment_sum(msg, dst, num_segments=n)
        out = agg.reshape(n, H * C) + bias
        return jax.nn.elu(out)

    def _L1_mix_ref(x, w_qkv, bn_gamma, bn_beta, w_dw, w_pw, w_res, b_res):
        import jax, jax.numpy as jnp
        import numpy as np
        C_CURV = 1.0
        MIN_NORM = 1e-15
        BALL_EPS = 1e-05
        ATT_EPS = 1e-15
        DIM = 32

        def _norm(x):
            return jnp.clip(jnp.linalg.norm(x, axis=-1, keepdims=True), MIN_NORM)

        def proj(x, c):
            maxnorm = (1.0 - BALL_EPS) / jnp.sqrt(c)
            n = _norm(x)
            return jnp.where(n > maxnorm, x / n * maxnorm, x)

        def expmap0(u, c):
            sc = jnp.sqrt(c)
            n = _norm(u)
            return jnp.tanh(sc * n) * u / (sc * n)

        def logmap0(p, c):
            sc = jnp.sqrt(c)
            n = _norm(p)
            return jnp.arctanh(jnp.clip(sc * n, -1.0 + 1e-07, 1.0 - 1e-07)) * p / (sc * n)

        def mobius_add(x, y, c):
            x2 = jnp.sum(x * x, -1, keepdims=True)
            y2 = jnp.sum(y * y, -1, keepdims=True)
            xy = jnp.sum(x * y, -1, keepdims=True)
            num = (1 + 2 * c * xy + c * y2) * x + (1 - c * x2) * y
            den = 1 + 2 * c * xy + c * c * x2 * y2
            return num / jnp.clip(den, MIN_NORM)

        def conv1d(x, w, pad, groups=1):
            return jax.lax.conv_general_dilated(x, w, (1,), [(pad, pad)], dimension_numbers=('NCH', 'OIH', 'NCH'), feature_group_count=groups)

        def batchnorm(x, gamma, beta):
            mean = jnp.mean(x, axis=(0, 2), keepdims=True)
            var = jnp.var(x, axis=(0, 2), keepdims=True)
            xn = (x - mean) * jax.lax.rsqrt(var + 1e-05)
            return gamma[None, :, None] * xn + beta[None, :, None]

        def _reference_tuple_inner(x, w_qkv, bn_gamma, bn_beta, w_dw, w_pw, w_res, b_res):
            c = C_CURV
            h = logmap0(proj(x, c), c)
            h = jnp.transpose(h, (1, 2, 0))
            h = conv1d(h, w_qkv, pad=2)
            h = batchnorm(h, bn_gamma, bn_beta)
            h = jax.nn.relu(jnp.transpose(h, (2, 0, 1)))
            qkv = proj(expmap0(h, c), c)
            t = jnp.transpose(logmap0(proj(qkv, c), c), (1, 2, 0))
            s = conv1d(t, w_dw, pad=2, groups=t.shape[1])
            s = conv1d(s, w_pw, pad=0, groups=t.shape[1] // DIM)
            cat = jnp.concatenate([t, s], axis=1)
            ai = proj(expmap0(jnp.transpose(cat, (2, 0, 1)), c), c)
            t2 = logmap0(proj(ai, c), c)
            L, N, C2 = t2.shape
            g = C2 // (3 * DIM)
            qkv3 = jnp.transpose(t2, (1, 2, 0)).reshape(N, g, 3 * DIM, L)
            q, k, v = jnp.split(qkv3, 3, axis=2)
            q = jax.nn.relu(q)
            k = jax.nn.relu(k)
            vk = jnp.einsum('ngdl,ngel->ngde', v, k)
            out = jnp.einsum('ngde,ngdl->ngdl', vk, q)
            out = out / (jnp.sum(v, -1, keepdims=True) + ATT_EPS)
            out = jnp.transpose(out.reshape(N, g * DIM, L), (2, 0, 1))
            fx_h = proj(expmap0(out, c), c)
            ft = jnp.transpose(logmap0(proj(fx_h, c), c), (1, 2, 0))
            ft = conv1d(ft, w_res, pad=0) + b_res[None, :, None]
            fx = proj(expmap0(jnp.transpose(ft, (2, 0, 1)), c), c)
            residual = mobius_add(fx, x, c)
            return (fx, residual)
        return _reference_tuple_inner(x, w_qkv, bn_gamma, bn_beta, w_dw, w_pw, w_res, b_res)[0]

    def _L1_ffn_ref(x, sW1, sb1, sW2, sb2, sW3, sb3, eW1, eb1, eW2, eb2, eW3, eb3, gW, gb):
        import jax, jax.numpy as jnp
        import numpy as np
        B, A = (256, 8)
        IN, OUT = (256, 256)
        SH1, SH2 = (256, 128)
        EH1, EH2 = (128, 64)
        E, TOPK = (4, 2)

        def _shared_mlp(x, W1, b1, W2, b2, W3, b3):
            h = jax.nn.relu(x @ W1 + b1)
            h = jax.nn.relu(h @ W2 + b2)
            return h @ W3 + b3

        def _experts_mlp(x, eW1, eb1, eW2, eb2, eW3, eb3):
            h = jax.nn.relu(jnp.einsum('baf,efh->ebah', x, eW1) + eb1[:, None, None, :])
            h = jax.nn.relu(jnp.einsum('ebah,ehg->ebag', h, eW2) + eb2[:, None, None, :])
            o = jnp.einsum('ebag,ego->ebao', h, eW3) + eb3[:, None, None, :]
            return jnp.moveaxis(o, 0, -1)
        all_out = _experts_mlp(x, eW1, eb1, eW2, eb2, eW3, eb3)
        shared = _shared_mlp(x, sW1, sb1, sW2, sb2, sW3, sb3)
        gates = jax.nn.softmax(x @ gW + gb, axis=-1)
        topv, topi = jax.lax.top_k(gates, TOPK)
        topw = jax.nn.softmax(topv, axis=-1)
        sel = jnp.take_along_axis(all_out, topi[:, :, None, :], axis=-1)
        gated = jnp.sum(sel * topw[:, :, None, :], axis=-1)
        return shared + gated
    edge_index = jnp.stack([src, dst])
    xn = _layernorm(x, axis=-1)
    x = x + _L0_gnn_ref(xn, src, dst, edge_weight, L0_gnn_weight, L0_gnn_bias) + _L0_mix_ref(xn[None], L0_mix_Wq, L0_mix_bq, L0_mix_Wk, L0_mix_bk, L0_mix_Wv, L0_mix_bv, L0_mix_Wo, L0_mix_bo, L0_mix_W1, L0_mix_b1, L0_mix_W2, L0_mix_b2, L0_mix_ln1_g, L0_mix_ln1_b, L0_mix_ln2_g, L0_mix_ln2_b)[0]
    x = x + _L0_ffn_ref(_layernorm(x, axis=-1)[None], L0_ffn_gamma, L0_ffn_beta, L0_ffn_Wr, L0_ffn_br, L0_ffn_W1, L0_ffn_b1, L0_ffn_W2, L0_ffn_b2)[0]
    xn = _layernorm(x, axis=-1)
    x = x + _L1_gnn_ref(xn, edge_index, L1_gnn_W, L1_gnn_att_src, L1_gnn_att_dst, L1_gnn_bias) + _L1_mix_ref(xn[None], L1_mix_w_qkv, L1_mix_bn_gamma, L1_mix_bn_beta, L1_mix_w_dw, L1_mix_w_pw, L1_mix_w_res, L1_mix_b_res)[0]
    x = x + _L1_ffn_ref(_layernorm(x, axis=-1)[None], L1_ffn_sW1, L1_ffn_sb1, L1_ffn_sW2, L1_ffn_sb2, L1_ffn_sW3, L1_ffn_sb3, L1_ffn_eW1, L1_ffn_eb1, L1_ffn_eW2, L1_ffn_eb2, L1_ffn_eW3, L1_ffn_eb3, L1_ffn_gW, L1_ffn_gb)[0]
    return x

_drawn_inputs = setup_inputs


def setup_inputs(seed=0):
    import zlib

    import numpy as np

    out = dict(_drawn_inputs(seed))
    spreads = {'L0_gnn_bias': (0.0, 0.289),
     'L0_mix_bq': (0.0, 2.0),
     'L0_mix_bk': (0.0, 2.0),
     'L0_mix_bv': (0.0, 0.28),
     'L0_mix_bo': (0.0, 0.297),
     'L0_mix_b1': (0.0, 0.495),
     'L0_mix_b2': (0.0, 0.35),
     'L0_mix_ln1_g': (1.0, 0.2),
     'L0_mix_ln1_b': (0.0, 0.296),
     'L0_mix_ln2_g': (1.0, 0.2),
     'L0_mix_ln2_b': (0.0, 0.309),
     'L0_ffn_br': (0.0, 0.542),
     'L1_mix_bn_gamma': (1.0, 0.6),
     'L1_mix_bn_beta': (0.0, 2.0),
     'L1_mix_b_res': (0.0, 2.0),
     'L1_ffn_sb1': (0.0, 2.0),
     'L1_ffn_sb2': (0.0, 2.0),
     'L1_ffn_sb3': (0.0, 1.054),
     'L1_ffn_eb1': (0.0, 0.8),
     'L1_ffn_eb2': (0.0, 0.8),
     'L1_ffn_eb3': (0.0, 1.445),
     'L1_ffn_gb': (0.0, 0.8)}
    factors = {'L0_mix_Wq': 8.0,
     'L0_mix_Wk': 8.0,
     'L0_mix_Wv': 8.0,
     'L0_ffn_gamma': 8.0,
     'L0_ffn_beta': 8.0,
     'L0_ffn_Wr': 5.57,
     'L0_ffn_W1': 3.959,
     'L0_ffn_b1': 8.0,
     'L0_ffn_W2': 3.843,
     'L0_ffn_b2': 21.837,
     'L1_gnn_att_dst': 17.504,
     'L1_gnn_bias': 33.652,
     'L1_mix_w_qkv': 26.237,
     'L1_mix_w_dw': 59.292,
     'L1_mix_w_pw': 40.183,
     'L1_mix_w_res': 17.063,
     'L1_ffn_eW1': 4.829,
     'L1_ffn_eW2': 4.252,
     'L1_ffn_eW3': 3.354,
     'L1_ffn_gW': 3.183,
     'L1_ffn_sW1': 5.38,
     'L1_ffn_sW2': 3.914}
    for name, (base, spread) in spreads.items():
        noise = np.random.default_rng([zlib.crc32(name.encode()), seed]).standard_normal(out[name].shape)
        drawn = base * np.exp(spread * noise) if base else spread * noise
        out[name] = jnp.asarray(drawn.astype(out[name].dtype))
    for name, factor in factors.items():
        out[name] = (out[name] * factor).astype(out[name].dtype)
    return out
```

```python
import math
from contextlib import ExitStack

import numpy as np

import concourse.bass as bass
from concourse import mybir

F32 = mybir.dt.float32
I32 = mybir.dt.int32
U32 = mybir.dt.uint32
BF16 = mybir.dt.bfloat16
ALU = mybir.AluOpType
ACT = mybir.ActivationFunctionType
AX = mybir.AxisListType

P = 128
N = 6250
D = 256
T = (N + P - 1) // P
NP = T * P
PAIRS = (T - 1) // 2
EDGES = 100000
STEPS = 18
HALF = STEPS // 2
CAP = STEPS * P
EPAD = 100096 + CAP
EC = 100096 // P
GROUP = 7
HEADS = 8
FF = 1024
NEXP, HID = 8, 512
CQ = 768
TBL = D + 4
BIG = 1.0e30
EPS = 1e-5
MAXNORM = float(np.float32(1.0 - 1e-5))
ATANH_MAX = math.atanh(MAXNORM)
NODES_OF_EDGES_PAD = 1 << 20


class Ctx:
    pass


def row(ap, parts=P):
    return ap.unsqueeze(0).broadcast_to([parts, ap.shape[0]])


def load_columns(eng, out, vector):
    return eng.dma_start(out, vector.rearrange("(c p) -> p c", p=P), allow_slow_non_contiguous=True)


def newton_rsqrt(dve, out, x, tmp):
    dve.tensor_scalar(out.bitcast(I32), x.bitcast(I32), -0.5, 1597463007.0, ALU.mult, ALU.add)
    dve.drain()
    for _ in range(3):
        if x.shape[-1] == 1:
            dve.scalar_tensor_tensor(tmp, out, x, out, ALU.mult, ALU.mult)
        else:
            dve.tensor_tensor(tmp, out, x, ALU.mult)
            dve.drain()
            dve.tensor_tensor(tmp, tmp, out, ALU.mult)
        dve.drain()
        dve.tensor_scalar(tmp, tmp, -0.5, 1.5, ALU.mult, ALU.add)
        dve.drain()
        dve.tensor_tensor(out, out, tmp, ALU.mult)
        dve.drain()


def normalise(dve, out, x, stats, mv, rs, tmp, wait_for_out=None):
    dve.bn_stats(stats, x)
    dve.drain()
    dve.bn_aggr(mv, stats)
    dve.drain()
    dve.tensor_scalar(mv[:, 1:2], mv[:, 1:2], EPS, None, ALU.add)
    dve.drain()
    newton_rsqrt(dve, rs, mv[:, 1:2], tmp)
    if wait_for_out:
        wait_for_out()
    dve.tensor_scalar(out, x, mv[:, 0:1], rs, ALU.subtract, ALU.mult)


def uses_before(t, b):
    return t * 8 - 8 * b


def over_pairs(eng, step, first=0, count=T):
    with eng.Fori(0, count // 2) as i:
        step(i * 2 + first, 0)
        step(i * 2 + (first + 1), 1)
    if count % 2:
        step(first + count - 1, (count - 1) % 2)


def build_edge_tables(nc, g):
    with ExitStack() as ctx:
        sb = lambda n, s, d=F32: ctx.enter_context(nc.sbuf_tensor(n, s, d))
        sem = lambda n: ctx.enter_context(nc.semaphore(n))
        dst_i = sb("et_dst_i", [P, EC], I32)
        dst_f = sb("et_dst_f", [P, EC])
        below = sb("et_below", [P, EC])
        thresholds = sb("et_thr", [P, T])
        counts = sb("et_counts", [P, T])
        ones = sb("et_ones", [P, P])
        rows_i = sb("et_rows_i", [STEPS * GROUP, 2, P], I32)
        rows_f = sb("et_rows_f", [STEPS * GROUP, 5, P])
        tile_base = sb("et_base", [P, T])
        cols = sb("et_cols", [P, 2, STEPS * GROUP])
        ends = ctx.enter_context(nc.psum_tensor("et_ends", [P, T], F32))
        turned = ctx.enter_context(nc.psum_tensor("et_turned", [P, 5, P], F32))
        loaded, made, counted, summed = sem("et_loaded"), sem("et_made"), sem("et_counted"), sem("et_summed")
        starts_ready, rows_in, rows_ready, turned_ready, taken = sem("et_starts"), sem("et_rows_in"), sem("et_rows_ready"), sem("et_turned_s"), sem("et_taken")
        GW = STEPS * GROUP
        block = ctx.enter_context(nc.Block())

        @block.sync
        def _(sp):
            sp.dma_start(dst_i[:, :], g.dst.rearrange("(n) -> n")[0:P * EC].rearrange("(p c) -> p c", p=P)).then_inc(loaded, 16)
            sp.wait_ge(starts_ready, 1)
            with sp.Fori(0, T // GROUP) as m:
                sp.wait_ge(taken, m)
                for k in range(GROUP):
                    e = sp.value_load(g.starts[0:1, bass.ds(m * GROUP + k, 1)], min_val=0, max_val=EDGES)
                    part = slice(k * STEPS, (k + 1) * STEPS)
                    sp.dma_start(rows_i[part, 0, :], g.src[bass.ds(e, CAP)].rearrange("(j p) -> j p", p=P)).then_inc(rows_in, 16)
                    sp.dma_start(rows_i[part, 1, :], g.dst[bass.ds(e, CAP)].rearrange("(j p) -> j p", p=P)).then_inc(rows_in, 16)
                    sp.dma_start(rows_f[part, 2, :], g.ew[bass.ds(e, CAP)].rearrange("(j p) -> j p", p=P)).then_inc(rows_in, 16)

        @block.gpsimd
        def _(pool):
            pool.memset(ones[:, :], 1.0)
            pool.iota(thresholds[:, :], [[P, T]], base=P, channel_multiplier=0, allow_small_or_imprecise_dtypes=True)
            pool.iota(tile_base[:, :], [[P, T]], base=0, channel_multiplier=0, allow_small_or_imprecise_dtypes=True)
            pool.iota(g.node[:, :], [[1, P]], base=0, channel_multiplier=0, allow_small_or_imprecise_dtypes=True)
            pool.memset(g.ident[:, :], 1.0)
            pool.drain()
            pool.affine_select(out=g.ident[:, :], in_=g.ident[:, :], compare_op=ALU.is_equal, fill=0.0,
                               base=0, pattern=[[-1, P]], channel_multiplier=1)
            pool.drain()
            pool.memset(g.scratch1[:, :], 0.0).then_inc(made, 1)

        @block.vector
        def _(dve):
            dve.wait_ge(loaded, 16)
            dve.tensor_copy(dst_f[:, :], dst_i[:, :])
            dve.wait_ge(made, 1)
            dve.drain()
            with dve.Fori(0, T) as t:
                dve.tensor_scalar(below[:, :], dst_f[:, :], thresholds[:, bass.ds(t, 1)], 0.0, ALU.is_lt, ALU.add,
                                  accum_out=counts[:, bass.ds(t, 1)])
                dve.drain()
            dve.memset(g.starts[:, 0:1], 0).then_inc(counted, 1)
            dve.wait_ge(summed, 1)
            dve.tensor_copy(g.starts[:, 1:T + 1], ends[:, :]).then_inc(starts_ready, 1)
            with dve.Fori(0, T // GROUP) as m:
                dve.wait_ge(rows_in, (m + 1) * (48 * GROUP))
                dve.tensor_copy(rows_f[:, 0:2, :], rows_i[:, :, :])
                dve.drain()
                dve.memset(rows_f[:, 3:4, P - 1:P], 1.0)
                dve.memset(rows_f[:, 4:5, 0:1], -BIG)
                dve.tensor_tensor(rows_f[:, 3, 0:P - 1], rows_f[:, 1, 0:P - 1], rows_f[:, 1, 1:P], ALU.not_equal)
                dve.drain()
                dve.tensor_scalar(rows_f[:, 4, 1:P], rows_f[:, 3, 0:P - 1], -BIG, None, ALU.mult).then_inc(rows_ready, 1)
                dve.wait_ge(turned_ready, m + 1)
                at = bass.ds(m * GW, GW)
                dve.tensor_copy(cols[:, :, :], turned[:, 0:2, 0:GW])
                dve.tensor_copy(g.e_weight[:, at], turned[:, 2, 0:GW])
                dve.tensor_copy(g.e_last[:, at], turned[:, 3, 0:GW])
                dve.tensor_copy(g.e_first[:, at], turned[:, 4, 0:GW])
                dve.drain()
                dve.tensor_copy(g.e_src[:, at], cols[:, 0, :])
                dve.tensor_tensor(g.e_dst[:, at].rearrange("p (k j) -> p k j", k=GROUP), cols[:, 1, :].rearrange("p (k j) -> p k j", k=GROUP),
                                  tile_base[:, bass.ds(m * GROUP, GROUP)].unsqueeze(2).broadcast_to([P, GROUP, STEPS]), ALU.subtract)
                dve.drain()
                dve.memset(g.scratch1[:, 0:1], 0.0).then_inc(taken, 1)
                dve.drain()

        @block.tensor
        def _(pe):
            pe.wait_ge(counted, 1)
            pe.wait_ge(made, 1)
            pe.matmul(ends[:, :], ones[:, :], counts[:, :], start=True, stop=True).then_inc(summed, 1)
            with pe.Fori(0, T // GROUP) as m:
                pe.wait_ge(rows_ready, m + 1)
                pe.wait_ge(taken, m)
                for k in range(5):
                    last = pe.transpose(turned[:, k, 0:GW], rows_f[:, k, :], g.ident[0:GW, 0:GW])
                last.then_inc(turned_ready, 1)


def layer0_projections(nc, g):
    with ExitStack() as ctx:
        sb = lambda n, s, d=F32: ctx.enter_context(nc.sbuf_tensor(n, s, d))
        sem = lambda n: ctx.enter_context(nc.semaphore(n))
        def ps(n, s):
            flat = ctx.enter_context(nc.psum_tensor(n, [P, 512], F32))[:, 0:math.prod(s[1:])]
            return flat.rearrange("p (a n) -> p a n", a=s[1]) if len(s) == 3 else flat

        w_kvs = sb("a_w_kvs", [P, 2, 3 * D])
        w_q = sb("a_w_q", [P, 2, D])
        b_k, b_v, b_q = sb("a_bk", [P, D]), sb("a_bv", [P, D]), sb("a_bq", [P, 2])
        valid = sb("a_valid", [P, T])
        x_in = sb("a_x", [P, 2, D])
        stats, mv, rs, tmp = sb("a_stats", [P, 2, 6]), sb("a_mv", [P, 2, 2]), sb("a_rs", [P, 2]), sb("a_tmp", [P, 2])
        xt = sb("a_xt", [P, 2, 2, P])
        k_lin, k_neg, k_phi = sb("a_klin", [P, D]), sb("a_kneg", [P, 2, D]), sb("a_kphi", [P, 2, D])
        v_one = sb("a_vone", [P, 2, 2, P + 1])
        sup = sb("a_sup", [P, 2, D])
        q_neg = sb("a_qneg", [P, 2, D])
        q_pos = sb("a_qpos", [P, 2, D])
        kv_sum = sb("a_kvsum", [P, 2, P + 1])
        turned = ps("a_turned", [P, 2, P])
        kv_ps = ps("a_kvps", [P, 2 * D])
        sup_ps = ps("a_supps", [P, D])
        q_ps = ps("a_qps", [P, D])
        sum_ps = ps("a_sumps", [P, 2, P + 1])
        weights_in, valid_made = sem("a_weights"), sem("a_valid_s")
        x_loaded = [sem("a_xl0"), sem("a_xl1")]
        sup_stored = [sem("a_ss0"), sem("a_ss1")]
        x_free, xt_free = sem("a_x_free"), sem("a_xt_free")
        xn_ready, x_turned, xt_ready = sem("a_xn"), sem("a_turned_s"), sem("a_xtr")
        projected, lin_ready, exp_ready, phi_ready, sums_ready, sup_ready, summed_up, q_done = (sem("a_" + s) for s in ("proj", "lin", "exp", "phi", "sums", "sup_s", "up", "qd"))
        block = ctx.enter_context(nc.Block())

        @block.sync
        def _(sp):
            for k, w in enumerate((g.w["L0_mix_Wk"], g.w["L0_mix_Wv"], g.w["L0_gnn_weight"])):
                sp.dma_start(w_kvs[:, :, k * D:(k + 1) * D], w.rearrange("(c p) n -> p c n", p=P)).then_inc(weights_in, 16)
            sp.dma_start(w_q[:, :, :], g.w["L0_mix_Wq"].rearrange("(c p) n -> p c n", p=P)).then_inc(weights_in, 16)
            sp.dma_start(b_k[:, :], row(g.w["L0_mix_bk"])).then_inc(weights_in, 16)
            sp.dma_start(b_v[:, :], row(g.w["L0_mix_bv"])).then_inc(weights_in, 16)
            load_columns(sp, b_q[:, :], g.w["L0_mix_bq"]).then_inc(weights_in, 16)

            def step(t, b):
                sp.wait_ge(x_free, t + 1)
                sp.dma_start(x_in[:, b, :], g.x[bass.ds(t * P, P), :]).then_inc(x_loaded[b], 16)
            over_pairs(sp, step)

        @block.gpsimd
        def _(pool):
            pool.memset(valid[:, :], 1.0)
            pool.drain()
            pool.affine_select(out=valid[:, :], in_=valid[:, :], compare_op=ALU.is_gt, fill=0.0,
                               base=N, pattern=[[-P, T]], channel_multiplier=-1).then_inc(valid_made, 1)

            def step(t, b):
                pool.wait_ge(sup_ready, t + 1)
                pool.dma_start(g.sup_table[bass.ds(t * P, P), :], sup[:, b, :]).then_inc(sup_stored[b], 16)
            over_pairs(pool, step)
            pool.wait_ge(sup_stored[0], 16 * ((T + 1) // 2))
            pool.wait_ge(sup_stored[1], 16 * (T // 2))

        @block.scalar
        def _(act):
            def step(t, b):
                act.wait_ge(x_turned, t + 1)
                act.wait_ge(xt_free, t + 1)
                act.copy(xt[:, b, :, :], turned[:, :, :]).then_inc(xt_ready, 1)
                act.wait_ge(lin_ready, t + 1)
                act.activation(k_neg[:, b, :], k_neg[:, b, :], ACT.Exp)
                act.activation(q_neg[:, b, :], q_neg[:, b, :], ACT.Exp).then_inc(exp_ready, 1)
                act.wait_ge(projected, t + 1)
                act.wait_ge(sup_stored[b], uses_before(t, b))
                act.copy(sup[:, b, :], sup_ps[:, :]).then_inc(sup_ready, 1)
            over_pairs(act, step)

        @block.vector
        def _(dve):
            dve.memset(kv_sum[:, :, :], 0.0)
            dve.memset(g.kv[:, :, :], 0.0)
            dve.memset(g.ksum[:, :, :], 0.0)
            dve.drain()
            dve.sem_inc(x_free, 2)
            dve.sem_inc(xt_free, 2)
            dve.wait_ge(valid_made, 1)
            dve.wait_ge(weights_in, 16 * 7)

            def norm(t, b):
                dve.wait_ge(x_loaded[b], uses_before(t, b) + 16)
                xn = g.xn[:, bass.ds(t, 1), :].rearrange("p a n -> p (a n)")
                normalise(dve, x_in[:, b, :], x_in[:, b, :], stats[:, b, :], mv[:, b, :], rs[:, b:b + 1], tmp[:, b:b + 1])
                dve.drain()
                dve.tensor_copy(xn, x_in[:, b, :]).then_inc(xn_ready, 1)

            def step(t, b, last=False):
                dve.wait_ge(projected, t + 1)
                dve.tensor_tensor(k_lin[:, :], kv_ps[:, 0:D], b_k[:, :], ALU.add)
                dve.tensor_tensor(v_one[:, b, :, 0:P], kv_ps[:, D:2 * D].rearrange("p (a n) -> p a n", a=2), b_v[:, :].rearrange("p (a n) -> p a n", a=2), ALU.add)
                for h in range(2):
                    dve.tensor_scalar(q_neg[:, b, h * P:(h + 1) * P], q_ps[:, h * P:(h + 1) * P], b_q[:, h:h + 1], 0.0, ALU.add, ALU.min)
                    dve.tensor_scalar(q_pos[:, b, h * P:(h + 1) * P], q_ps[:, h * P:(h + 1) * P], b_q[:, h:h + 1], 0.0, ALU.add, ALU.max)
                dve.drain()
                dve.tensor_scalar(k_neg[:, b, :], k_lin[:, :], 0.0, None, ALU.min).then_inc(lin_ready, 1)
                if not last:
                    norm(t + 1, 1 - b)
                for h in range(2):
                    dve.tensor_copy(v_one[:, b, h, P:P + 1], valid[:, bass.ds(t, 1)])
                    dve.tensor_scalar(v_one[:, b, h, 0:P], v_one[:, b, h, 0:P], valid[:, bass.ds(t, 1)], None, ALU.mult)
                dve.wait_ge(exp_ready, t + 1)
                dve.scalar_tensor_tensor(k_phi[:, b, :], k_lin[:, :], 0.0, k_neg[:, b, :], ALU.max, ALU.add)
                dve.drain()
                dve.tensor_tensor(g.q_phi[:, :, bass.ds(t * P, P)], q_pos[:, b, :].rearrange("p (a n) -> p a n", a=2),
                                  q_neg[:, b, :].rearrange("p (a n) -> p a n", a=2), ALU.add).then_inc(phi_ready, 1)
                dve.wait_ge(sums_ready, t + 1)
                dve.tensor_tensor(kv_sum[:, :, :], kv_sum[:, :, :], sum_ps[:, :, :], ALU.add).then_inc(summed_up, 1)
            norm(0, 0)
            with dve.Fori(0, PAIRS) as i:
                step(i * 2, 0)
                step(i * 2 + 1, 1)
            step(T - 1, 0, last=True)
            dve.drain()
            for h in range(2):
                for r in range(4):
                    s = slice(32 * r, 32 * r + 32)
                    dve.tensor_copy(g.kv[s, h, s], kv_sum[s, h, s])
                    dve.tensor_copy(g.ksum[s, h, s], kv_sum[s, h, P:P + 1].broadcast_to([32, 32]))

        @block.tensor
        def _(pe):
            pe.wait_ge(weights_in, 16 * 7)

            def step(t, b):
                pe.wait_ge(xn_ready, t + 1)
                pe.wait_ge(xt_ready, t)
                for h in range(2):
                    last = pe.transpose(turned[:, h, :], x_in[:, b, h * P:(h + 1) * P], g.ident[:, :])
                last.then_inc(x_turned, 1)
                pe.wait_ge(xt_ready, t + 1)
                pe.wait_ge(phi_ready, t)
                pe.wait_ge(sup_ready, t)
                pe.sem_inc(x_free, 1)
                for h in range(2):
                    pe.matmul(kv_ps[:, :], xt[:, b, h, :], w_kvs[:, h, 0:2 * D], start=h == 0, stop=h == 1)
                for h in range(2):
                    pe.matmul(sup_ps[:, :], xt[:, b, h, :], w_kvs[:, h, 2 * D:3 * D], start=h == 0, stop=h == 1)
                for o in range(2):
                    for h in range(2):
                        last = pe.matmul(q_ps[:, o * P:(o + 1) * P], w_q[:, h, o * P:(o + 1) * P], xt[:, b, h, :], start=h == 0, stop=h == 1)
                last.then_inc(projected, 1)
                pe.wait_ge(phi_ready, t + 1)
                pe.wait_ge(summed_up, t)
                pe.sem_inc(xt_free, 1)
                for h in range(2):
                    last = pe.matmul(sum_ps[:, h, :], k_phi[:, b, h * P:(h + 1) * P], v_one[:, b, h, :], start=True, stop=True)
                last.then_inc(sums_ready, 1)
            over_pairs(pe, step)


def layer0_graph_and_attention(nc, g):
    with ExitStack() as ctx:
        sb = lambda n, s, d=F32: ctx.enter_context(nc.sbuf_tensor(n, s, d))
        sem = lambda n: ctx.enter_context(nc.semaphore(n))
        bank = lambda n: ctx.enter_context(nc.psum_tensor(n, [P, 512], F32))
        w_o, w_1, w_2 = sb("b_wo", [P, 2, D]), sb("b_w1", [P, 2, FF]), sb("b_w2", [P, FF // P, D])
        b_o, ln1_g, ln1_b, ln2_g, ln2_b, b_2, b_gnn = (sb("b_row" + str(i), [P, D]) for i in range(7))
        b_1 = sb("b_b1", [P, FF // P])
        messages = sb("b_messages", [P, 2, STEPS, D])
        sources = sb("b_sources", [P, 2, STEPS], I32)
        spread = sb("b_spread", [P, 2, HALF, P])
        x_in = sb("b_x", [P, 2, D])
        gathered = sb("b_gathered", [P, 2, D])
        ratio, inverse = sb("b_ratio", [P, 2, P]), sb("b_inverse", [P, 2, P])
        h1 = sb("b_h1", [P, 2, D])
        h1_t = sb("b_h1t", [P, 2, P])
        hidden = sb("b_hidden", [P, FF // P, P])
        work, total = sb("b_work", [P, D]), sb("b_total", [P, D])
        stats, mv, rs, tmp = sb("b_stats", [P, 6]), sb("b_mv", [P, 2]), sb("b_rs", [P, 1]), sb("b_tmp", [P, 1])
        agg_ps, attn_ps, out_ps, turned_ps, down_ps = (bank("b_" + n) for n in ("agg", "attn", "outp", "turn", "down"))
        up_ps = [bank("b_up0"), bank("b_up1")]
        names = ("weights gathers_begun sources_ready spread_ready spread_free messages_free x_free attn_done ratio_ready out_done h1_ready "
                 "turned_done h1t_ready up_done hidden_ready down_done down_used agg_done agg_copied x1_ready").split()
        s = {n: sem("b_" + n) for n in names}
        messages_in = [sem("b_messages_in0"), sem("b_messages_in1")]
        x_loaded = [sem("b_x_loaded0"), sem("b_x_loaded1")]
        block = ctx.enter_context(nc.Block())
        LOADS = 16 * 11

        def turns(eng, step, last):
            step(0, 0, True)
            with eng.Fori(0, PAIRS) as i:
                step(i * 2 + 1, 1, False)
                step(i * 2 + 2, 0, False)
            last(T - 1, 0)

        @block.sync
        def _(sp):
            sp.dma_start(w_o[:, :, :], g.w["L0_mix_Wo"].rearrange("(c p) n -> p c n", p=P)).then_inc(s["weights"], 16)
            for out, vector in ((b_o, g.w["L0_mix_bo"]), (ln1_g, g.w["L0_mix_ln1_g"]), (ln1_b, g.w["L0_mix_ln1_b"])):
                sp.dma_start(out[:, :], row(vector)).then_inc(s["weights"], 16)
            sp.dma_start(w_1[:, :, :], g.w["L0_mix_W1"].rearrange("(c p) n -> p c n", p=P)).then_inc(s["weights"], 16)
            sp.dma_start(w_2[:, :, :], g.w["L0_mix_W2"].rearrange("(c p) n -> p c n", p=P)).then_inc(s["weights"], 16)
            load_columns(sp, b_1[:, :], g.w["L0_mix_b1"]).then_inc(s["weights"], 16)
            for out, vector in ((ln2_g, g.w["L0_mix_ln2_g"]), (ln2_b, g.w["L0_mix_ln2_b"]), (b_2, g.w["L0_mix_b2"]), (b_gnn, g.w["L0_gnn_bias"])):
                sp.dma_start(out[:, :], row(vector)).then_inc(s["weights"], 16)

            def step(t, b):
                sp.wait_ge(s["x_free"], t + 1)
                sp.dma_start(x_in[:, b, :], g.x[bass.ds(t * P, P), :]).then_inc(x_loaded[b], 16)
            over_pairs(sp, step)

        @block.gpsimd
        def _(pool):
            def step(t, b):
                pool.wait_ge(s["messages_free"], t + 1)
                pool.tensor_copy(sources[:, b, :], g.e_src[:, bass.ds(t * STEPS, STEPS)]).then_inc(s["sources_ready"], 1)
                pool.wait_ge(s["sources_ready"], t + 1)
                pool.sem_inc(s["gathers_begun"], 1)
                for j in range(STEPS):
                    pool.indirect_dma_start(messages[:, b, j, :], None, g.sup_table[:, :],
                                            bass.IndirectOffsetOnAxis(ap=sources[:, b, j:j + 1], axis=0)).then_inc(messages_in[b], 16)
            over_pairs(pool, step)

        @block.scalar
        def _(act):
            def copy_sums(t, b):
                act.wait_ge(s["agg_done"], t + 1)
                act.wait_ge(s["x1_ready"], t)
                act.copy(gathered[:, b, :], agg_ps[:, 0:D]).then_inc(s["agg_copied"], 1)

            def step(t, b, first):
                copy_sums(t, b)
                act.wait_ge(s["turned_done"], t + 1)
                act.copy(h1_t[:, :, :], turned_ps[:, 0:D].rearrange("p (c n) -> p c n", c=2)).then_inc(s["h1t_ready"], 1)
                for u in range(2):
                    act.wait_ge(s["up_done"], t * 2 + u + 1)
                    for c in range(4):
                        chunk = act.activation(hidden[:, u * 4 + c, :], up_ps[u][:, c * P:(c + 1) * P], ACT.Relu, bias=b_1[:, u * 4 + c:u * 4 + c + 1])
                    chunk.then_inc(s["hidden_ready"], 1)
            act.wait_ge(s["weights"], LOADS)
            turns(act, step, lambda t, b: None)

        @block.vector
        def _(dve):
            def spread_edges(t, half):
                dve.wait_ge(s["spread_free"], t * 2 + half + 1)
                for j in range(HALF):
                    e = bass.ds(t * STEPS + half * HALF + j, 1)
                    last = dve.tensor_scalar(spread[:, half, j, :], g.node[:, :], g.e_dst[:, e], g.e_weight[:, e], ALU.is_equal, ALU.mult)
                last.then_inc(s["spread_ready"], 1)

            def attention(t, b):
                dve.wait_ge(s["attn_done"], t + 1)
                dve.tensor_scalar(inverse[:, :, :], attn_ps[:, D:2 * D].rearrange("p (c n) -> p c n", c=2), 1e-6, None, ALU.add)
                dve.drain()
                dve.reciprocal(inverse[:, :, :], inverse[:, :, :])
                dve.drain()
                dve.tensor_tensor(ratio[:, :, :], attn_ps[:, 0:D].rearrange("p (c n) -> p c n", c=2), inverse[:, :, :], ALU.mult).then_inc(s["ratio_ready"], 1)

            def first_norm(t, b):
                dve.wait_ge(s["out_done"], t + 1)
                dve.tensor_tensor(work[:, :], out_ps[:, 0:D], b_o[:, :], ALU.add)
                dve.drain()
                dve.tensor_tensor(work[:, :], work[:, :], g.xn[:, bass.ds(t, 1), :].rearrange("p a n -> p (a n)"), ALU.add)
                dve.drain()
                normalise(dve, work[:, :], work[:, :], stats[:, :], mv[:, :], rs[:, :], tmp[:, :])
                dve.drain()
                dve.tensor_tensor(work[:, :], work[:, :], ln1_g[:, :], ALU.mult)
                dve.drain()
                dve.tensor_tensor(h1[:, b, :], work[:, :], ln1_b[:, :], ALU.add).then_inc(s["h1_ready"], 1)

            def second_norm(t, b):
                dve.wait_ge(s["down_done"], t + 1)
                dve.tensor_tensor(total[:, :], down_ps[:, 0:D], b_2[:, :], ALU.add).then_inc(s["down_used"], 1)
                dve.drain()
                dve.tensor_tensor(total[:, :], total[:, :], h1[:, b, :], ALU.add)
                dve.drain()
                normalise(dve, total[:, :], total[:, :], stats[:, :], mv[:, :], rs[:, :], tmp[:, :])
                dve.drain()
                dve.tensor_tensor(total[:, :], total[:, :], ln2_g[:, :], ALU.mult)
                dve.drain()
                dve.tensor_tensor(total[:, :], total[:, :], ln2_b[:, :], ALU.add)
                dve.wait_ge(x_loaded[b], uses_before(t, b) + 16)
                dve.wait_ge(s["agg_copied"], t + 1)
                dve.tensor_tensor(x_in[:, b, :], x_in[:, b, :], b_gnn[:, :], ALU.add)
                dve.drain()
                dve.tensor_tensor(x_in[:, b, :], x_in[:, b, :], gathered[:, b, :], ALU.add)
                dve.drain()
                dve.tensor_tensor(g.xn[:, bass.ds(t, 1), :].rearrange("p a n -> p (a n)"), x_in[:, b, :], total[:, :], ALU.add).then_inc(s["x1_ready"], 1)
                dve.wait_ge(s["x1_ready"], t + 1)
                dve.sem_inc(s["x_free"], 1)

            def step(t, b, first, final=False):
                attention(t, b)
                if not final:
                    spread_edges(t + 1, 0)
                first_norm(t, b)
                if not final:
                    spread_edges(t + 1, 1)
                if not first:
                    second_norm(t - 1, 1 - b)

            for free in ("spread_free", "messages_free", "x_free"):
                dve.sem_inc(s[free], 2)
            dve.wait_ge(s["weights"], LOADS)
            spread_edges(0, 0)
            spread_edges(0, 1)
            step(0, 0, True)
            with dve.Fori(0, PAIRS - 1) as i:
                step(i * 2 + 1, 1, False)
                step(i * 2 + 2, 0, False)
            step(T - 2, 1, False)
            step(T - 1, 0, False, final=True)
            second_norm(T - 1, 0)

        @block.tensor
        def _(pe):
            def sums(t, b, half):
                pe.wait_ge(s["spread_ready"], t * 2 + half + 1)
                for j in range(half * HALF, half * HALF + HALF):
                    last = pe.matmul(agg_ps[:, 0:D], spread[:, half, j % HALF, :], messages[:, b, j, :], start=j == 0, stop=j == STEPS - 1)
                return last

            def down(t, b):
                pe.wait_ge(s["hidden_ready"], t * 2 + 2)
                pe.wait_ge(s["down_used"], t)
                for c in range(FF // P):
                    last = pe.matmul(down_ps[:, 0:D], hidden[:, c, :], w_2[:, c, :], start=c == 0, stop=c == FF // P - 1)
                last.then_inc(s["down_done"], 1)

            def step(t, b, first):
                pe.wait_ge(s["ratio_ready"], t)
                for c in range(2):
                    pe.matmul(attn_ps[:, c * P:(c + 1) * P], g.kv[:, c, :], g.q_phi[:, c, bass.ds(t * P, P)], start=True, stop=True)
                for c in range(2):
                    last = pe.matmul(attn_ps[:, D + c * P:D + (c + 1) * P], g.ksum[:, c, :], g.q_phi[:, c, bass.ds(t * P, P)], start=True, stop=True)
                last.then_inc(s["attn_done"], 1)
                pe.wait_ge(messages_in[b], uses_before(t, b) * STEPS + 16 * STEPS)
                pe.wait_ge(s["agg_copied"], t)
                sums(t, b, 0).then_inc(s["spread_free"], 1)
                pe.wait_ge(s["ratio_ready"], t + 1)
                pe.wait_ge(s["h1_ready"], t)
                for c in range(2):
                    last = pe.matmul(out_ps[:, 0:D], ratio[:, c, :], w_o[:, c, :], start=c == 0, stop=c == 1)
                last.then_inc(s["out_done"], 1)
                sums(t, b, 1).then_inc(s["agg_done"], 1)
                pe.wait_ge(s["agg_done"], t + 1)
                pe.sem_inc(s["spread_free"], 1)
                pe.sem_inc(s["messages_free"], 1)
                if not first:
                    down(t - 1, 1 - b)
                pe.wait_ge(s["h1_ready"], t + 1)
                pe.wait_ge(s["h1t_ready"], t)
                for c in range(2):
                    last = pe.transpose(turned_ps[:, c * P:(c + 1) * P], h1[:, b, c * P:(c + 1) * P], g.ident[:, :])
                last.then_inc(s["turned_done"], 1)
                pe.wait_ge(s["h1t_ready"], t + 1)
                if not first:
                    pe.wait_ge(s["down_done"], t)
                for u in range(2):
                    pe.wait_ge(s["hidden_ready"], t * 2 + u)
                    for o in range(u * 4, u * 4 + 4):
                        for c in range(2):
                            last = pe.matmul(up_ps[u][:, (o % 4) * P:(o % 4 + 1) * P], w_1[:, c, o * P:(o + 1) * P], h1_t[:, c, :], start=c == 0, stop=c == 1)
                    last.then_inc(s["up_done"], 1)
            pe.wait_ge(s["weights"], LOADS)
            turns(pe, step, down)


def layer0_experts(nc, g):
    with ExitStack() as ctx:
        sb = lambda n, s, d=F32: ctx.enter_context(nc.sbuf_tensor(n, s, d))
        sem = lambda n: ctx.enter_context(nc.semaphore(n))
        bank = lambda n: ctx.enter_context(nc.psum_tensor(n, [P, 512], F32))
        HC = HID // P
        w_1 = sb("d_w1", [P, NEXP, 2, HID])
        w_2 = sb("d_w2", [P, NEXP, HC, D])
        b_1 = sb("d_b1", [P, NEXP * HC])
        b_2 = sb("d_b2", [NEXP, D])
        w_r = sb("d_wr", [P, 2, NEXP])
        b_r, gamma, beta = sb("d_br", [P, NEXP]), sb("d_gamma", [P, D]), sb("d_beta", [P, D])
        work = sb("d_work", [P, D])
        xe = sb("d_xe", [P, 2, D])
        xe_t = sb("d_xet", [P, 2, 2, P])
        hidden = sb("d_hidden", [P, 2, HC, P])
        logits, top, best = sb("d_logits", [P, NEXP]), sb("d_top", [P, 8]), sb("d_best", [P, 8], U32)
        best_f, gap, ratio, share = sb("d_bestf", [P, 8]), sb("d_gap", [P, 1]), sb("d_ratio", [P, 1]), sb("d_share", [P, 2])
        weight = sb("d_weight", [P, 2, NEXP])
        second = sb("d_second", [P, NEXP])
        weight_t = sb("d_weightt", [NEXP, P])
        stats, mv, rs, tmp = sb("d_stats", [P, 6]), sb("d_mv", [P, 2]), sb("d_rs", [P, 1]), sb("d_tmp", [P, 1])
        turned_ps, route_ps, weight_ps, bias_ps = (bank("d_" + n) for n in ("turn", "route", "weightps", "biasps"))
        up_ps = [bank("d_up0"), bank("d_up1")]
        down_ps = [bank("d_down0"), bank("d_down1")]
        names = ("weights xe_ready turned_done xet_ready routed gap_ready ratio_ready weight_ready weight_turned "
                 "weightt_ready bias_done bias_used up_done hidden_ready down_done down_used").split()
        s = {n: sem("d_" + n) for n in names}
        LOADS = 16 * 8
        block = ctx.enter_context(nc.Block())

        @block.sync
        def _(sp):
            sp.dma_start(gamma[:, :], row(g.w["L0_ffn_gamma"])).then_inc(s["weights"], 16)
            sp.dma_start(beta[:, :], row(g.w["L0_ffn_beta"])).then_inc(s["weights"], 16)
            sp.dma_start(w_r[:, :, :], g.w["L0_ffn_Wr"].rearrange("(c p) n -> p c n", p=P)).then_inc(s["weights"], 16)
            sp.dma_start(b_r[:, :], row(g.w["L0_ffn_br"])).then_inc(s["weights"], 16)
            sp.dma_start(b_2[:, :], g.w["L0_ffn_b2"]).then_inc(s["weights"], 16)
            load_columns(sp, b_1[:, :], g.w["L0_ffn_b1"].rearrange("e n -> (e n)")).then_inc(s["weights"], 16)
            sp.dma_start(w_1[:, :, :, :], g.w["L0_ffn_W1"].rearrange("e (c p) n -> p e c n", p=P)).then_inc(s["weights"], 16)
            sp.dma_start(w_2[:, :, :, :], g.w["L0_ffn_W2"].rearrange("e (c p) n -> p e c n", p=P)).then_inc(s["weights"], 16)

        def tiles(eng, step):
            with eng.Fori(0, PAIRS) as i:
                step(i * 2, 0, False)
                step(i * 2 + 1, 1, False)
            step(T - 1, 0, True)

        @block.scalar
        def _(act):
            def copy_turned(t, b):
                act.wait_ge(s["turned_done"], t + 1)
                act.copy(xe_t[:, b, :, :], turned_ps[:, 0:D].rearrange("p (c n) -> p c n", c=2)).then_inc(s["xet_ready"], 1)

            def exponent(t, b):
                act.wait_ge(s["gap_ready"], t + 1)
                act.activation(ratio[:, :], gap[:, :], ACT.Exp).then_inc(s["ratio_ready"], 1)

            def copy_weights(t, b):
                act.wait_ge(s["weight_turned"], t + 1)
                act.copy(weight_t[:, :], weight_ps[0:NEXP, 0:P]).then_inc(s["weightt_ready"], 1)

            def step(t, b, final):
                for e in range(NEXP):
                    act.wait_ge(s["up_done"], t * NEXP + e + 1)
                    for c in range(HC):
                        last = act.activation(hidden[:, e % 2, c, :], up_ps[e % 2][:, c * P:(c + 1) * P], ACT.Gelu,
                                              bias=b_1[:, e * HC + c:e * HC + c + 1])
                    last.then_inc(s["hidden_ready"], 1)
                    if not final and e == 4:
                        copy_turned(t + 1, 1 - b)
                    if not final and e == 5:
                        exponent(t + 1, 1 - b)
                    if not final and e == 7:
                        copy_weights(t + 1, 1 - b)
            act.wait_ge(s["weights"], LOADS)
            copy_turned(0, 0)
            exponent(0, 0)
            copy_weights(0, 0)
            tiles(act, step)

        @block.vector
        def _(dve):
            def rows(t):
                return g.xn[:, bass.ds(t, 1), :].rearrange("p a n -> p (a n)")

            def first_norm(t, b):
                normalise(dve, work[:, :], rows(t), stats[:, :], mv[:, :], rs[:, :], tmp[:, :])
                dve.drain()

            def second_norm(t, b):
                normalise(dve, work[:, :], work[:, :], stats[:, :], mv[:, :], rs[:, :], tmp[:, :])
                dve.drain()

            def affine(t, b):
                dve.tensor_tensor(work[:, :], work[:, :], gamma[:, :], ALU.mult)
                dve.drain()
                dve.tensor_tensor(xe[:, b, :], work[:, :], beta[:, :], ALU.add).then_inc(s["xe_ready"], 1)

            def choose(t, b):
                dve.wait_ge(s["routed"], t + 1)
                dve.tensor_tensor(logits[:, :], route_ps[:, 0:NEXP], b_r[:, :], ALU.add)
                dve.drain()
                dve.max(top[:, :], logits[:, :])
                dve.drain()
                dve.tensor_tensor(gap[:, :], top[:, 1:2], top[:, 0:1], ALU.subtract).then_inc(s["gap_ready"], 1)
                dve.max_index(best[:, :], top[:, :], logits[:, :])
                dve.drain()
                dve.tensor_copy(best_f[:, :], best[:, :])

            def weigh(t, b):
                dve.wait_ge(s["ratio_ready"], t + 1)
                dve.tensor_scalar(share[:, 0:1], ratio[:, :], 1.0, None, ALU.add)
                dve.drain()
                dve.reciprocal(share[:, 0:1], share[:, 0:1])
                dve.drain()
                dve.tensor_tensor(share[:, 1:2], share[:, 0:1], ratio[:, :], ALU.mult)
                dve.drain()
                dve.tensor_scalar(weight[:, b, :], g.node[:, 0:NEXP], best_f[:, 0:1], share[:, 0:1], ALU.is_equal, ALU.mult)
                dve.tensor_scalar(second[:, :], g.node[:, 0:NEXP], best_f[:, 1:2], share[:, 1:2], ALU.is_equal, ALU.mult)
                dve.drain()
                dve.tensor_tensor(weight[:, b, :], weight[:, b, :], second[:, :], ALU.add).then_inc(s["weight_ready"], 1)

            def add_expert(t, b, e):
                dve.wait_ge(s["down_done"], t * NEXP + e + 1)
                dve.scalar_tensor_tensor(rows(t), down_ps[e % 2][:, 0:D], weight[:, b, e:e + 1], rows(t), ALU.mult, ALU.add).then_inc(s["down_used"], 1)
                dve.drain()

            def step(t, b, final):
                dve.wait_ge(s["bias_done"], t + 1)
                dve.tensor_tensor(rows(t), rows(t), bias_ps[:, 0:D], ALU.add).then_inc(s["bias_used"], 1)
                dve.drain()
                for e in range(NEXP):
                    if not final:
                        if e == 0:
                            first_norm(t + 1, 1 - b)
                        if e == 1:
                            second_norm(t + 1, 1 - b)
                        if e == 2:
                            affine(t + 1, 1 - b)
                        if e == 5:
                            choose(t + 1, 1 - b)
                        if e == 6:
                            weigh(t + 1, 1 - b)
                    add_expert(t, b, e)
            dve.wait_ge(s["weights"], LOADS)
            for part in (first_norm, second_norm, affine, choose, weigh):
                part(0, 0)
            tiles(dve, step)

        @block.tensor
        def _(pe):
            def turn(t, b):
                pe.wait_ge(s["xe_ready"], t + 1)
                for c in range(2):
                    last = pe.transpose(turned_ps[:, c * P:(c + 1) * P], xe[:, b, c * P:(c + 1) * P], g.ident[:, :])
                last.then_inc(s["turned_done"], 1)

            def route(t, b):
                pe.wait_ge(s["xet_ready"], t + 1)
                for c in range(2):
                    last = pe.matmul(route_ps[:, 0:NEXP], xe_t[:, b, c, :], w_r[:, c, :], start=c == 0, stop=c == 1)
                last.then_inc(s["routed"], 1)

            def turn_weights(t, b):
                pe.wait_ge(s["weight_ready"], t + 1)
                pe.transpose(weight_ps[0:NEXP, 0:P], weight[:, b, :], g.ident[:, :]).then_inc(s["weight_turned"], 1)

            def biases(t, b):
                pe.wait_ge(s["weightt_ready"], t + 1)
                pe.wait_ge(s["bias_used"], t)
                pe.matmul(bias_ps[:, 0:D], weight_t[:, :], b_2[:, :], start=True, stop=True).then_inc(s["bias_done"], 1)

            def up(t, b, e):
                pe.wait_ge(s["hidden_ready"], (t * NEXP + e - 1) if e >= 1 else t * NEXP)
                for c in range(HC):
                    for k in range(2):
                        last = pe.matmul(up_ps[e % 2][:, c * P:(c + 1) * P], w_1[:, e, k, c * P:(c + 1) * P], xe_t[:, b, k, :], start=k == 0, stop=k == 1)
                last.then_inc(s["up_done"], 1)

            def down(t, b, e):
                pe.wait_ge(s["hidden_ready"], t * NEXP + e + 1)
                pe.wait_ge(s["down_used"], (t * NEXP + e - 1) if e >= 1 else t * NEXP)
                for c in range(HC):
                    last = pe.matmul(down_ps[e % 2][:, 0:D], hidden[:, e % 2, c, :], w_2[:, e, c, :], start=c == 0, stop=c == HC - 1)
                last.then_inc(s["down_done"], 1)

            def step(t, b, final):
                for e in range(NEXP):
                    up(t, b, e)
                    if not final:
                        if e == 4:
                            turn(t + 1, 1 - b)
                        if e == 5:
                            route(t + 1, 1 - b)
                        if e == 7:
                            turn_weights(t + 1, 1 - b)
                    if e:
                        down(t, b, e - 1)
                if not final:
                    biases(t + 1, 1 - b)
                down(t, b, NEXP - 1)
            pe.wait_ge(s["weights"], LOADS)
            for part in (turn, route, turn_weights, biases):
                part(0, 0)
            tiles(pe, step)


def layer1_projections(nc, g):
    with ExitStack() as ctx:
        sb = lambda n, s, d=F32: ctx.enter_context(nc.sbuf_tensor(n, s, d))
        sem = lambda n: ctx.enter_context(nc.semaphore(n))
        bank = lambda n: ctx.enter_context(nc.psum_tensor(n, [P, 512], F32))
        w_att = sb("c_watt", [P, 2, TBL + 4])
        att = sb("c_att", [P, 2, D])
        folded = sb("c_folded", [P, 2, 4, 64])
        w_conv = sb("c_wconv", [P, 2, CQ])
        valid = sb("c_valid", [P, T])
        stats, mv_one, mv = sb("c_stats", [P, 6]), sb("c_mvone", [P, 2]), sb("c_mv", [P, T, 2])
        mean, var, rstd, rstd_log = (sb("c_" + n, [P, T]) for n in ("mean", "var", "rstd", "rstdlog"))
        norm2, inv, clipped, sq, series, log_up, log_down, tmp, small = (sb("c_s" + str(i), [P, T]) for i in range(9))
        pair = sb("c_pair", [P, 2, 2, D])
        pair_t = sb("c_pairt", [P, 2, 4, P])
        table = sb("c_table", [P, 2, TBL])
        conv = sb("c_conv", [P, 2, 6, P])
        turned_ps, att_ps, conv_ps0, conv_ps1 = (bank("c_" + n) for n in ("turn", "attps", "conv0", "conv1"))
        names = ("weights valid_made clipped_ready logs_ready pair_ready turned_done pairt_ready projected dst_taken "
                 "table_ready conv_ready stats_taken").split()
        s = {n: sem("c_" + n) for n in names}
        table_out = [sem("c_table_out0"), sem("c_table_out1")]
        conv_out = [sem("c_conv_out0"), sem("c_conv_out1")]
        LOADS = 16 * 4
        block = ctx.enter_context(nc.Block())

        @block.sync
        def _(sp):
            sp.dma_start(w_att[:, :, 0:D], g.w["L1_gnn_W"].rearrange("(c p) n -> p c n", p=P)).then_inc(s["weights"], 16)
            sp.dma_start(att[:, 0, :], row(g.w["L1_gnn_att_src"].rearrange("h c -> (h c)"))).then_inc(s["weights"], 16)
            sp.dma_start(att[:, 1, :], row(g.w["L1_gnn_att_dst"].rearrange("h c -> (h c)"))).then_inc(s["weights"], 16)
            sp.dma_start(w_conv[:, :, :], g.w["L1_mix_w_qkv"][:, 2, :].rearrange("(c p) n -> p c n", p=P)).then_inc(s["weights"], 16)

            def step(t, b):
                sp.wait_ge(s["table_ready"], t + 1)
                sp.dma_start(g.att_table[bass.ds(t * P, P), :], table[:, b, :]).then_inc(table_out[b], 16)
                sp.wait_ge(s["conv_ready"], t + 1)
                sp.dma_start(g.conv[bass.ds(t, 1), :, :].rearrange("a (c p) n -> p (a c) n", p=P), conv[:, b, :, :]).then_inc(conv_out[b], 16)
            over_pairs(sp, step)
            for done in (table_out, conv_out):
                sp.wait_ge(done[0], 16 * ((T + 1) // 2))
                sp.wait_ge(done[1], 16 * (T // 2))

        @block.gpsimd
        def _(pool):
            pool.memset(valid[:, :], 1.0)
            pool.drain()
            pool.affine_select(out=valid[:, :], in_=valid[:, :], compare_op=ALU.is_gt, fill=0.0,
                               base=N, pattern=[[-P, T]], channel_multiplier=-1).then_inc(s["valid_made"], 1)

        @block.scalar
        def _(act):
            act.wait_ge(s["clipped_ready"], 1)
            act.activation(log_up[:, :], clipped[:, :], ACT.Ln, bias=1.0)
            act.activation(log_down[:, :], small[:, :], ACT.Ln).then_inc(s["logs_ready"], 1)

            def step(t, b):
                act.wait_ge(s["turned_done"], t + 1)
                act.copy(pair_t[:, b, :, :], turned_ps[:, :].rearrange("p (c n) -> p c n", c=4)).then_inc(s["pairt_ready"], 1)
                act.wait_ge(s["projected"], t + 1)
                act.wait_ge(table_out[b], uses_before(t, b))
                act.wait_ge(s["dst_taken"], t + 1)
                act.copy(table[:, b, :], att_ps[:, 0:TBL]).then_inc(s["table_ready"], 1)
                act.wait_ge(conv_out[b], uses_before(t, b))
                act.wait_ge(s["stats_taken"], t)
                act.copy(conv[:, b, 0:4, :], conv_ps0[:, :].rearrange("p (c n) -> p c n", c=4))
                act.copy(conv[:, b, 4:6, :], conv_ps1[:, 0:2 * P].rearrange("p (c n) -> p c n", c=2)).then_inc(s["conv_ready"], 1)
            over_pairs(act, step)

        @block.vector
        def _(dve):
            with dve.Fori(0, T) as t:
                dve.bn_stats(stats[:, :], g.xn[:, bass.ds(t, 1), :].rearrange("p a n -> p (a n)"))
                dve.drain()
                dve.bn_aggr(mv_one[:, :], stats[:, :])
                dve.drain()
                dve.tensor_copy(mv[:, bass.ds(t, 1), :].rearrange("p a n -> p (a n)"), mv_one[:, :])
            dve.drain()
            dve.tensor_copy(mean[:, :], mv[:, :, 0])
            dve.tensor_scalar(var[:, :], mv[:, :, 1], EPS, None, ALU.add)
            dve.drain()
            newton_rsqrt(dve, rstd[:, :], var[:, :], tmp[:, :])
            dve.tensor_tensor(norm2[:, :], rstd[:, :], rstd[:, :], ALU.mult)
            dve.drain()
            dve.scalar_tensor_tensor(norm2[:, :], mv[:, :, 1], float(D), norm2[:, :], ALU.mult, ALU.mult)
            dve.drain()
            dve.tensor_scalar(norm2[:, :], norm2[:, :], 1e-30, None, ALU.max)
            dve.drain()
            newton_rsqrt(dve, inv[:, :], norm2[:, :], tmp[:, :])
            dve.tensor_tensor(clipped[:, :], norm2[:, :], inv[:, :], ALU.mult)
            dve.drain()
            dve.tensor_scalar(clipped[:, :], clipped[:, :], MAXNORM, None, ALU.min)
            dve.drain()
            dve.tensor_scalar(small[:, :], clipped[:, :], -1.0, 1.0, ALU.mult, ALU.add)
            dve.drain()
            dve.tensor_tensor(sq[:, :], clipped[:, :], clipped[:, :], ALU.mult).then_inc(s["clipped_ready"], 1)
            dve.drain()
            dve.tensor_scalar(series[:, :], sq[:, :], 1.0 / 11, 1.0 / 9, ALU.mult, ALU.add)
            dve.drain()
            for c in (7, 5, 3, 1):
                dve.tensor_tensor(series[:, :], series[:, :], sq[:, :], ALU.mult)
                dve.drain()
                dve.tensor_scalar(series[:, :], series[:, :], 1.0 / c, None, ALU.add)
                dve.drain()
            dve.tensor_tensor(series[:, :], series[:, :], clipped[:, :], ALU.mult)
            dve.wait_ge(s["logs_ready"], 1)
            dve.tensor_tensor(log_up[:, :], log_up[:, :], log_down[:, :], ALU.subtract)
            dve.drain()
            dve.tensor_scalar(log_up[:, :], log_up[:, :], 0.5, None, ALU.mult)
            dve.tensor_scalar(small[:, :], clipped[:, :], 0.25, None, ALU.is_lt)
            dve.drain()
            dve.tensor_tensor(series[:, :], series[:, :], log_up[:, :], ALU.subtract)
            dve.drain()
            dve.tensor_tensor(series[:, :], series[:, :], small[:, :], ALU.mult)
            dve.drain()
            dve.tensor_tensor(series[:, :], series[:, :], log_up[:, :], ALU.add)
            dve.drain()
            dve.tensor_tensor(series[:, :], series[:, :], inv[:, :], ALU.mult)
            dve.wait_ge(s["valid_made"], 1)
            dve.drain()
            dve.tensor_tensor(series[:, :], series[:, :], valid[:, :], ALU.mult)
            dve.drain()
            dve.tensor_tensor(rstd_log[:, :], series[:, :], rstd[:, :], ALU.mult)
            dve.wait_ge(s["weights"], LOADS)
            for c in range(2):
                for k in range(2):
                    dve.tensor_tensor(folded[:, k, :, :], w_att[:, c, 0:D].rearrange("p (h n) -> p h n", h=4), att[:, k, :].rearrange("p (h n) -> p h n", h=4), ALU.mult)
                dve.drain()
                dve.reduce_sum(w_att[:, c, D:D + 8].rearrange("p (k h) -> p k h", k=2), folded[:, :, :, :], axis=AX.X)
                dve.drain()

            def rows(t, b):
                dve.wait_ge(s["turned_done"], t)
                x2 = g.xn[:, bass.ds(t, 1), :].rearrange("p a n -> p (a n)")
                at = bass.ds(t, 1)
                dve.tensor_scalar(pair[:, b, 0, :], x2, mean[:, at], rstd[:, at], ALU.subtract, ALU.mult)
                dve.tensor_scalar(pair[:, b, 1, :], x2, mean[:, at], rstd_log[:, at], ALU.subtract, ALU.mult).then_inc(s["pair_ready"], 1)

            def step(t, b, final=False):
                if not final:
                    rows(t + 1, 1 - b)
                dve.wait_ge(s["projected"], t + 1)
                dve.tensor_copy(g.a_dst[:, bass.ds(t, 1), :].rearrange("p a n -> p (a n)"), att_ps[:, TBL:TBL + 4]).then_inc(s["dst_taken"], 1)
                dve.wait_ge(s["conv_ready"], t + 1)
                for c in range(6):
                    last = dve.bn_stats(g.conv_stats[:, c, bass.ds(t, 1), :].rearrange("p a n -> p (a n)"), conv[:, b, c, :])
                last.then_inc(s["stats_taken"], 1)
            rows(0, 0)
            with dve.Fori(0, PAIRS) as i:
                step(i * 2, 0)
                step(i * 2 + 1, 1)
            step(T - 1, 0, final=True)

        @block.tensor
        def _(pe):
            pe.wait_ge(s["weights"], LOADS)

            def step(t, b):
                pe.wait_ge(s["pair_ready"], t + 1)
                pe.wait_ge(s["pairt_ready"], t)
                for k in range(2):
                    for c in range(2):
                        last = pe.transpose(turned_ps[:, (k * 2 + c) * P:(k * 2 + c + 1) * P], pair[:, b, k, c * P:(c + 1) * P], g.ident[:, :])
                last.then_inc(s["turned_done"], 1)
                pe.wait_ge(s["pairt_ready"], t + 1)
                pe.wait_ge(s["conv_ready"], t)
                for c in range(2):
                    pe.matmul(att_ps[:, 0:TBL + 4], pair_t[:, b, c, :], w_att[:, c, :], start=c == 0, stop=c == 1)
                for o in range(6):
                    out = (conv_ps0 if o < 4 else conv_ps1)[:, (o % 4) * P:(o % 4 + 1) * P]
                    for c in range(2):
                        last = pe.matmul(out, w_conv[:, c, o * P:(o + 1) * P], pair_t[:, b, 2 + c, :], start=c == 0, stop=c == 1)
                last.then_inc(s["projected"], 1)
            over_pairs(pe, step)


def split_bf16(dve, parts, x, rest):
    dve.tensor_copy(parts[0], x)
    dve.drain()
    dve.tensor_tensor(rest, x, parts[0], ALU.subtract)
    dve.drain()
    dve.tensor_copy(parts[1], rest)
    dve.drain()
    dve.tensor_tensor(rest, rest, parts[1], ALU.subtract)
    dve.drain()
    dve.tensor_copy(parts[2], rest)


def layer1_outputs(nc, g):
    with ExitStack() as ctx:
        sb = lambda n, s, d=F32: ctx.enter_context(nc.sbuf_tensor(n, s, d))
        sem = lambda n: ctx.enter_context(nc.semaphore(n))
        bank = lambda n, d=F32: ctx.enter_context(nc.psum_tensor(n, [P, 2048 // (4 if d == F32 else 2)], d))
        S4 = STEPS * 4
        sources = sb("e_sources", [P, 2, STEPS], I32)
        messages = sb("e_messages", [P, 2, STEPS, TBL])
        own = sb("e_own", [P, 2, TBL])
        spread, spread_h, spread_t = sb("e_spread", [P, STEPS, P]), sb("e_spreadh", [P, STEPS, P], BF16), sb("e_spreadt", [P, STEPS, P], BF16)
        ident_h = sb("e_identh", [P, P], BF16)
        score, first = sb("e_score", [P, STEPS, 4]), sb("e_first4", [P, STEPS, 4])
        rows_t, run = sb("e_rowst", [S4, 2 * P]), sb("e_run", [S4, P])
        run_last, rest = sb("e_runlast", [P, STEPS, 4]), sb("e_rest", [P, STEPS, 4])
        run_h = sb("e_runh", [P, STEPS, 13], BF16)
        picked, picked_sum, absent = sb("e_picked", [P, STEPS, 13]), sb("e_pickedsum", [P, STEPS, 4]), sb("e_absent", [P, STEPS, 1])
        per_node, node_rest, node_h = sb("e_pernode", [P, 8]), sb("e_noderest", [P, 8]), sb("e_nodeh", [P, 3, 8], BF16)
        top_src, own_z = sb("e_topsrc", [P, 4]), sb("e_ownz", [P, 4])
        fetched, fetched_sum = sb("e_fetched", [P, STEPS, 24]), sb("e_fetchedsum", [P, STEPS, 8])
        z = sb("e_z", [P, S4 + 4])
        ex = sb("e_ex", [P, 2, S4 + 4])
        agg, den = sb("e_agg", [P, D]), sb("e_den", [P, 4])
        b_gat = sb("e_bgat", [P, D])
        gat_neg, gat = sb("e_gatneg", [P, D]), sb("e_gat", [P, 2, D])
        conv_in = sb("e_conv", [P, 2, 6, P])
        bn_mv, bn_a, bn_b, bn_t, gamma, beta = sb("e_bnmv", [P, 6, 2]), sb("e_bna", [P, 6]), sb("e_bnb", [P, 6]), sb("e_bnt", [P, 6]), sb("e_gamma", [P, 6]), sb("e_beta", [P, 6])
        w_dw, w_pw = sb("e_wdw", [P, 6]), sb("e_wpw", [P, 6, P])
        cat = sb("e_cat", [P, 16, 96])
        squares = sb("e_squares", [P, 2 * CQ])
        norm2, r1, t1, scale1 = sb("e_norm2", [P, 1]), sb("e_r1", [P, 1]), sb("e_t1", [P, 1]), sb("e_scale1", [P, 1])
        k_sum, mixed, divisor = sb("e_ksum", [P, 16]), sb("e_mixed", [P, 16, 32]), sb("e_divisor", [P, 16, 32])
        norm3, scale3 = sb("e_norm3", [P, 1]), sb("e_scale3", [P, 1])
        mixed_t, w_res, b_res = sb("e_mixedt", [P, 4, P]), sb("e_wres", [P, 4, D]), sb("e_bres", [P, D])
        ft, norm4, r4, tanh4, length4 = sb("e_ft", [P, D]), sb("e_norm4", [P, 1]), sb("e_r4", [P, 1]), sb("e_tanh4", [P, 1]), sb("e_length4", [P, 1])
        xf, xf_t = sb("e_xf", [P, D]), sb("e_xft", [P, 2, P])
        stats, mv, rs = sb("e_stats", [P, 6]), sb("e_mv", [P, 2]), sb("e_rs", [P, 1])
        s_w1, s_w2, s_w3 = sb("e_sw1", [P, 2, D]), sb("e_sw2", [P, 2, P]), sb("e_sw3", [P, D])
        x_w1, x_w2, x_w3 = sb("e_xw1", [P, 4, 2, P]), sb("e_xw2", [P, 4, 64]), sb("e_xw3", [64, 4, D])
        s_b1, s_b2, x_b1, x_b2 = sb("e_sb1", [P, 2]), sb("e_sb2", [P, 1]), sb("e_xb1", [P, 4]), sb("e_xb2", [64, 4])
        out_b = sb("e_outb", [5, D])
        g_w, g_b = sb("e_gw", [P, 2, 4]), sb("e_gb", [P, 4])
        hid_s, hid_x, hid_s2, hid_x2 = sb("e_hids", [P, 2, P]), sb("e_hidx", [P, 4, P]), sb("e_hids2", [P, P]), sb("e_hidx2", [64, 4, P])
        gate, gate_e, gate_m, gate_s = sb("e_gate", [P, 8]), sb("e_gatee", [P, 4]), sb("e_gatem", [P, 1]), sb("e_gates", [P, 1])
        top, best, best_f, gap, ratio, share = sb("e_top", [P, 8]), sb("e_best", [P, 8], U32), sb("e_bestf", [P, 8]), sb("e_gap", [P, 1]), sb("e_ratio", [P, 1]), sb("e_share", [P, 2])
        weight, second, weight_t = sb("e_weightx", [P, 5]), sb("e_second", [P, 4]), sb("e_weightt", [5, P])
        result = sb("e_result", [P, 2, D])
        st_ps = [bank("e_st0", BF16), bank("e_st1", BF16)]
        sc_ps, agg_ps, m_ps, f_ps = bank("e_sc"), bank("e_aggps"), [bank("e_m0"), bank("e_m1")], [bank("e_f0"), bank("e_f1")]
        names = ("weights identh sources_ready gathers_begun messages_free own_free spread_ready spreadh_ready scores_ready turned_rows rows_ready "
                 "run_ready run_turned st_done st_copied runh_ready picked_done picked_ready nodeh_ready fetched_done fetched_ready "
                 "z_ready ex_ready scaled agg_done gat_neg gat_exp "
                 "bn_ready h_in lifted m_done m_copied norm2_ready scale1_ready scaled_cat mixed_ready norm3_ready mixed_turned mixedt_ready res_done "
                 "ft_ready norm4_ready length_ready tanh_ready x3_ready "
                 "xf_ready xf_turned xft_ready hidden1 hidden1_ready hidden2 hidden2_ready gate_max gate_exp gap_ready ratio_ready weight_ready weight_turned weightt_ready "
                 "shared_done expert_done expert_used result_ready").split()
        s = {n: sem("e_" + n) for n in names}
        messages_in = [sem("e_messages_in0"), sem("e_messages_in1")]
        own_in = [sem("e_own_in0"), sem("e_own_in1")]
        conv_loaded = [sem("e_conv_in0"), sem("e_conv_in1")]
        result_out = [sem("e_result_out0"), sem("e_result_out1")]
        LOADS = 16 * 28
        block = ctx.enter_context(nc.Block())

        def one_turn(order, chains, t, b, on):
            G, X, F = chains
            parts = {"G": G(t + 1, 1 - b) if on[0] else {}, "X": X(t, b) if on[1] else {}, "F": F(t - 1, 1 - b) if on[2] else {}}
            for name in order:
                chain, part = name.split(".")
                if part in parts[chain]:
                    parts[chain][part]()

        def turns(eng, turn):
            turn(-1, 1, True, False, False)
            turn(0, 0, True, True, False)
            with eng.Fori(0, PAIRS - 1) as i:
                turn(i * 2 + 1, 1, True, True, True)
                turn(i * 2 + 2, 0, True, True, True)
            turn(T - 2, 1, True, True, True)
            turn(T - 1, 0, False, True, True)
            turn(T, 1, False, False, True)

        @block.sync
        def _(sp):
            def load(out, src):
                sp.dma_start(out, src).then_inc(s["weights"], 16)
            load(w_res[:, :, :], g.w["L1_mix_w_res"][:, 0, :].rearrange("(c p) n -> p c n", p=P))
            load(s_w1[:, :, :], g.w["L1_ffn_sW1"].rearrange("(c p) n -> p c n", p=P))
            load(s_w2[:, :, :], g.w["L1_ffn_sW2"].rearrange("(c p) n -> p c n", p=P))
            load(s_w3[:, :], g.w["L1_ffn_sW3"])
            load(x_w1[:, :, :, :], g.w["L1_ffn_eW1"].rearrange("e (c p) n -> p e c n", p=P))
            load(x_w2[:, :, :], g.w["L1_ffn_eW2"].rearrange("e p n -> p e n"))
            load(x_w3[:, :, :], g.w["L1_ffn_eW3"].rearrange("e p n -> p e n"))
            load(out_b[0:4, :], g.w["L1_ffn_eb3"])
            load(out_b[4:5, :], row(g.w["L1_ffn_sb3"], 1))
            load(g_w[:, :, :], g.w["L1_ffn_gW"].rearrange("(c p) n -> p c n", p=P))
            load(g_b[:, :], row(g.w["L1_ffn_gb"]))
            load(b_gat[:, :], row(g.w["L1_gnn_bias"]))
            load(b_res[:, :], row(g.w["L1_mix_b_res"]))
            for out, vector in ((gamma, g.w["L1_mix_bn_gamma"]), (beta, g.w["L1_mix_bn_beta"]), (w_dw, g.w["L1_mix_w_dw"][0, 2, :]),
                                (s_b1, g.w["L1_ffn_sb1"]), (s_b2, g.w["L1_ffn_sb2"]), (x_b1, g.w["L1_ffn_eb1"].rearrange("e n -> (e n)"))):
                load_columns(sp, out[:, :], vector).then_inc(s["weights"], 16)
            sp.dma_start(x_b2[:, :], g.w["L1_ffn_eb2"].rearrange("e n -> n e"), allow_slow_non_contiguous=True).then_inc(s["weights"], 16)
            sp.wait_ge(s["identh"], 1)
            for r in range(4):
                part = slice(32 * r, 32 * r + 32)
                load(w_pw[part, :, part], g.w["L1_mix_w_pw"][:, 0, :].rearrange("p (c r n) -> p c r n", r=4, n=32)[:, :, r, :])
            load(own[:, 0, :], g.att_table[0:P, :])
            load(own[:, 1, :], g.att_table[P:2 * P, :])
            load(conv_in[:, 0, :, :], g.conv[0, :, :].rearrange("(c p) n -> p c n", p=P))
            load(conv_in[:, 1, :, :], g.conv[1, :, :].rearrange("(c p) n -> p c n", p=P))

            def store(t, b):
                sp.wait_ge(s["result_ready"], t + 1)
                sp.dma_start(g.out[bass.ds(t * P, P), :], result[:, b, :]).then_inc(result_out[b], 16)

            def refill(t, b):
                sp.wait_ge(s["own_free"], t - 1)
                sp.dma_start(own[:, b, :], g.att_table[bass.ds(t * P, P), :]).then_inc(own_in[b], 16)
                sp.wait_ge(s["lifted"], t - 1)
                sp.dma_start(conv_in[:, b, :, :], g.conv[bass.ds(t, 1), :, :].rearrange("a (c p) n -> p (a c) n", p=P)).then_inc(conv_loaded[b], 16)

            refill(2, 0)
            with sp.Fori(0, PAIRS - 1) as i:
                refill(i * 2 + 3, 1)
                store(i * 2, 0)
                refill(i * 2 + 4, 0)
                store(i * 2 + 1, 1)
            store(T - 3, 0)
            store(T - 2, 1)
            store(T - 1, 0)
            sp.wait_ge(result_out[0], 16 * ((T + 1) // 2))
            sp.wait_ge(result_out[1], 16 * (T // 2))

        @block.gpsimd
        def _(pool):
            pool.memset(w_pw[:, :, :], 0.0)
            pool.drain()
            pool.tensor_copy(ident_h[:, :], g.ident[:, :]).then_inc(s["identh"], 1)

            def step(t, b):
                pool.wait_ge(s["messages_free"], t + 1)
                pool.tensor_copy(sources[:, b, :], g.e_src[:, bass.ds(t * STEPS, STEPS)]).then_inc(s["sources_ready"], 1)
                pool.wait_ge(s["sources_ready"], t + 1)
                pool.sem_inc(s["gathers_begun"], 1)
                for j in range(STEPS):
                    pool.indirect_dma_start(messages[:, b, j, :], None, g.att_table[:, :],
                                            bass.IndirectOffsetOnAxis(ap=sources[:, b, j:j + 1], axis=0)).then_inc(messages_in[b], 16)
            over_pairs(pool, step)

        @block.scalar
        def _(act):
            def G(t, b):
                def halves():
                    act.wait_ge(s["agg_done"], t)
                    act.wait_ge(s["spread_ready"], t + 1)
                    act.copy(spread_h[:, :, :], spread[:, :, :]).then_inc(s["spreadh_ready"], 1)

                def rows_():
                    act.wait_ge(s["turned_rows"], t + 1)
                    act.copy(rows_t[:, :], sc_ps[0:S4, 0:2 * P]).then_inc(s["rows_ready"], 1)

                def turned():
                    for r in range(3):
                        act.wait_ge(s["st_done"], t * 3 + r + 1)
                        act.copy(spread_t[:, r * 6:r * 6 + 6, :], st_ps[r % 2][:, 0:6 * P].rearrange("p (j n) -> p j n", j=6)).then_inc(s["st_copied"], 1)

                def picks():
                    act.wait_ge(s["picked_done"], t + 1)
                    act.copy(picked[:, :, :], sc_ps[:, 0:STEPS * 13].rearrange("p (j n) -> p j n", j=STEPS)).then_inc(s["picked_ready"], 1)

                def fetches():
                    act.wait_ge(s["fetched_done"], t + 1)
                    act.copy(fetched[:, :, :], sc_ps[:, 0:STEPS * 24].rearrange("p (j n) -> p j n", j=STEPS)).then_inc(s["fetched_ready"], 1)

                def exps():
                    act.wait_ge(s["z_ready"], t + 1)
                    act.activation(ex[:, b, :], z[:, :], ACT.Exp).then_inc(s["ex_ready"], 1)

                def elu():
                    act.wait_ge(s["gat_neg"], t + 1)
                    act.activation(gat_neg[:, :], gat_neg[:, :], ACT.Exp).then_inc(s["gat_exp"], 1)
                return {"halves": halves, "rows": rows_, "turned": turned, "picks": picks, "fetches": fetches, "exps": exps, "elu": elu}

            def X(t, b):
                def relu():
                    act.wait_ge(conv_loaded[b], uses_before(t, b))
                    for c in range(6):
                        last = act.activation(conv_in[:, b, c, :], conv_in[:, b, c, :], ACT.Relu, bias=bn_b[:, c:c + 1], scale=bn_a[:, c:c + 1])
                    last.then_inc(s["h_in"], 1)

                def copies():
                    flat = cat[:, :, :].rearrange("p a n -> p (a n)")
                    act.wait_ge(s["mixed_ready"], t)
                    for r in range(2):
                        act.wait_ge(s["m_done"], t * 2 + r + 1)
                        act.copy(flat[:, r * 384:r * 384 + 384], m_ps[0][:, 0:384])
                        act.copy(flat[:, CQ + r * 384:CQ + r * 384 + 384], m_ps[1][:, 0:384]).then_inc(s["m_copied"], 1)
                    act.drain()
                    act.activation(squares[:, :], flat, ACT.Square, accum_out=norm2[:, :]).then_inc(s["norm2_ready"], 1)

                def scale():
                    act.wait_ge(s["scale1_ready"], t + 1)
                    act.activation(cat[:, :, 0:64], cat[:, :, 0:64], ACT.Relu, scale=scale1[:, :])
                    act.activation(cat[:, :, 64:96], cat[:, :, 64:96], ACT.Copy, scale=scale1[:, :]).then_inc(s["scaled_cat"], 1)

                def square3():
                    act.wait_ge(s["mixed_ready"], t + 1)
                    act.activation(squares[:, 0:512], mixed[:, :, :].rearrange("p a n -> p (a n)"), ACT.Square, accum_out=norm3[:, :]).then_inc(s["norm3_ready"], 1)

                def turned():
                    act.wait_ge(s["mixed_turned"], t + 1)
                    act.copy(mixed_t[:, :, :], f_ps[0][:, :].rearrange("p (c n) -> p c n", c=4)).then_inc(s["mixedt_ready"], 1)

                def square4():
                    act.drain()
                    act.wait_ge(s["ft_ready"], t + 1)
                    act.activation(squares[:, 0:D], ft[:, :], ACT.Square, accum_out=norm4[:, :]).then_inc(s["norm4_ready"], 1)

                def tanh():
                    act.wait_ge(s["length_ready"], t + 1)
                    act.activation(tanh4[:, :], length4[:, :], ACT.Tanh).then_inc(s["tanh_ready"], 1)
                return {"relu": relu, "copies": copies, "scale": scale, "square3": square3, "turned": turned, "square4": square4, "tanh": tanh}

            def F(t, b):
                def turned():
                    act.wait_ge(s["xf_turned"], t + 1)
                    act.copy(xf_t[:, :, :], f_ps[0][:, 0:D].rearrange("p (c n) -> p c n", c=2)).then_inc(s["xft_ready"], 1)

                def layer_1():
                    act.wait_ge(s["hidden1"], t + 1)
                    for c in range(2):
                        act.activation(hid_s[:, c, :], f_ps[1][:, c * P:(c + 1) * P], ACT.Relu, bias=s_b1[:, c:c + 1])
                    for e in range(4):
                        last = act.activation(hid_x[:, e, :], f_ps[0][:, e * P:(e + 1) * P], ACT.Relu, bias=x_b1[:, e:e + 1])
                    last.then_inc(s["hidden1_ready"], 1)

                def gates():
                    act.wait_ge(s["gate_max"], t + 1)
                    act.activation(gate_e[:, :], gate[:, 0:4], ACT.Exp, bias=gate_m[:, :], accum_out=gate_s[:, :]).then_inc(s["gate_exp"], 1)

                def layer_2():
                    act.wait_ge(s["hidden2"], t + 1)
                    act.activation(hid_s2[:, :], f_ps[1][:, 0:P], ACT.Relu, bias=s_b2[:, :])
                    for e in range(4):
                        last = act.activation(hid_x2[:, e, :], f_ps[0][0:64, e * P:(e + 1) * P], ACT.Relu, bias=x_b2[:, e:e + 1])
                    last.then_inc(s["hidden2_ready"], 1)

                def ratios():
                    act.wait_ge(s["gap_ready"], t + 1)
                    act.activation(ratio[:, :], gap[:, :], ACT.Exp).then_inc(s["ratio_ready"], 1)

                def weights():
                    act.wait_ge(s["weight_turned"], t + 1)
                    act.copy(weight_t[:, :], m_ps[0][0:5, 0:P]).then_inc(s["weightt_ready"], 1)
                return {"turned": turned, "layer_1": layer_1, "gates": gates, "layer_2": layer_2, "ratios": ratios, "weights": weights}

            ORDER = ("G.halves F.turned X.relu G.rows X.copies G.turned F.layer_1 F.gates X.scale G.picks F.layer_2 F.ratios X.square3 "
                     "G.fetches F.weights X.turned G.exps X.square4 X.tanh G.elu").split()
            act.wait_ge(s["weights"], LOADS)
            act.wait_ge(s["bn_ready"], 1)

            def turn(t, b, *on):
                one_turn(ORDER, (G, X, F), t, b, on)
            turns(act, turn)

        @block.vector
        def _(dve):
            def rows(t):
                return g.xn[:, bass.ds(t, 1), :].rearrange("p a n -> p (a n)")

            def heads(x):
                return x.rearrange("p (h n) -> p h n", h=4)

            def wide(x, n):
                return x.unsqueeze(2).broadcast_to([P, x.shape[1], n])

            def G(t, b):
                at = bass.ds(t * STEPS, STEPS)

                def build():
                    dve.wait_ge(s["agg_done"], t)
                    dve.wait_ge(s["spreadh_ready"], t)
                    for j in range(STEPS):
                        last = dve.tensor_scalar(spread[:, j, :], g.node[:, :], g.e_dst[:, bass.ds(t * STEPS + j, 1)], None, ALU.is_equal)
                    last.then_inc(s["spread_ready"], 1)
                    dve.wait_ge(messages_in[b], uses_before(t, b) * STEPS + 16 * STEPS)
                    dve.tensor_copy(score[:, :, :], messages[:, b, :, D:TBL])
                    dve.tensor_copy(first[:, :, :], wide(g.e_first[:, at], 4)).then_inc(s["scores_ready"], 1)

                def scan():
                    dve.wait_ge(s["rows_ready"], t + 1)
                    dve.tensor_tensor_scan(run[:, :], rows_t[:, P:2 * P], rows_t[:, 0:P], -BIG, ALU.add, ALU.max).then_inc(s["run_ready"], 1)

                def last_of_run():
                    dve.wait_ge(s["run_turned"], t + 1)
                    dve.tensor_tensor(run_last[:, :, :], sc_ps[:, 2 * P:2 * P + S4].rearrange("p (j n) -> p j n", j=STEPS), wide(g.e_last[:, at], 4), ALU.mult)
                    dve.tensor_copy(run_h[:, :, 12:13], wide(g.e_last[:, at], 1))
                    dve.drain()
                    split_bf16(dve, [run_h[:, :, 4 * k:4 * k + 4] for k in range(3)], run_last[:, :, :], rest[:, :, :])
                    dve.drain()
                    dve.sem_inc(s["runh_ready"], 1)

                def node_max():
                    dve.wait_ge(s["picked_ready"], t + 1)
                    dve.tensor_tensor(picked_sum[:, :, :], picked[:, :, 0:4], picked[:, :, 4:8], ALU.add)
                    dve.tensor_scalar(absent[:, :, :], picked[:, :, 12:13], -1.0, BIG, ALU.add, ALU.mult)
                    dve.drain()
                    dve.tensor_tensor(picked_sum[:, :, :], picked_sum[:, :, :], picked[:, :, 8:12], ALU.add)
                    dve.drain()
                    dve.tensor_tensor(picked_sum[:, :, :], picked_sum[:, :, :], absent[:, :, :].broadcast_to([P, STEPS, 4]), ALU.add)
                    dve.drain()
                    dve.tensor_reduce(top_src[:, :], picked_sum[:, :, :].rearrange("p j h -> p h j"), AX.X, ALU.max)
                    dve.drain()
                    dve.wait_ge(own_in[b], uses_before(t, b))
                    dve.tensor_tensor(top_src[:, :], top_src[:, :], own[:, b, D:TBL], ALU.max)
                    a_dst = g.a_dst[:, bass.ds(t, 1), :].rearrange("p a n -> p (a n)")
                    dve.tensor_copy(per_node[:, 0:4], a_dst)
                    dve.tensor_tensor(own_z[:, :], own[:, b, D:TBL], a_dst, ALU.add)
                    dve.drain()
                    dve.tensor_tensor(top_src[:, :], top_src[:, :], a_dst, ALU.add)
                    dve.drain()
                    dve.scalar_tensor_tensor(per_node[:, 4:8], top_src[:, :], 0.2, top_src[:, :], ALU.mult, ALU.max)
                    dve.scalar_tensor_tensor(own_z[:, :], own_z[:, :], 0.2, own_z[:, :], ALU.mult, ALU.max)
                    dve.drain()
                    dve.tensor_tensor(z[:, S4:S4 + 4], own_z[:, :], per_node[:, 4:8], ALU.subtract)
                    split_bf16(dve, [node_h[:, k, :] for k in range(3)], per_node[:, :], node_rest[:, :])
                    dve.drain()
                    dve.sem_inc(s["nodeh_ready"], 1)

                def exponents():
                    dve.wait_ge(s["fetched_ready"], t + 1)
                    dve.tensor_tensor(fetched_sum[:, :, :], fetched[:, :, 0:8], fetched[:, :, 8:16], ALU.add)
                    dve.drain()
                    dve.tensor_tensor(fetched_sum[:, :, :], fetched_sum[:, :, :], fetched[:, :, 16:24], ALU.add)
                    dve.drain()
                    dve.tensor_tensor(score[:, :, :], score[:, :, :], fetched_sum[:, :, 0:4], ALU.add)
                    dve.drain()
                    dve.scalar_tensor_tensor(score[:, :, :], score[:, :, :], 0.2, score[:, :, :], ALU.mult, ALU.max)
                    dve.drain()
                    dve.tensor_tensor(score[:, :, :], score[:, :, :], fetched_sum[:, :, 4:8], ALU.subtract)
                    dve.drain()
                    dve.tensor_scalar(z[:, 0:S4], score[:, :, :].rearrange("p j h -> p (j h)"), 0.0, None, ALU.min).then_inc(s["z_ready"], 1)

                def scale():
                    dve.wait_ge(s["ex_ready"], t + 1)
                    for half in range(2):
                        part = slice(half * HALF, half * HALF + HALF)
                        e = ex[:, b, half * HALF * 4:(half + 1) * HALF * 4]
                        for j in range(half * HALF, half * HALF + HALF):
                            mj = heads(messages[:, b, j, 0:D])
                            dve.tensor_tensor(mj, mj, wide(ex[:, b, 4 * j:4 * j + 4], 64), ALU.mult)
                        dve.tensor_copy(messages[:, b, part, D:TBL], e.rearrange("p (j h) -> p j h", h=4)).then_inc(s["scaled"], 1)

                def finish():
                    dve.wait_ge(s["agg_done"], t + 1)
                    own_ex = ex[:, b, S4:S4 + 4]
                    dve.tensor_tensor(heads(own[:, b, 0:D]), heads(own[:, b, 0:D]), wide(own_ex, 64), ALU.mult)
                    dve.tensor_tensor(den[:, :], agg_ps[:, D:TBL], own_ex, ALU.add)
                    dve.drain()
                    dve.reciprocal(den[:, :], den[:, :])
                    dve.tensor_tensor(agg[:, :], agg_ps[:, 0:D], own[:, b, 0:D], ALU.add)
                    dve.drain()
                    dve.tensor_tensor(heads(agg[:, :]), heads(agg[:, :]), wide(den[:, :], 64), ALU.mult)
                    dve.drain()
                    dve.tensor_tensor(agg[:, :], agg[:, :], b_gat[:, :], ALU.add)
                    dve.drain()
                    dve.tensor_scalar(gat_neg[:, :], agg[:, :], 0.0, None, ALU.min).then_inc(s["gat_neg"], 1)
                    dve.sem_inc(s["own_free"], 1)
                    dve.wait_ge(s["gat_exp"], t + 1)
                    dve.scalar_tensor_tensor(gat[:, b, :], agg[:, :], 0.0, gat_neg[:, :], ALU.max, ALU.add)
                    dve.drain()
                    dve.tensor_scalar(gat[:, b, :], gat[:, b, :], -1.0, None, ALU.add)
                    dve.drain()
                return {"build": build, "scan": scan, "last_of_run": last_of_run, "node_max": node_max, "exponents": exponents, "scale": scale, "finish": finish}

            def X(t, b):
                def scale_1():
                    dve.wait_ge(s["norm2_ready"], t + 1)
                    dve.tensor_scalar(norm2[:, :], norm2[:, :], 1e-30, None, ALU.max)
                    dve.drain()
                    newton_rsqrt(dve, r1[:, :], norm2[:, :], t1[:, :])
                    dve.tensor_scalar(scale1[:, :], r1[:, :], ATANH_MAX, 1.0, ALU.mult, ALU.min).then_inc(s["scale1_ready"], 1)

                def attend():
                    dve.wait_ge(s["scaled_cat"], t + 1)
                    dve.wait_ge(s["mixedt_ready"], t)
                    dve.wait_ge(s["norm3_ready"], t)
                    q, k, v = cat[:, :, 0:32], cat[:, :, 32:64], cat[:, :, 64:96]
                    dve.tensor_scalar(divisor[:, :, :], v, 1e-15, None, ALU.add)
                    dve.reduce_sum(k_sum[:, :], k, axis=AX.X)
                    dve.drain()
                    dve.reciprocal(divisor[:, :, :], divisor[:, :, :])
                    dve.tensor_tensor(mixed[:, :, :], v, wide(k_sum[:, :], 32), ALU.mult)
                    dve.drain()
                    dve.tensor_tensor(mixed[:, :, :], mixed[:, :, :], q, ALU.mult)
                    dve.drain()
                    dve.tensor_tensor(mixed[:, :, :], mixed[:, :, :], divisor[:, :, :], ALU.mult).then_inc(s["mixed_ready"], 1)

                def scale_3():
                    dve.wait_ge(s["norm3_ready"], t + 1)
                    dve.tensor_scalar(norm3[:, :], norm3[:, :], 1e-30, None, ALU.max)
                    dve.drain()
                    newton_rsqrt(dve, r1[:, :], norm3[:, :], t1[:, :])
                    dve.tensor_scalar(scale3[:, :], r1[:, :], ATANH_MAX, 1.0, ALU.mult, ALU.min)
                    dve.drain()

                def tangent():
                    dve.wait_ge(s["res_done"], t + 1)
                    dve.scalar_tensor_tensor(ft[:, :], f_ps[1][:, 0:D], scale3[:, :], b_res[:, :], ALU.mult, ALU.add).then_inc(s["ft_ready"], 1)

                def length():
                    dve.wait_ge(s["norm4_ready"], t + 1)
                    dve.tensor_scalar(norm4[:, :], norm4[:, :], 1e-30, None, ALU.max)
                    dve.drain()
                    newton_rsqrt(dve, r4[:, :], norm4[:, :], t1[:, :])
                    dve.tensor_tensor(length4[:, :], norm4[:, :], r4[:, :], ALU.mult).then_inc(s["length_ready"], 1)

                def sum_up():
                    dve.wait_ge(s["tanh_ready"], t + 1)
                    dve.scalar_tensor_tensor(length4[:, :], tanh4[:, :], MAXNORM, r4[:, :], ALU.min, ALU.mult)
                    dve.tensor_tensor(gat[:, b, :], gat[:, b, :], rows(t), ALU.add)
                    dve.drain()
                    dve.scalar_tensor_tensor(rows(t), ft[:, :], length4[:, :], gat[:, b, :], ALU.mult, ALU.add)
                    dve.drain()
                    dve.sem_inc(s["x3_ready"], 1)
                return {"scale_1": scale_1, "attend": attend, "scale_3": scale_3, "tangent": tangent, "length": length, "sum_up": sum_up}

            def F(t, b):
                def norm():
                    normalise(dve, xf[:, :], rows(t), stats[:, :], mv[:, :], rs[:, :], t1[:, :],
                              lambda: dve.wait_ge(s["xf_turned"], t))
                    dve.drain()
                    dve.sem_inc(s["xf_ready"], 1)

                def gate_1():
                    dve.wait_ge(s["hidden1"], t + 1)
                    dve.tensor_tensor(gate[:, 0:4], m_ps[1][:, 0:4], g_b[:, :], ALU.add)
                    dve.drain()
                    dve.tensor_reduce(gate_m[:, :], gate[:, 0:4], AX.X, ALU.max)
                    dve.drain()
                    dve.tensor_scalar(gate_m[:, :], gate_m[:, :], -1.0, None, ALU.mult).then_inc(s["gate_max"], 1)

                def gate_2():
                    dve.wait_ge(s["gate_exp"], t + 1)
                    dve.reciprocal(gate_s[:, :], gate_s[:, :])
                    dve.drain()
                    dve.tensor_scalar(gate[:, 0:4], gate_e[:, :], gate_s[:, :], None, ALU.mult)
                    dve.drain()
                    dve.max(top[:, :], gate[:, :])
                    dve.drain()
                    dve.tensor_tensor(gap[:, :], top[:, 1:2], top[:, 0:1], ALU.subtract).then_inc(s["gap_ready"], 1)
                    dve.max_index(best[:, :], top[:, :], gate[:, :])
                    dve.drain()
                    dve.tensor_copy(best_f[:, :], best[:, :])

                def gate_3():
                    dve.wait_ge(s["ratio_ready"], t + 1)
                    dve.tensor_scalar(share[:, 0:1], ratio[:, :], 1.0, None, ALU.add)
                    dve.drain()
                    dve.reciprocal(share[:, 0:1], share[:, 0:1])
                    dve.drain()
                    dve.tensor_tensor(share[:, 1:2], share[:, 0:1], ratio[:, :], ALU.mult)
                    dve.drain()
                    dve.tensor_scalar(weight[:, 0:4], g.node[:, 0:4], best_f[:, 0:1], share[:, 0:1], ALU.is_equal, ALU.mult)
                    dve.tensor_scalar(second[:, :], g.node[:, 0:4], best_f[:, 1:2], share[:, 1:2], ALU.is_equal, ALU.mult)
                    dve.drain()
                    dve.tensor_tensor(weight[:, 0:4], weight[:, 0:4], second[:, :], ALU.add).then_inc(s["weight_ready"], 1)

                def outputs():
                    dve.wait_ge(s["shared_done"], t + 1)
                    dve.wait_ge(result_out[b], uses_before(t, b))
                    res = result[:, b, :]
                    dve.tensor_tensor(res, rows(t), f_ps[1][:, 0:D], ALU.add)
                    for e, ps_ in enumerate((f_ps[0], m_ps[0], m_ps[1], f_ps[0])):
                        dve.drain()
                        dve.wait_ge(s["expert_done"], t * 4 + e + 1)
                        last = dve.scalar_tensor_tensor(res, ps_[:, 0:D], weight[:, e:e + 1], res, ALU.mult, ALU.add)
                        if e < 3:
                            last.then_inc(s["expert_used"], 1)
                    dve.drain()
                    dve.sem_inc(s["expert_used"], 1)
                    dve.sem_inc(s["result_ready"], 1)
                return {"norm": norm, "gate_1": gate_1, "gate_2": gate_2, "gate_3": gate_3, "outputs": outputs}

            ORDER = ("G.build F.norm G.scan F.gate_1 X.scale_1 G.last_of_run F.gate_2 X.attend G.node_max F.gate_3 X.scale_3 "
                     "G.exponents F.outputs G.scale X.tangent X.length G.finish X.sum_up").split()

            def turn(t, b, *on):
                one_turn(ORDER, (G, X, F), t, b, on)
            dve.memset(gate[:, :], -1.0)
            dve.memset(weight[:, 4:5], 1.0)
            dve.sem_inc(s["messages_free"], 2)
            dve.wait_ge(s["weights"], LOADS)
            for c in range(6):
                dve.bn_aggr(bn_mv[:, c, :], g.conv_stats[:, c, :, :].rearrange("p a n -> p (a n)"))
            dve.drain()
            ma, va = bn_mv[:, :, 0], bn_mv[:, :, 1]
            dve.tensor_tensor(bn_t[:, :], ma, ma, ALU.mult)
            dve.drain()
            dve.tensor_scalar(bn_t[:, :], bn_t[:, :], -float(NP) * (NP - N) / float(N) ** 2, EPS, ALU.mult, ALU.add)
            dve.tensor_scalar(va, va, float(NP) / N, None, ALU.mult)
            dve.tensor_scalar(ma, ma, float(NP) / N, None, ALU.mult)
            dve.drain()
            dve.tensor_tensor(bn_t[:, :], bn_t[:, :], va, ALU.add)
            dve.drain()
            newton_rsqrt(dve, bn_a[:, :], bn_t[:, :], bn_b[:, :])
            dve.tensor_tensor(bn_a[:, :], bn_a[:, :], gamma[:, :], ALU.mult)
            dve.drain()
            dve.tensor_tensor(bn_t[:, :], ma, bn_a[:, :], ALU.mult)
            dve.tensor_tensor(w_pw[:, :, :], w_pw[:, :, :], wide(w_dw[:, :], P), ALU.mult)
            dve.drain()
            dve.tensor_tensor(bn_b[:, :], beta[:, :], bn_t[:, :], ALU.subtract)
            dve.drain()
            dve.sem_inc(s["bn_ready"], 1)
            turns(dve, turn)

        @block.tensor
        def _(pe):
            def G(t, b):
                def scores():
                    pe.wait_ge(s["scores_ready"], t + 1)
                    pe.wait_ge(s["fetched_ready"], t)
                    pe.transpose(sc_ps[0:S4, 0:P], score[:, :, :].rearrange("p j h -> p (j h)"), g.ident[:, :])
                    pe.transpose(sc_ps[0:S4, P:2 * P], first[:, :, :].rearrange("p j h -> p (j h)"), g.ident[:, :]).then_inc(s["turned_rows"], 1)

                def turn_spread():
                    pe.wait_ge(s["spreadh_ready"], t + 1)
                    for r in range(3):
                        if r == 0:
                            pe.wait_ge(s["st_copied"], t * 3)
                        if r == 2:
                            pe.wait_ge(s["st_copied"], t * 3 + 1)
                        for j in range(6):
                            last = pe.transpose(st_ps[r % 2][:, j * P:(j + 1) * P], spread_h[:, r * 6 + j, :], ident_h[:, :])
                        last.then_inc(s["st_done"], 1)

                def turn_run():
                    pe.wait_ge(s["run_ready"], t + 1)
                    pe.transpose(sc_ps[:, 2 * P:2 * P + S4], run[:, :], g.ident[0:S4, 0:S4]).then_inc(s["run_turned"], 1)

                def pick():
                    pe.wait_ge(s["runh_ready"], t + 1)
                    for j in range(STEPS):
                        last = pe.matmul(sc_ps[:, j * 13:(j + 1) * 13], spread_h[:, j, :], run_h[:, j, :], start=True, stop=True)
                    last.then_inc(s["picked_done"], 1)

                def fetch():
                    pe.wait_ge(s["nodeh_ready"], t + 1)
                    pe.wait_ge(s["st_copied"], t * 3 + 3)
                    for j in range(STEPS):
                        last = pe.matmul(sc_ps[:, j * 24:(j + 1) * 24], spread_t[:, j, :], node_h[:, :, :].rearrange("p k n -> p (k n)"), start=True, stop=True)
                    last.then_inc(s["fetched_done"], 1)

                def sums():
                    for half in range(2):
                        pe.wait_ge(s["scaled"], t * 2 + half + 1)
                        if half == 0:
                            pe.wait_ge(s["gat_neg"], t)
                        for j in range(half * HALF, half * HALF + HALF):
                            last = pe.matmul(agg_ps[:, 0:TBL], spread[:, j, :], messages[:, b, j, :], start=j == 0, stop=j == STEPS - 1)
                    last.then_inc(s["agg_done"], 1)
                    pe.wait_ge(s["agg_done"], t + 1)
                    pe.sem_inc(s["messages_free"], 1)
                return {"scores": scores, "turn_spread": turn_spread, "turn_run": turn_run, "pick": pick, "fetch": fetch, "sums": sums}

            def X(t, b):
                def lift():
                    pe.wait_ge(s["h_in"], t + 1)
                    for r in range(2):
                        pe.wait_ge(s["m_copied"], t * 2 + r)
                        for c in range(3):
                            pe.transpose(m_ps[0][:, c * P:(c + 1) * P], conv_in[:, b, r * 3 + c, :], g.ident[:, :])
                        for c in range(3):
                            last = pe.matmul(m_ps[1][:, c * P:(c + 1) * P], conv_in[:, b, r * 3 + c, :], w_pw[:, r * 3 + c, :], start=True, stop=True)
                        last.then_inc(s["m_done"], 1)
                    pe.wait_ge(s["m_done"], t * 2 + 2)
                    pe.sem_inc(s["lifted"], 1)

                def turn_mixed():
                    pe.wait_ge(s["mixed_ready"], t + 1)
                    pe.wait_ge(s["expert_used"], t * 4)
                    for c in range(4):
                        last = pe.transpose(f_ps[0][:, c * P:(c + 1) * P], mixed[:, c * 4:c * 4 + 4, :].rearrange("p a n -> p (a n)"), g.ident[:, :])
                    last.then_inc(s["mixed_turned"], 1)

                def residual():
                    pe.wait_ge(s["mixedt_ready"], t + 1)
                    for c in range(4):
                        last = pe.matmul(f_ps[1][:, 0:D], mixed_t[:, c, :], w_res[:, c, :], start=c == 0, stop=c == 3)
                    last.then_inc(s["res_done"], 1)
                return {"lift": lift, "turn_mixed": turn_mixed, "residual": residual}

            def F(t, b):
                def turned():
                    pe.wait_ge(s["xf_ready"], t + 1)
                    pe.wait_ge(s["mixedt_ready"], t + 1)
                    for c in range(2):
                        last = pe.transpose(f_ps[0][:, c * P:(c + 1) * P], xf[:, c * P:(c + 1) * P], g.ident[:, :])
                    last.then_inc(s["xf_turned"], 1)

                def layer_1():
                    pe.wait_ge(s["xft_ready"], t + 1)
                    pe.wait_ge(s["ft_ready"], t + 1)
                    pe.wait_ge(s["m_copied"], 2 * T if isinstance(t, int) and t == T - 1 else t * 2 + 4)
                    for c in range(2):
                        pe.matmul(m_ps[1][:, 0:4], xf_t[:, c, :], g_w[:, c, :], start=c == 0, stop=c == 1)
                    for o in range(2):
                        for c in range(2):
                            pe.matmul(f_ps[1][:, o * P:(o + 1) * P], s_w1[:, c, o * P:(o + 1) * P], xf_t[:, c, :], start=c == 0, stop=c == 1)
                    for e in range(4):
                        for c in range(2):
                            last = pe.matmul(f_ps[0][:, e * P:(e + 1) * P], x_w1[:, e, c, :], xf_t[:, c, :], start=c == 0, stop=c == 1)
                    last.then_inc(s["hidden1"], 1)

                def layer_2():
                    pe.wait_ge(s["hidden1_ready"], t + 1)
                    for c in range(2):
                        pe.matmul(f_ps[1][:, 0:P], s_w2[:, c, :], hid_s[:, c, :], start=c == 0, stop=c == 1)
                    for e in range(4):
                        last = pe.matmul(f_ps[0][0:64, e * P:(e + 1) * P], x_w2[:, e, :], hid_x[:, e, :], start=True, stop=True)
                    last.then_inc(s["hidden2"], 1)

                def weights():
                    pe.wait_ge(s["weight_ready"], t + 1)
                    pe.transpose(m_ps[0][0:5, 0:P], weight[:, :], g.ident[:, :]).then_inc(s["weight_turned"], 1)

                def outputs():
                    pe.wait_ge(s["hidden2_ready"], t + 1)
                    pe.wait_ge(s["weightt_ready"], t + 1)
                    pe.matmul(f_ps[1][:, 0:D], hid_s2[:, :], s_w3[:, :], start=True, stop=False)
                    pe.matmul(f_ps[1][:, 0:D], weight_t[:, :], out_b[:, :], start=False, stop=True).then_inc(s["shared_done"], 1)
                    for e, ps_ in enumerate((f_ps[0], m_ps[0], m_ps[1], f_ps[0])):
                        if e == 3:
                            pe.wait_ge(s["expert_used"], t * 4 + 1)
                        pe.matmul(ps_[:, 0:D], hid_x2[:, e, :], x_w3[:, e, :], start=True, stop=True).then_inc(s["expert_done"], 1)
                return {"turned": turned, "layer_1": layer_1, "layer_2": layer_2, "weights": weights, "outputs": outputs}

            ORDER = ("G.scores F.turned X.lift G.turn_spread G.turn_run F.layer_1 G.pick F.layer_2 F.weights G.fetch F.outputs "
                     "X.turn_mixed X.residual G.sums").split()

            def turn(t, b, *on):
                one_turn(ORDER, (G, X, F), t, b, on)
            pe.wait_ge(s["weights"], LOADS)
            turns(pe, turn)


WEIGHTS = ['L0_gnn_weight', 'L0_gnn_bias', 'L0_mix_Wq', 'L0_mix_bq', 'L0_mix_Wk', 'L0_mix_bk', 'L0_mix_Wv', 'L0_mix_bv',
           'L0_mix_Wo', 'L0_mix_bo', 'L0_mix_W1', 'L0_mix_b1', 'L0_mix_W2', 'L0_mix_b2', 'L0_mix_ln1_g', 'L0_mix_ln1_b',
           'L0_mix_ln2_g', 'L0_mix_ln2_b', 'L0_ffn_gamma', 'L0_ffn_beta', 'L0_ffn_Wr', 'L0_ffn_br', 'L0_ffn_W1',
           'L0_ffn_b1', 'L0_ffn_W2', 'L0_ffn_b2', 'L1_gnn_W', 'L1_gnn_att_src', 'L1_gnn_att_dst', 'L1_gnn_bias',
           'L1_mix_w_qkv', 'L1_mix_bn_gamma', 'L1_mix_bn_beta', 'L1_mix_w_dw', 'L1_mix_w_pw', 'L1_mix_w_res',
           'L1_mix_b_res', 'L1_ffn_sW1', 'L1_ffn_sb1', 'L1_ffn_sW2', 'L1_ffn_sb2', 'L1_ffn_sW3', 'L1_ffn_sb3',
           'L1_ffn_eW1', 'L1_ffn_eb1', 'L1_ffn_eW2', 'L1_ffn_eb2', 'L1_ffn_eW3', 'L1_ffn_eb3', 'L1_ffn_gW', 'L1_ffn_gb']
TURNED = {'L1_mix_w_qkv': (1, 2, 0), 'L1_mix_w_dw': (1, 2, 0), 'L1_mix_w_pw': (1, 2, 0), 'L1_mix_w_res': (1, 2, 0)}


def build(nc, g):
    with ExitStack() as ctx:
        sb = lambda n, s, d=F32: ctx.enter_context(nc.sbuf_tensor(n, s, d))
        g.ident = sb("ident", [P, P])
        g.node = sb("node", [P, P])
        g.starts = sb("starts", [P, T + 1], I32)
        g.scratch1 = sb("scratch1", [P, 1])
        g.e_src = sb("e_src", [P, T * STEPS], I32)
        g.e_dst, g.e_weight, g.e_last, g.e_first = (sb("e_" + n, [P, T * STEPS]) for n in ("dst", "weight", "last", "first"))
        g.xn = sb("nodes", [P, T, D])
        g.sup_table = nc.dram_tensor("sup_table", [NP, D], F32).ap()
        g.att_table = nc.dram_tensor("att_table", [NP, TBL], F32).ap()
        g.conv = nc.dram_tensor("conv", [T, CQ, P], F32).ap()
        build_edge_tables(nc, g)
        with ExitStack() as c2:
            sb2 = lambda n, s, d=F32: c2.enter_context(nc.sbuf_tensor(n, s, d))
            g.q_phi = sb2("q_phi", [P, 2, NP])
            g.kv, g.ksum = sb2("kv", [P, 2, P]), sb2("ksum", [P, 2, P])
            layer0_projections(nc, g)
            layer0_graph_and_attention(nc, g)
        layer0_experts(nc, g)
        g.a_dst = sb("a_dst", [P, T, 4])
        g.conv_stats = sb("conv_stats", [P, 6, T, 6])
        layer1_projections(nc, g)
        layer1_outputs(nc, g)


def declare(nc, g, arrays):
    g.w = {name: nc.dram_tensor(name, a.shape, mybir.dt.from_np(a.dtype), kind="ExternalInput").ap() for name, a in arrays.items()}
    g.x, g.src, g.dst, g.ew = g.w["x"], g.w["src"], g.w["dst"], g.w["ew"]
    g.out = nc.dram_tensor("out", (NP, D), F32, kind="ExternalOutput").ap()


def lay_out(inputs):
    arrays = {}
    x = np.zeros((NP, D), np.float32)
    x[:N] = inputs["x"]
    src = np.zeros((EPAD,), np.int32)
    src[:EDGES] = inputs["src"]
    dst = np.full((EPAD,), NODES_OF_EDGES_PAD, np.int32)
    dst[:EDGES] = inputs["dst"]
    ew = np.zeros((EPAD,), np.float32)
    ew[:EDGES] = inputs["edge_weight"]
    arrays.update(x=x, src=src, dst=dst, ew=ew)
    for name in WEIGHTS:
        a = np.asarray(inputs[name])
        arrays[name] = np.ascontiguousarray(a.transpose(TURNED[name]) if name in TURNED else a)
    return arrays


def kernel(**inputs):
    import concourse.bacc as bacc
    from concourse.bass_utils import run_bass_kernel_spmd

    nc = bacc.Bacc("TRN2", target_bir_lowering=False, num_devices=1)
    arrays = lay_out(inputs)
    g = Ctx()
    declare(nc, g, arrays)
    build(nc, g)
    r = run_bass_kernel_spmd(nc, [arrays], core_ids=[0])
    return r.results[0]["out"][:N]
```

```python
import math
from contextlib import ExitStack

import numpy as np

import concourse.bass as bass
from concourse import mybir

F32 = mybir.dt.float32
I32 = mybir.dt.int32
U32 = mybir.dt.uint32
BF16 = mybir.dt.bfloat16
ALU = mybir.AluOpType
ACT = mybir.ActivationFunctionType
AX = mybir.AxisListType

P = 128
N = 6250
D = 256
T = (N + P - 1) // P
NP = T * P
PAIRS = (T - 1) // 2
EDGES = 100000
STEPS = 18
HALF = STEPS // 2
CAP = STEPS * P
EPAD = 100096 + CAP
EC = 100096 // P
GROUP = 7
HEADS = 8
FF = 1024
NEXP, HID = 8, 512
CQ = 768
TBL = D + 12
BIG = 1.0e30
EPS = 1e-5
MAXNORM = float(np.float32(1.0 - 1e-5))
ATANH_MAX = math.atanh(MAXNORM)
NODES_OF_EDGES_PAD = 1 << 20


class Ctx:

    def __init__(self):
        self.used = []

    def semaphore(self, nc, ctx, name):
        handle = ctx.enter_context(nc.semaphore(name))
        self.used.append(handle)
        return handle

    def clear_semaphores(self, nc):
        used, self.used = self.used, []
        with nc.Block() as block:
            @block.sync
            def _(sp):
                for handle in used:
                    sp.sem_clear(handle)


def row(ap, parts=P):
    return ap.unsqueeze(0).broadcast_to([parts, ap.shape[0]])


def load_columns(eng, out, vector):
    return eng.dma_start(out, vector.rearrange("(c p) -> p c", p=P), allow_slow_non_contiguous=True)


def newton_rsqrt(dve, out, x, tmp):
    dve.tensor_scalar(out.bitcast(I32), x.bitcast(I32), -0.5, 1597463007.0, ALU.mult, ALU.add)
    dve.drain()
    for _ in range(3):
        if x.shape[-1] == 1:
            dve.scalar_tensor_tensor(tmp, out, x, out, ALU.mult, ALU.mult)
        else:
            dve.tensor_tensor(tmp, out, x, ALU.mult)
            dve.drain()
            dve.tensor_tensor(tmp, tmp, out, ALU.mult)
        dve.drain()
        dve.tensor_scalar(tmp, tmp, -0.5, 1.5, ALU.mult, ALU.add)
        dve.drain()
        dve.tensor_tensor(out, out, tmp, ALU.mult)
        dve.drain()


def normalise(dve, out, x, stats, mv, rs, tmp, wait_for_out=None):
    dve.bn_stats(stats, x)
    dve.drain()
    dve.bn_aggr(mv, stats)
    dve.drain()
    dve.tensor_scalar(mv[:, 1:2], mv[:, 1:2], EPS, None, ALU.add)
    dve.drain()
    newton_rsqrt(dve, rs, mv[:, 1:2], tmp)
    if wait_for_out:
        wait_for_out()
    dve.tensor_scalar(out, x, mv[:, 0:1], rs, ALU.subtract, ALU.mult)


def uses_before(t, b):
    return t * 8 - 8 * b


def over_pairs(eng, step):
    step(0, 0)
    step(1, 1)
    with eng.Fori(0, PAIRS - 1) as i:
        step(i * 2 + 2, 0)
        step(i * 2 + 3, 1)
    step(T - 1, 0)


def over_tiles(eng, step):
    step(0, 0)
    step(1, 1)
    step(2, 0)
    with eng.Fori(0, (T - 5) // 2) as i:
        step(i * 2 + 3, 1)
        step(i * 2 + 4, 0)
    step(T - 2, 1)
    step(T - 1, 0)


def at_most(t, n):
    return isinstance(t, int) and t <= n


def at_least(t, n):
    return isinstance(t, int) and t >= n


def build_edge_tables(nc, g):
    with ExitStack() as ctx:
        sb = lambda n, s, d=F32: ctx.enter_context(nc.sbuf_tensor(n, s, d))
        sem = lambda n: g.semaphore(nc, ctx, n)
        dst_i = sb("et_dst_i", [P, EC], I32)
        dst_next, dst_nf = sb("et_dst_next", [P, EC], I32), sb("et_dst_nf", [P, EC])
        sizes, general = sb("et_sizes", [P, T]), sb("et_general", [P, 2])
        dst_f = sb("et_dst_f", [P, EC])
        below = sb("et_below", [P, EC])
        thresholds = sb("et_thr", [P, T])
        counts = sb("et_counts", [P, T + 1])
        ones = sb("et_ones", [P, P])
        rows_i2 = sb("et_rows_i", [STEPS * GROUP, 2, 2, P], I32)
        rows_f2 = sb("et_rows_f", [STEPS * GROUP, 2, 5, P])
        tile_base = sb("et_base", [P, T])
        cols = sb("et_cols", [P, 2, STEPS * GROUP])
        ends = ctx.enter_context(nc.psum_tensor("et_ends", [P, T + 1], F32))
        turned = ctx.enter_context(nc.psum_tensor("et_turned", [P, 5, P], F32))
        loaded, made, counted, summed = sem("et_loaded"), sem("et_made"), sem("et_counted"), sem("et_summed")
        starts_ready, rows_in, rows_ready, turned_ready, taken = sem("et_starts"), [sem("et_rows_in0"), sem("et_rows_in1")], sem("et_rows_ready"), sem("et_turned_s"), sem("et_taken")
        copied, x_in = sem("et_copied"), sem("et_x_in")
        stats, mv = sb("et_stats", [P, GROUP, 6]), sb("et_mv", [P, GROUP, 2])
        variance, tmp = sb("et_variance", [P, T]), sb("et_tmp", [P, T])
        GW = STEPS * GROUP
        block = ctx.enter_context(nc.Block())

        def groups(eng, step):
            step(0, 0)
            with eng.Fori(0, (T // GROUP - 1) // 2) as i:
                step(i * 2 + 1, 1)
                step(i * 2 + 2, 0)

        @block.sync
        def _(sp):
            sp.dma_start(dst_i[:, :], g.dst[0:P * EC].rearrange("(p c) -> p c", p=P)).then_inc(loaded, 16)
            sp.dma_start(dst_next[:, :], g.dst[1:P * EC + 1].rearrange("(p c) -> p c", p=P)).then_inc(loaded, 16)
            sp.dma_start(g.xn[:, :, :], g.x.rearrange("(t p) n -> p t n", p=P)).then_inc(x_in, 16)
            sp.dma_start(g.x_plus, g.x).then_inc(copied, 16)
            sp.wait_ge(starts_ready, 1)

            def step(m, b):
                rows_i, rows_f = rows_i2[:, b, :, :], rows_f2[:, b, :, :]
                sp.wait_ge(taken, m + 1)
                for k in range(GROUP):
                    e = sp.value_load(g.starts[0:1, bass.ds(m * GROUP + k, 1)], min_val=0, max_val=EDGES)
                    part = slice(k * STEPS, (k + 1) * STEPS)
                    sp.dma_start(rows_i[part, 0, :], g.src[bass.ds(e, CAP)].rearrange("(j p) -> j p", p=P)).then_inc(rows_in[b], 16)
                    sp.dma_start(rows_i[part, 1, :], g.dst[bass.ds(e, CAP)].rearrange("(j p) -> j p", p=P)).then_inc(rows_in[b], 16)
                    sp.dma_start(rows_f[part, 2, :], g.ew[bass.ds(e, CAP)].rearrange("(j p) -> j p", p=P)).then_inc(rows_in[b], 16)
            groups(sp, step)
            sp.wait_ge(copied, 16)

        @block.gpsimd
        def _(pool):
            pool.memset(ones[:, :], 1.0)
            pool.iota(thresholds[:, :], [[P, T]], base=P, channel_multiplier=0, allow_small_or_imprecise_dtypes=True)
            pool.iota(tile_base[:, :], [[P, T]], base=0, channel_multiplier=0, allow_small_or_imprecise_dtypes=True)
            pool.iota(g.node[:, :], [[1, P]], base=0, channel_multiplier=0, allow_small_or_imprecise_dtypes=True)
            pool.memset(g.ident[:, :], 1.0)
            pool.drain()
            pool.affine_select(out=g.ident[:, :], in_=g.ident[:, :], compare_op=ALU.is_equal, fill=0.0,
                               base=0, pattern=[[-1, P]], channel_multiplier=1)
            pool.drain()
            pool.memset(g.marker[:, :], 0.0).then_inc(made, 1)

        @block.vector
        def _(dve):
            dve.sem_inc(taken, 2)
            dve.wait_ge(loaded, 32)
            dve.tensor_copy(dst_f[:, :], dst_i[:, :])
            dve.tensor_copy(dst_nf[:, :], dst_next[:, :])
            dve.wait_ge(made, 1)
            dve.drain()
            with dve.Fori(0, T // GROUP) as m:
                for k in range(GROUP):
                    t = bass.ds(m * GROUP + k, 1)
                    dve.tensor_scalar(below[:, :], dst_f[:, :], thresholds[:, t], 0.0, ALU.is_lt, ALU.add, accum_out=counts[:, t])
                    dve.drain()
            dve.tensor_tensor(below[:, :], dst_f[:, :], dst_nf[:, :], ALU.is_gt)
            dve.drain()
            dve.reduce_sum(counts[:, T:T + 1], below[:, :], axis=AX.X)
            dve.drain()
            dve.memset(g.starts[:, 0:1], 0).then_inc(counted, 1)
            dve.wait_ge(summed, 1)
            dve.tensor_copy(g.starts[:, 1:T + 1], ends[:, 0:T]).then_inc(starts_ready, 1)
            dve.tensor_copy(sizes[:, :], ends[:, 0:T])
            dve.drain()
            dve.tensor_tensor(below[:, 1:T], sizes[:, 1:T], sizes[:, 0:T - 1], ALU.subtract)
            dve.tensor_copy(below[:, 0:1], sizes[:, 0:1])
            dve.drain()
            dve.tensor_reduce(general[:, 0:1], below[:, 0:T], AX.X, ALU.max)
            dve.tensor_scalar(general[:, 1:2], ends[:, T:T + 1], 0.5, None, ALU.is_gt)
            dve.drain()
            dve.tensor_scalar(general[:, 0:1], general[:, 0:1], CAP + 0.5, None, ALU.is_gt)
            dve.drain()
            dve.tensor_tensor(general[:, 0:1], general[:, 0:1], general[:, 1:2], ALU.max)
            dve.drain()
            dve.tensor_copy(g.general[:, :], general[:, 0:1])
            dve.tensor_scalar(general[:, 0:1], general[:, 0:1], float(1 << 22), None, ALU.mult)
            dve.drain()
            dve.tensor_scalar(tile_base[:, :], tile_base[:, :], general[:, 0:1], None, ALU.add)
            dve.drain()
            dve.wait_ge(x_in, 16)

            def step(m, b):
                rows_i, rows_f = rows_i2[:, b, :, :], rows_f2[:, b, :, :]
                for k in range(GROUP):
                    dve.bn_stats(stats[:, k, :], g.xn[:, bass.ds(m * GROUP + k, 1), :].rearrange("p a n -> p (a n)"))
                dve.drain()
                for k in range(GROUP):
                    dve.bn_aggr(mv[:, k, :], stats[:, k, :])
                dve.drain()
                dve.tensor_copy(g.x_mean[:, bass.ds(m * GROUP, GROUP)], mv[:, :, 0])
                dve.tensor_scalar(variance[:, bass.ds(m * GROUP, GROUP)], mv[:, :, 1], EPS, None, ALU.add)
                dve.wait_ge(rows_in[b], m * (24 * GROUP) + (48 - 24 * b) * GROUP)
                dve.tensor_copy(rows_f[:, 0:2, :], rows_i[:, :, :])
                dve.drain()
                dve.memset(rows_f[:, 3:4, P - 1:P], 1.0)
                dve.memset(rows_f[:, 4:5, 0:1], -BIG)
                dve.tensor_tensor(rows_f[:, 3, 0:P - 1], rows_f[:, 1, 0:P - 1], rows_f[:, 1, 1:P], ALU.not_equal)
                dve.drain()
                dve.tensor_scalar(rows_f[:, 4, 1:P], rows_f[:, 3, 0:P - 1], -BIG, None, ALU.mult).then_inc(rows_ready, 1)
                dve.wait_ge(turned_ready, m + 1)
                at = bass.ds(m * GW, GW)
                dve.tensor_copy(cols[:, :, :], turned[:, 0:2, 0:GW])
                dve.tensor_copy(g.e_weight[:, at], turned[:, 2, 0:GW])
                dve.tensor_copy(g.e_last[:, at], turned[:, 3, 0:GW])
                dve.tensor_copy(g.e_first[:, at], turned[:, 4, 0:GW])
                dve.drain()
                dve.tensor_copy(g.e_src[:, at], cols[:, 0, :])
                dve.tensor_tensor(g.e_dst[:, at].rearrange("p (k j) -> p k j", k=GROUP), cols[:, 1, :].rearrange("p (k j) -> p k j", k=GROUP),
                                  tile_base[:, bass.ds(m * GROUP, GROUP)].unsqueeze(2).broadcast_to([P, GROUP, STEPS]), ALU.subtract)
                dve.drain()
                dve.memset(g.marker[:, 0:1], 0.0).then_inc(taken, 1)
                dve.drain()
            groups(dve, step)
            newton_rsqrt(dve, g.x_rstd[:, :], variance[:, :], tmp[:, :])

        @block.tensor
        def _(pe):
            pe.wait_ge(counted, 1)
            pe.wait_ge(made, 1)
            pe.matmul(ends[:, :], ones[:, :], counts[:, :], start=True, stop=True).then_inc(summed, 1)

            def step(m, b):
                rows_f = rows_f2[:, b, :, :]
                pe.wait_ge(rows_ready, m + 1)
                pe.wait_ge(taken, m + 2)
                for k in range(5):
                    last = pe.transpose(turned[:, k, 0:GW], rows_f[:, k, :], g.ident[0:GW, 0:GW])
                last.then_inc(turned_ready, 1)
            groups(pe, step)


def layer0_projections(nc, g):
    with ExitStack() as ctx:
        sb = lambda n, s, d=F32: ctx.enter_context(nc.sbuf_tensor(n, s, d))
        sem = lambda n: g.semaphore(nc, ctx, n)
        bank = lambda n: ctx.enter_context(nc.psum_tensor(n, [P, 512], F32))
        w_kvs = sb("a_w_kvs", [P, 2, 3 * D])
        w_q = sb("a_w_q", [P, 2, D])
        b_k, b_v, b_q = sb("a_bk", [P, D]), sb("a_bv", [P, D]), sb("a_bq", [P, 2])
        valid = sb("a_valid", [P, 1])
        xn = sb("a_xn", [P, 2, D])
        xt = sb("a_xt", [P, 2, 2, P])
        k_lin, k_exp, k_phi = sb("a_klin", [P, 2, D]), sb("a_kexp", [P, 2, D]), sb("a_kphi", [P, 2, D])
        v_one = sb("a_vone", [P, 2, 2, P + 1])
        sup = sb("a_sup", [P, 2, D])
        q_exp, q_pos = sb("a_qexp", [P, 2, D]), sb("a_qpos", [P, 2, D])
        kv_sum = sb("a_kvsum", [P, 2, P + 1])
        turned, sum_ps = bank("a_turned"), bank("a_sumps")
        kv_ps, q_ps, sup_ps = ([bank("a_" + n + str(b)) for b in range(2)] for n in ("kvps", "qps", "supps"))
        sup_stored = [sem("a_ss0"), sem("a_ss1")]
        names = ("weights valid_made xn_ready xn_kept x_turned xt_ready kv_done q_done sup_done kv_used lin_ready k_exp_ready "
                 "q_ready sup_ready phi_ready sums_ready summed_up").split()
        s = {n: sem("a_" + n) for n in names}
        block = ctx.enter_context(nc.Block())

        def turns(eng, step):
            step(0, 0)
            step(1, 1)
            step(2, 0)
            with eng.Fori(0, (T - 5) // 2) as i:
                step(i * 2 + 3, 1)
                step(i * 2 + 4, 0)
            step(T - 2, 1)
            step(T - 1, 0)

        def first(t):
            return isinstance(t, int) and t == 0

        def among_last(t, n):
            return isinstance(t, int) and t >= T - n

        @block.sync
        def _(sp):
            sp.dma_start(w_q[:, :, :], g.w["L0_mix_Wq"].rearrange("(c p) n -> p c n", p=P)).then_inc(s["weights"], 16)
            for k, w in enumerate(("L0_mix_Wk", "L0_mix_Wv", "L0_gnn_weight")):
                sp.dma_start(w_kvs[:, :, k * D:(k + 1) * D], g.w[w].rearrange("(c p) n -> p c n", p=P)).then_inc(s["weights"], 16)
            sp.dma_start(b_k[:, :], row(g.w["L0_mix_bk"])).then_inc(s["weights"], 16)
            sp.dma_start(b_v[:, :], row(g.w["L0_mix_bv"])).then_inc(s["weights"], 16)
            load_columns(sp, b_q[:, :], g.w["L0_mix_bq"]).then_inc(s["weights"], 16)

            def step(t, b):
                sp.wait_ge(s["sup_ready"], t + 3)
                sp.dma_start(g.sup_table[bass.ds(t * P, P), :], sup[:, b, :]).then_inc(sup_stored[b], 16)
            over_pairs(sp, step)
            sp.wait_ge(sup_stored[0], 16 * ((T + 1) // 2))
            sp.wait_ge(sup_stored[1], 16 * (T // 2))

        @block.gpsimd
        def _(pool):
            pool.memset(v_one[:, :, :, P:P + 1], 1.0)
            pool.memset(valid[:, :], 1.0)
            pool.drain()
            pool.affine_select(out=valid[:, :], in_=valid[:, :], compare_op=ALU.is_gt, fill=0.0,
                               base=N - (T - 1) * P, pattern=[[-1, 1]], channel_multiplier=-1).then_inc(s["valid_made"], 1)

            def keep(t, b):
                pool.wait_ge(s["xn_ready"], t + 1)
                pool.tensor_copy(g.xn[:, bass.ds(t, 1), :].rearrange("p a n -> p (a n)"), xn[:, b, :]).then_inc(s["xn_kept"], 1)
            over_pairs(pool, keep)

        @block.scalar
        def _(act):
            def copy_turned(t, b):
                act.wait_ge(s["x_turned"], t + 3)
                act.copy(xt[:, b, :, :], turned[:, 0:D].rearrange("p (c n) -> p c n", c=2)).then_inc(s["xt_ready"], 1)

            def step(t, b):
                if not among_last(t, 1):
                    act.wait_ge(s["sup_done"], t)
                    copy_turned(t + 1, 1 - b)
                act.wait_ge(s["lin_ready"], t + 1)
                act.activation(k_exp[:, b, :], k_lin[:, b, :], ACT.Exp).then_inc(s["k_exp_ready"], 1)
                act.wait_ge(s["phi_ready"], t + 1)
                act.wait_ge(s["q_done"], t + 1)
                for h in range(2):
                    act.activation(q_exp[:, b, h * P:(h + 1) * P], q_ps[b][:, h * P:(h + 1) * P], ACT.Exp, bias=b_q[:, h:h + 1])
                for h in range(2):
                    last = act.activation(q_pos[:, b, h * P:(h + 1) * P], q_ps[b][:, h * P:(h + 1) * P], ACT.Relu, bias=b_q[:, h:h + 1])
                last.then_inc(s["q_ready"], 1)
                act.wait_ge(s["sup_done"], t + 1)
                act.wait_ge(sup_stored[b], uses_before(t, b))
                act.copy(sup[:, b, :], sup_ps[b][:, 0:D]).then_inc(s["sup_ready"], 1)
            act.wait_ge(s["weights"], 16 * 7)
            act.sem_inc(s["sup_ready"], 2)
            act.sem_inc(s["q_ready"], 2)
            copy_turned(0, 0)
            turns(act, step)

        @block.vector
        def _(dve):
            def norm(t, b):
                at = bass.ds(t, 1)
                dve.wait_ge(s["xn_kept"], t + 1)
                dve.wait_ge(s["x_turned"], t + 1)
                dve.tensor_scalar(xn[:, b, :], g.xn[:, at, :].rearrange("p a n -> p (a n)"), g.x_mean[:, at], g.x_rstd[:, at],
                                  ALU.subtract, ALU.mult).then_inc(s["xn_ready"], 1)

            def add_sums(t):
                dve.wait_ge(s["sums_ready"], t + 1)
                dve.tensor_tensor(kv_sum[:, :, :], kv_sum[:, :, :], sum_ps[:, 0:2 * P + 2].rearrange("p (a n) -> p a n", a=2), ALU.add).then_inc(s["summed_up"], 1)

            def step(t, b):
                if not among_last(t, 2):
                    norm(t + 2, b)
                dve.wait_ge(s["kv_done"], t + 1)
                dve.tensor_tensor(k_lin[:, b, :], kv_ps[b][:, 0:D], b_k[:, :], ALU.add).then_inc(s["lin_ready"], 1)
                dve.tensor_tensor(v_one[:, b, :, 0:P], kv_ps[b][:, D:2 * D].rearrange("p (a n) -> p a n", a=2), b_v[:, :].rearrange("p (a n) -> p a n", a=2), ALU.add).then_inc(s["kv_used"], 1)
                if not first(t):
                    add_sums(t - 1)
                dve.wait_ge(s["k_exp_ready"], t + 1)
                dve.tensor_scalar(k_exp[:, b, :], k_exp[:, b, :], 1.0, None, ALU.min)
                dve.drain()
                dve.scalar_tensor_tensor(k_phi[:, b, :], k_lin[:, b, :], 0.0, k_exp[:, b, :], ALU.max, ALU.add)
                if among_last(t, 1):
                    dve.drain()
                    dve.tensor_scalar(k_phi[:, b, :], k_phi[:, b, :], valid[:, :], None, ALU.mult)
                dve.wait_ge(s["q_ready"], t + 3)
                dve.scalar_tensor_tensor(g.q_phi[:, :, bass.ds(t * P, P)], q_exp[:, b, :].rearrange("p (a n) -> p a n", a=2), 1.0,
                                         q_pos[:, b, :].rearrange("p (a n) -> p a n", a=2), ALU.min, ALU.add).then_inc(s["phi_ready"], 1)
            dve.memset(kv_sum[:, :, :], 0.0)
            dve.memset(g.kv[:, :, :], 0.0)
            dve.memset(g.ksum[:, :, :], 0.0)
            dve.drain()
            dve.sem_inc(s["kv_used"], 2)
            dve.sem_inc(s["phi_ready"], 2)
            dve.sem_inc(s["xn_kept"], 2)
            dve.sem_inc(s["x_turned"], 2)
            dve.sem_inc(s["summed_up"], 1)
            dve.wait_ge(s["valid_made"], 1)
            norm(0, 0)
            norm(1, 1)
            dve.wait_ge(s["weights"], 16 * 7)
            turns(dve, step)
            add_sums(T - 1)
            dve.drain()
            for h in range(2):
                for r in range(4):
                    part = slice(32 * r, 32 * r + 32)
                    dve.tensor_copy(g.kv[part, h, part], kv_sum[part, h, part])
                    dve.tensor_copy(g.ksum[part, h, part], kv_sum[part, h, P:P + 1].broadcast_to([32, 32]))

        @block.tensor
        def _(pe):
            def turn(t, b):
                pe.wait_ge(s["xn_ready"], t + 1)
                pe.wait_ge(s["xt_ready"], t)
                for h in range(2):
                    last = pe.transpose(turned[:, h * P:(h + 1) * P], xn[:, b, h * P:(h + 1) * P], g.ident[:, :])
                last.then_inc(s["x_turned"], 1)

            def sums(t, b):
                pe.wait_ge(s["phi_ready"], t + 3)
                pe.wait_ge(s["summed_up"], t + 1)
                for h in range(2):
                    last = pe.matmul(sum_ps[:, h * (P + 1):(h + 1) * (P + 1)], k_phi[:, b, h * P:(h + 1) * P], v_one[:, b, h, :], start=True, stop=True)
                last.then_inc(s["sums_ready"], 1)

            def step(t, b):
                pe.wait_ge(s["xt_ready"], t + 1)
                pe.wait_ge(s["kv_used"], t + 1)
                for h in range(2):
                    last = pe.matmul(kv_ps[b][:, :], xt[:, b, h, :], w_kvs[:, h, 0:2 * D], start=h == 0, stop=h == 1)
                last.then_inc(s["kv_done"], 1)
                if not among_last(t, 1):
                    turn(t + 1, 1 - b)
                pe.wait_ge(s["q_ready"], t + 1)
                for o in range(2):
                    for h in range(2):
                        last = pe.matmul(q_ps[b][:, o * P:(o + 1) * P], w_q[:, h, o * P:(o + 1) * P], xt[:, b, h, :], start=h == 0, stop=h == 1)
                last.then_inc(s["q_done"], 1)
                pe.wait_ge(s["sup_ready"], t + 1)
                for h in range(2):
                    last = pe.matmul(sup_ps[b][:, 0:D], xt[:, b, h, :], w_kvs[:, h, 2 * D:3 * D], start=h == 0, stop=h == 1)
                last.then_inc(s["sup_done"], 1)
                if not first(t):
                    sums(t - 1, 1 - b)
            pe.wait_ge(s["weights"], 16 * 7)
            turn(0, 0)
            turns(pe, step)
            sums(T - 1, 0)


def layer0_edges_of_any_order(nc, g):
    with ExitStack() as ctx:
        sb = lambda n, s, d=F32: ctx.enter_context(nc.sbuf_tensor(n, s, d))
        sem = lambda n: g.semaphore(nc, ctx, n)
        sums = sb("ga_sums", [P, T, D])
        source, target, edge_w = sb("ga_source", [P, 1], I32), sb("ga_target", [P, 1], I32), sb("ga_w", [P, 1])
        target_f, relative, tile_base = sb("ga_targetf", [P, 1]), sb("ga_relative", [P, T]), sb("ga_base", [P, T])
        messages, spread = sb("ga_messages", [P, D]), sb("ga_spread", [P, P])
        product = ctx.enter_context(nc.psum_tensor("ga_product", [P, 512], F32))
        x_in, edges_in, gather_begun, messages_in, base_made = sem("ga_x_in"), sem("ga_edges_in"), sem("ga_begun"), g.messages_in[4], sem("ga_base_made")
        step_begun = sem("ga_step_begun")
        spread_ready, product_done, edges_used, stored = sem("ga_spread_ready"), sem("ga_product_done"), sem("ga_edges_used"), sem("ga_stored")
        block = ctx.enter_context(nc.Block())

        @block.sync
        def _(sp):
            general = sp.value_load(g.general[0:1, 0:1], min_val=0, max_val=1)
            with sp.If(general > 0):
                sp.dma_start(sums[:, :, :], g.x.rearrange("(t p) n -> p t n", p=P)).then_inc(x_in, 16)
                with sp.Fori(0, EC) as c:
                    sp.wait_ge(edges_used, c + 1)
                    sp.dma_start(source[:, :], g.src[bass.ds(c * P, P)].unsqueeze(1)).then_inc(edges_in, 16)
                    sp.dma_start(target[:, :], g.dst[bass.ds(c * P, P)].unsqueeze(1)).then_inc(edges_in, 16)
                    sp.dma_start(edge_w[:, :], g.ew[bass.ds(c * P, P)].unsqueeze(1)).then_inc(edges_in, 16)
                sp.wait_ge(edges_used, EC + 1)
                sp.dma_start(g.x_plus.rearrange("(t p) n -> p t n", p=P), sums[:, :, :]).then_inc(stored, 16)
                sp.wait_ge(stored, 16)

        @block.gpsimd
        def _(pool):
            pool.iota(tile_base[:, :], [[P, T]], base=0, channel_multiplier=0, allow_small_or_imprecise_dtypes=True).then_inc(base_made, 1)
            general = pool.value_load(g.general[0:1, 0:1], min_val=0, max_val=1)
            with pool.If(general > 0):
                with pool.Fori(0, EC) as c:
                    pool.wait_ge(edges_in, (c + 1) * 48)
                    pool.sem_inc(gather_begun, 1)
                    pool.indirect_dma_start(messages[:, :], None, g.sup_table[:, :],
                                            bass.IndirectOffsetOnAxis(ap=source[:, 0:1], axis=0)).then_inc(messages_in, 16)

        @block.vector
        def _(dve):
            general = dve.value_load(g.general[0:1, 0:1], min_val=0, max_val=1)
            with dve.If(general > 0):
                dve.sem_inc(edges_used, 1)
                dve.wait_ge(base_made, 1)
                dve.wait_ge(x_in, 16)
                with dve.Fori(0, EC) as c:
                    dve.wait_ge(edges_in, (c + 1) * 48)
                    dve.tensor_copy(target_f[:, :], target[:, :])
                    dve.drain()
                    dve.tensor_scalar(relative[:, :], tile_base[:, :], target_f[:, :], -1.0, ALU.subtract, ALU.mult)
                    dve.drain()
                    with dve.Fori(0, T) as t:
                        at = bass.ds(t, 1)
                        dve.tensor_scalar(spread[:, :], g.node[:, :], relative[:, at], edge_w[:, :], ALU.is_equal, ALU.mult).then_inc(spread_ready, 1)
                        dve.wait_ge(product_done, c * T + t + 1)
                        mine = sums[:, at, :].rearrange("p a n -> p (a n)")
                        dve.tensor_tensor(mine, mine, product[:, 0:D], ALU.add)
                        dve.drain()
                    dve.sem_inc(edges_used, 1)

        @block.tensor
        def _(pe):
            general = pe.value_load(g.general[0:1, 0:1], min_val=0, max_val=1)
            with pe.If(general > 0):
                with pe.Fori(0, EC) as c:
                    pe.wait_ge(messages_in, (c + 1) * 16)
                    pe.sem_inc(step_begun, 1)
                    with pe.Fori(0, T) as t:
                        pe.wait_ge(spread_ready, c * T + t + 1)
                        pe.matmul(product[:, 0:D], spread[:, :], messages[:, :], start=True, stop=True).then_inc(product_done, 1)


def layer1_edges_of_any_order(nc, g):
    with ExitStack() as ctx:
        sb = lambda n, s, d=F32: ctx.enter_context(nc.sbuf_tensor(n, s, d))
        sem = lambda n: g.semaphore(nc, ctx, n)
        rows = sb("gb_rows", [P, T, TBL])
        source, target, target_f = sb("gb_source", [P, 1], I32), sb("gb_target", [P, P], I32), sb("gb_targetf", [P, P])
        messages, ones, node_id = sb("gb_messages", [P, TBL]), sb("gb_ones", [P, P]), sb("gb_nodeid", [P, T])
        diagonal, scores = sb("gb_diagonal", [P, 4, P]), sb("gb_scores", [P, 4, P])
        penalty, alpha, turned = sb("gb_penalty", [P, P]), sb("gb_alpha", [P, 4, P]), sb("gb_turned", [P, 4, P])
        top, decay, part = sb("gb_top", [P, 4]), sb("gb_decay", [P, 4]), sb("gb_part", [P, 4])
        scores_ps, turned_ps, product = (ctx.enter_context(nc.psum_tensor("gb_ps" + n, [P, 512], F32)) for n in "abc")
        names = ("constants rows_in edges_in begun diagonal_ready scores_done alpha_ready exp_ready turned_done turned_ready "
                 "product_done edges_used stored").split()
        s = {n: sem("gb_" + n) for n in names}
        s["messages_in"] = g.messages_in[5]
        block = ctx.enter_context(nc.Block())

        @block.sync
        def _(sp):
            general = sp.value_load(g.general[0:1, 0:1], min_val=0, max_val=1)
            with sp.If(general > 0):
                sp.dma_start(rows[:, :, :], g.att_table.rearrange("(t p) n -> p t n", p=P)).then_inc(s["rows_in"], 16)
                with sp.Fori(0, EC) as c:
                    sp.wait_ge(s["edges_used"], c + 1)
                    sp.dma_start(source[:, :], g.src[bass.ds(c * P, P)].unsqueeze(1)).then_inc(s["edges_in"], 16)
                    sp.dma_start(target[:, :], row(g.dst[bass.ds(c * P, P)])).then_inc(s["edges_in"], 16)
                sp.wait_ge(s["edges_used"], EC + 1)
                sp.dma_start(g.att_table.rearrange("(t p) n -> p t n", p=P), rows[:, :, :]).then_inc(s["stored"], 16)
                sp.wait_ge(s["stored"], 16)

        @block.gpsimd
        def _(pool):
            pool.iota(node_id[:, :], [[P, T]], base=0, channel_multiplier=1, allow_small_or_imprecise_dtypes=True)
            pool.memset(ones[:, :], 1.0)
            pool.drain()
            pool.sem_inc(s["constants"], 1)
            general = pool.value_load(g.general[0:1, 0:1], min_val=0, max_val=1)
            with pool.If(general > 0):
                with pool.Fori(0, EC) as c:
                    pool.wait_ge(s["edges_in"], (c + 1) * 32)
                    pool.sem_inc(s["begun"], 1)
                    pool.indirect_dma_start(messages[:, :], None, g.att_table[:, :],
                                            bass.IndirectOffsetOnAxis(ap=source[:, 0:1], axis=0)).then_inc(s["messages_in"], 16)

        @block.scalar
        def _(act):
            general = act.value_load(g.general[0:1, 0:1], min_val=0, max_val=1)
            with act.If(general > 0):
                with act.Fori(0, EC) as c:
                    with act.Fori(0, T) as t:
                        act.wait_ge(s["alpha_ready"], c * T + t + 1)
                        act.activation(alpha[:, :, :], alpha[:, :, :], ACT.Exp)
                        act.activation(decay[:, :], decay[:, :], ACT.Exp).then_inc(s["exp_ready"], 1)
                        act.wait_ge(s["turned_done"], c * T + t + 1)
                        act.copy(turned[:, :, :], turned_ps[:, :].rearrange("p (h n) -> p h n", h=4)).then_inc(s["turned_ready"], 1)

        @block.vector
        def _(dve):
            general = dve.value_load(g.general[0:1, 0:1], min_val=0, max_val=1)
            with dve.If(general > 0):
                dve.sem_inc(s["edges_used"], 1)
                dve.wait_ge(s["constants"], 1)
                dve.wait_ge(s["rows_in"], 16)
                with dve.Fori(0, EC) as c:
                    dve.wait_ge(s["edges_in"], (c + 1) * 32)
                    dve.tensor_copy(target_f[:, :], target[:, :])
                    dve.wait_ge(s["messages_in"], (c + 1) * 16)
                    for h in range(4):
                        last = dve.tensor_scalar(diagonal[:, h, :], g.ident[:, :], messages[:, D + h:D + h + 1], None, ALU.mult)
                    last.then_inc(s["diagonal_ready"], 1)
                    dve.wait_ge(s["scores_done"], c + 1)
                    dve.tensor_copy(scores[:, :, :], scores_ps[:, :].rearrange("p (h n) -> p h n", h=4))
                    dve.drain()
                    with dve.Fori(0, T) as t:
                        at = bass.ds(t, 1)
                        mine = rows[:, at, 0:D].rearrange("p a (h n) -> p (a h) n", h=4)
                        highest = rows[:, at, D + 4:D + 8].rearrange("p a n -> p (a n)")
                        weight = rows[:, at, D + 8:D + 12].rearrange("p a n -> p (a n)")
                        dve.tensor_scalar(penalty[:, :], target_f[:, :], node_id[:, at], BIG, ALU.is_equal, ALU.mult)
                        for h in range(4):
                            dve.tensor_scalar(alpha[:, h, :], scores[:, h, :], g.a_dst[:, at, h:h + 1].rearrange("p a n -> p (a n)"), None, ALU.add)
                        dve.drain()
                        dve.tensor_scalar(penalty[:, :], penalty[:, :], -BIG, None, ALU.add)
                        dve.scalar_tensor_tensor(alpha[:, :, :], alpha[:, :, :], 0.2, alpha[:, :, :], ALU.mult, ALU.max)
                        dve.drain()
                        dve.tensor_tensor(alpha[:, :, :], alpha[:, :, :], penalty[:, :].unsqueeze(1).broadcast_to([P, 4, P]), ALU.add)
                        dve.drain()
                        dve.tensor_reduce(top[:, :], alpha[:, :, :], AX.X, ALU.max)
                        dve.drain()
                        dve.tensor_tensor(top[:, :], top[:, :], highest, ALU.max)
                        dve.drain()
                        dve.tensor_tensor(decay[:, :], highest, top[:, :], ALU.subtract)
                        dve.tensor_tensor(alpha[:, :, :], alpha[:, :, :], top[:, :].unsqueeze(2).broadcast_to([P, 4, P]), ALU.subtract)
                        dve.drain()
                        dve.sem_inc(s["alpha_ready"], 1)
                        dve.tensor_copy(highest, top[:, :])
                        dve.wait_ge(s["exp_ready"], c * T + t + 1)
                        dve.reduce_sum(part[:, :], alpha[:, :, :], axis=AX.X)
                        dve.tensor_tensor(weight, weight, decay[:, :], ALU.mult)
                        dve.tensor_tensor(mine, mine, decay[:, :].unsqueeze(2).broadcast_to([P, 4, 64]), ALU.mult)
                        dve.drain()
                        dve.tensor_tensor(weight, weight, part[:, :], ALU.add)
                        dve.wait_ge(s["product_done"], c * T + t + 1)
                        dve.tensor_tensor(mine, mine, product[:, 0:D].rearrange("p (h n) -> p h n", h=4), ALU.add)
                        dve.drain()
                    dve.sem_inc(s["edges_used"], 1)

        @block.tensor
        def _(pe):
            general = pe.value_load(g.general[0:1, 0:1], min_val=0, max_val=1)
            with pe.If(general > 0):
                pe.wait_ge(s["constants"], 1)
                with pe.Fori(0, EC) as c:
                    pe.wait_ge(s["diagonal_ready"], c + 1)
                    pe.matmul(scores_ps[:, :], ones[:, :], diagonal[:, :, :].rearrange("p h n -> p (h n)"), start=True, stop=True).then_inc(s["scores_done"], 1)
                    with pe.Fori(0, T) as t:
                        pe.wait_ge(s["exp_ready"], c * T + t + 1)
                        for h in range(4):
                            last = pe.transpose(turned_ps[:, h * P:(h + 1) * P], alpha[:, h, :], g.ident[:, :])
                        last.then_inc(s["turned_done"], 1)
                        pe.wait_ge(s["turned_ready"], c * T + t + 1)
                        for h in range(4):
                            last = pe.matmul(product[:, h * 64:(h + 1) * 64], turned[:, h, :], messages[:, h * 64:(h + 1) * 64], start=True, stop=True)
                        last.then_inc(s["product_done"], 1)


def layer0_graph_and_attention(nc, g):
    with ExitStack() as ctx:
        sb = lambda n, s, d=F32: ctx.enter_context(nc.sbuf_tensor(n, s, d))
        sem = lambda n: g.semaphore(nc, ctx, n)
        bank = lambda n: ctx.enter_context(nc.psum_tensor(n, [P, 512], F32))
        w_o, w_1, w_2 = sb("b_wo", [P, 2, D]), sb("b_w1", [P, 2, FF]), sb("b_w2", [P, FF // P, D])
        b_o, ln1_g, ln1_b, ln2_g, ln2_b, b_2, b_gnn = (sb("b_row" + str(i), [P, D]) for i in range(7))
        b_1 = sb("b_b1", [P, FF // P])
        messages = sb("b_messages", [P, 2, STEPS, D])
        sources = sb("b_sources", [P, 2, STEPS], I32)
        spread = sb("b_spread", [P, 2, HALF, P])
        x_in = sb("b_x", [P, 2, D])
        gathered = sb("b_gathered", [P, 2, D])
        ratio, inverse = sb("b_ratio", [P, 2, P]), sb("b_inverse", [P, 2, P])
        h1 = sb("b_h1", [P, 2, D])
        h1_t = sb("b_h1t", [P, 2, P])
        hidden = sb("b_hidden", [P, FF // P, P])
        work, total = sb("b_work", [P, D]), sb("b_total", [P, D])
        stats = sb("b_stats", [P, 6])
        mv_1, mv_2, rs_1, rs_2 = sb("b_mv1", [P, 2]), sb("b_mv2", [P, 2]), sb("b_rs1", [P, 1]), sb("b_rs2", [P, 1])
        exponent = sb("b_exponent", [P, 1])
        agg_ps, attn_ps, out_ps, turned_ps, down_ps = (bank("b_" + n) for n in ("agg", "attn", "outp", "turn", "down"))
        up_ps = [bank("b_up0"), bank("b_up1")]
        names = ("weights gathers_begun sources_ready spread_ready spread_free messages_free x_free attn_done ratio_ready out_done h1_ready "
                 "turned_done h1t_ready up_done hidden_ready down_done down_used agg_done agg_copied x1_ready moments_1 moments_2 root_1 root_2 roots_begun").split()
        s = {n: sem("b_" + n) for n in names}
        messages_in = g.messages_in[0:2]
        x_loaded = [sem("b_x_loaded0"), sem("b_x_loaded1")]
        block = ctx.enter_context(nc.Block())
        LOADS = 16 * 11

        def turns(eng, step, last):
            step(0, 0, True)
            step(1, 1, False)
            step(2, 0, False)
            with eng.Fori(0, PAIRS - 2) as i:
                step(i * 2 + 3, 1, False)
                step(i * 2 + 4, 0, False)
            step(T - 2, 1, False)
            step(T - 1, 0, False)
            last(T - 1, 0)

        @block.sync
        def _(sp):
            sp.dma_start(w_o[:, :, :], g.w["L0_mix_Wo"].rearrange("(c p) n -> p c n", p=P)).then_inc(s["weights"], 16)
            for out, vector in ((b_o, g.w["L0_mix_bo"]), (ln1_g, g.w["L0_mix_ln1_g"]), (ln1_b, g.w["L0_mix_ln1_b"])):
                sp.dma_start(out[:, :], row(vector)).then_inc(s["weights"], 16)
            sp.dma_start(w_1[:, :, :], g.w["L0_mix_W1"].rearrange("(c p) n -> p c n", p=P)).then_inc(s["weights"], 16)
            sp.dma_start(w_2[:, :, :], g.w["L0_mix_W2"].rearrange("(c p) n -> p c n", p=P)).then_inc(s["weights"], 16)
            load_columns(sp, b_1[:, :], g.w["L0_mix_b1"]).then_inc(s["weights"], 16)
            for out, vector in ((ln2_g, g.w["L0_mix_ln2_g"]), (ln2_b, g.w["L0_mix_ln2_b"]), (b_2, g.w["L0_mix_b2"]), (b_gnn, g.w["L0_gnn_bias"])):
                sp.dma_start(out[:, :], row(vector)).then_inc(s["weights"], 16)

            def step(t, b):
                sp.wait_ge(s["x_free"], t + 1)
                sp.dma_start(x_in[:, b, :], g.x_plus[bass.ds(t * P, P), :]).then_inc(x_loaded[b], 16)
            over_pairs(sp, step)

        @block.gpsimd
        def _(pool):
            def gather(t, b, part):
                if part == 0:
                    pool.wait_ge(s["messages_free"], t + 1)
                    pool.tensor_copy(sources[:, b, :], g.e_src[:, bass.ds(t * STEPS, STEPS)]).then_inc(s["sources_ready"], 1)
                    pool.wait_ge(s["sources_ready"], t + 1)
                    pool.sem_inc(s["gathers_begun"], 1)
                for j in range(part * STEPS // 3, (part + 1) * STEPS // 3):
                    pool.indirect_dma_start(messages[:, b, j, :], None, g.sup_table[:, :],
                                            bass.IndirectOffsetOnAxis(ap=sources[:, b, j:j + 1], axis=0)).then_inc(messages_in[b], 16)

            def root(t, moments, mv, rs, done):
                pool.wait_ge(moments, t + 1)
                pool.sem_inc(s["roots_begun"], 1)
                pool.tensor_tensor(rs[:, :], mv[:, 1:2], exponent[:, :], ALU.pow).then_inc(done, 1)

            def step(t, b, first):
                last = isinstance(t, int) and t == T - 1
                root(t, s["moments_1"], mv_1, rs_1, s["root_1"])
                if not last:
                    gather(t + 1, 1 - b, 1)
                    gather(t + 1, 1 - b, 2)
                if not first:
                    root(t - 1, s["moments_2"], mv_2, rs_2, s["root_2"])
                if not (isinstance(t, int) and t >= T - 2):
                    gather(t + 2, b, 0)

            pool.memset(exponent[:, :], -0.5)
            pool.drain()
            for part in range(3):
                gather(0, 0, part)
            gather(1, 1, 0)
            step(0, 0, True)
            step(1, 1, False)
            step(2, 0, False)
            with pool.Fori(0, PAIRS - 2) as i:
                step(i * 2 + 3, 1, False)
                step(i * 2 + 4, 0, False)
            step(T - 2, 1, False)
            step(T - 1, 0, False)
            root(T - 1, s["moments_2"], mv_2, rs_2, s["root_2"])

        @block.scalar
        def _(act):
            def copy_sums(t, b):
                act.wait_ge(s["agg_done"], t + 1)
                if not (isinstance(t, int) and t < 2):
                    act.wait_ge(s["x1_ready"], t - 1)
                act.copy(gathered[:, b, :], agg_ps[:, 0:D]).then_inc(s["agg_copied"], 1)

            def step(t, b, first):
                copy_sums(t, b)
                act.wait_ge(s["turned_done"], t + 1)
                act.copy(h1_t[:, :, :], turned_ps[:, 0:D].rearrange("p (c n) -> p c n", c=2)).then_inc(s["h1t_ready"], 1)
                for u in range(2):
                    act.wait_ge(s["up_done"], t * 2 + u + 1)
                    for c in range(4):
                        chunk = act.activation(hidden[:, u * 4 + c, :], up_ps[u][:, c * P:(c + 1) * P], ACT.Relu, bias=b_1[:, u * 4 + c:u * 4 + c + 1])
                    chunk.then_inc(s["hidden_ready"], 1)
            act.wait_ge(s["weights"], LOADS)
            turns(act, step, lambda t, b: None)

        @block.vector
        def _(dve):
            def spread_edges(t, half):
                dve.wait_ge(s["spread_free"], t * 2 + half + 1)
                for j in range(HALF):
                    e = bass.ds(t * STEPS + half * HALF + j, 1)
                    last = dve.tensor_scalar(spread[:, half, j, :], g.node[:, :], g.e_dst[:, e], g.e_weight[:, e], ALU.is_equal, ALU.mult)
                last.then_inc(s["spread_ready"], 1)

            def attention(t, b):
                dve.wait_ge(s["attn_done"], t + 1)
                dve.tensor_scalar(inverse[:, :, :], attn_ps[:, D:2 * D].rearrange("p (c n) -> p c n", c=2), 1e-6, None, ALU.add)
                dve.drain()
                dve.reciprocal(inverse[:, :, :], inverse[:, :, :])
                dve.drain()
                dve.tensor_tensor(ratio[:, :, :], attn_ps[:, 0:D].rearrange("p (c n) -> p c n", c=2), inverse[:, :, :], ALU.mult).then_inc(s["ratio_ready"], 1)

            def first_moments(t, b):
                dve.wait_ge(s["out_done"], t + 1)
                dve.tensor_tensor(work[:, :], out_ps[:, 0:D], b_o[:, :], ALU.add)
                dve.drain()
                dve.tensor_tensor(work[:, :], work[:, :], g.xn[:, bass.ds(t, 1), :].rearrange("p a n -> p (a n)"), ALU.add)
                dve.drain()
                dve.bn_stats(stats[:, :], work[:, :])
                dve.drain()
                dve.bn_aggr(mv_1[:, :], stats[:, :])
                dve.drain()
                dve.tensor_scalar(mv_1[:, 1:2], mv_1[:, 1:2], EPS, None, ALU.add).then_inc(s["moments_1"], 1)

            def first_norm(t, b):
                dve.wait_ge(s["root_1"], t + 1)
                dve.tensor_scalar(work[:, :], work[:, :], mv_1[:, 0:1], rs_1[:, :], ALU.subtract, ALU.mult)
                dve.drain()
                dve.tensor_tensor(work[:, :], work[:, :], ln1_g[:, :], ALU.mult)
                dve.drain()
                dve.tensor_tensor(h1[:, b, :], work[:, :], ln1_b[:, :], ALU.add).then_inc(s["h1_ready"], 1)

            def second_moments(t, b):
                dve.wait_ge(s["down_done"], t + 1)
                dve.tensor_tensor(total[:, :], down_ps[:, 0:D], b_2[:, :], ALU.add).then_inc(s["down_used"], 1)
                dve.drain()
                dve.tensor_tensor(total[:, :], total[:, :], h1[:, b, :], ALU.add)
                dve.drain()
                dve.bn_stats(stats[:, :], total[:, :])
                dve.drain()
                dve.bn_aggr(mv_2[:, :], stats[:, :])
                dve.drain()
                dve.tensor_scalar(mv_2[:, 1:2], mv_2[:, 1:2], EPS, None, ALU.add).then_inc(s["moments_2"], 1)

            def second_norm(t, b):
                dve.wait_ge(s["root_2"], t + 1)
                dve.tensor_scalar(total[:, :], total[:, :], mv_2[:, 0:1], rs_2[:, :], ALU.subtract, ALU.mult)
                dve.drain()
                dve.tensor_tensor(total[:, :], total[:, :], ln2_g[:, :], ALU.mult)
                dve.drain()
                dve.tensor_tensor(total[:, :], total[:, :], ln2_b[:, :], ALU.add)
                dve.wait_ge(x_loaded[b], uses_before(t, b) + 16)
                dve.wait_ge(s["agg_copied"], t + 1)
                dve.tensor_tensor(x_in[:, b, :], x_in[:, b, :], b_gnn[:, :], ALU.add)
                dve.drain()
                dve.tensor_tensor(x_in[:, b, :], x_in[:, b, :], gathered[:, b, :], ALU.add)
                dve.drain()
                dve.tensor_tensor(g.xn[:, bass.ds(t, 1), :].rearrange("p a n -> p (a n)"), x_in[:, b, :], total[:, :], ALU.add).then_inc(s["x1_ready"], 1)
                dve.wait_ge(s["x1_ready"], t + 1)
                dve.sem_inc(s["x_free"], 1)

            def step(t, b, first, final=False):
                first_moments(t, b)
                if not final:
                    spread_edges(t + 1, 0)
                first_norm(t, b)
                if not final:
                    spread_edges(t + 1, 1)
                if not first:
                    second_moments(t - 1, 1 - b)
                if not final:
                    attention(t + 1, 1 - b)
                if not first:
                    second_norm(t - 1, 1 - b)

            for free in ("spread_free", "messages_free", "x_free"):
                dve.sem_inc(s[free], 2)
            dve.wait_ge(s["weights"], LOADS)
            spread_edges(0, 0)
            spread_edges(0, 1)
            attention(0, 0)
            step(0, 0, True)
            step(1, 1, False)
            step(2, 0, False)
            with dve.Fori(0, PAIRS - 2) as i:
                step(i * 2 + 3, 1, False)
                step(i * 2 + 4, 0, False)
            step(T - 2, 1, False)
            step(T - 1, 0, False, final=True)
            second_moments(T - 1, 0)
            second_norm(T - 1, 0)

        @block.tensor
        def _(pe):
            def sums(t, b, half):
                pe.wait_ge(s["spread_ready"], t * 2 + half + 1)
                for j in range(half * HALF, half * HALF + HALF):
                    last = pe.matmul(agg_ps[:, 0:D], spread[:, half, j % HALF, :], messages[:, b, j, :], start=j == 0, stop=j == STEPS - 1)
                return last

            def down(t, b):
                pe.wait_ge(s["hidden_ready"], t * 2 + 2)
                pe.wait_ge(s["down_used"], t)
                for c in range(FF // P):
                    last = pe.matmul(down_ps[:, 0:D], hidden[:, c, :], w_2[:, c, :], start=c == 0, stop=c == FF // P - 1)
                last.then_inc(s["down_done"], 1)

            def attend(t):
                pe.wait_ge(s["ratio_ready"], t)
                for c in range(2):
                    pe.matmul(attn_ps[:, c * P:(c + 1) * P], g.kv[:, c, :], g.q_phi[:, c, bass.ds(t * P, P)], start=True, stop=True)
                for c in range(2):
                    last = pe.matmul(attn_ps[:, D + c * P:D + (c + 1) * P], g.ksum[:, c, :], g.q_phi[:, c, bass.ds(t * P, P)], start=True, stop=True)
                last.then_inc(s["attn_done"], 1)

            def step(t, b, first):
                pe.wait_ge(s["ratio_ready"], t + 1)
                pe.wait_ge(s["h1_ready"], t)
                for c in range(2):
                    last = pe.matmul(out_ps[:, 0:D], ratio[:, c, :], w_o[:, c, :], start=c == 0, stop=c == 1)
                last.then_inc(s["out_done"], 1)
                pe.wait_ge(messages_in[b], uses_before(t, b) * STEPS + 16 * STEPS)
                pe.wait_ge(s["agg_copied"], t)
                sums(t, b, 0).then_inc(s["spread_free"], 1)
                sums(t, b, 1).then_inc(s["agg_done"], 1)
                pe.wait_ge(s["agg_done"], t + 1)
                pe.sem_inc(s["spread_free"], 1)
                pe.sem_inc(s["messages_free"], 1)
                if not (isinstance(t, int) and t == T - 1):
                    attend(t + 1)
                if not first:
                    down(t - 1, 1 - b)
                pe.wait_ge(s["h1_ready"], t + 1)
                pe.wait_ge(s["h1t_ready"], t)
                for c in range(2):
                    last = pe.transpose(turned_ps[:, c * P:(c + 1) * P], h1[:, b, c * P:(c + 1) * P], g.ident[:, :])
                last.then_inc(s["turned_done"], 1)
                pe.wait_ge(s["h1t_ready"], t + 1)
                if not first:
                    pe.wait_ge(s["down_done"], t)
                for u in range(2):
                    for o in range(u * 4, u * 4 + 4):
                        for c in range(2):
                            last = pe.matmul(up_ps[u][:, (o % 4) * P:(o % 4 + 1) * P], w_1[:, c, o * P:(o + 1) * P], h1_t[:, c, :], start=c == 0, stop=c == 1)
                    last.then_inc(s["up_done"], 1)
            pe.wait_ge(s["weights"], LOADS)
            attend(0)
            turns(pe, step, down)


def layer0_experts(nc, g):
    with ExitStack() as ctx:
        sb = lambda n, s, d=F32: ctx.enter_context(nc.sbuf_tensor(n, s, d))
        sem = lambda n: g.semaphore(nc, ctx, n)
        bank = lambda n: ctx.enter_context(nc.psum_tensor(n, [P, 512], F32))
        HC = HID // P
        w_1 = sb("d_w1", [P, NEXP, 2, HID])
        w_2 = sb("d_w2", [P, NEXP, HC, D])
        b_1 = sb("d_b1", [P, NEXP * HC])
        b_2 = sb("d_b2", [NEXP, D])
        w_r = sb("d_wr", [P, 2, NEXP])
        b_r, gamma, beta = sb("d_br", [P, NEXP]), sb("d_gamma", [P, D]), sb("d_beta", [P, D])
        work = sb("d_work", [P, D])
        xe = sb("d_xe", [P, 2, D])
        xe_t = sb("d_xet", [P, 2, 2, P])
        hidden = sb("d_hidden", [P, 2, HC, P])
        logits, top, best = sb("d_logits", [P, NEXP]), sb("d_top", [P, 8]), sb("d_best", [P, 8], U32)
        best_f, gap, ratio, share = sb("d_bestf", [P, 8]), sb("d_gap", [P, 1]), sb("d_ratio", [P, 1]), sb("d_share", [P, 2])
        weight = sb("d_weight", [P, 2, NEXP])
        second = sb("d_second", [P, NEXP])
        weight_t = sb("d_weightt", [NEXP, P])
        stats, mv, rs, tmp = sb("d_stats", [P, 6]), sb("d_mv", [P, 2]), sb("d_rs", [P, 1]), sb("d_tmp", [P, 1])
        turned_ps, route_ps, weight_ps, bias_ps = (bank("d_" + n) for n in ("turn", "route", "weightps", "biasps"))
        up_ps = [bank("d_up0"), bank("d_up1")]
        down_ps = [bank("d_down0"), bank("d_down1")]
        names = ("weights xe_ready turned_done xet_ready routed gap_ready ratio_ready weight_ready weight_turned "
                 "weightt_ready bias_done bias_used up_done hidden_ready down_done down_used").split()
        s = {n: sem("d_" + n) for n in names}
        expert_in = [sem("d_expert_in" + str(e)) for e in range(NEXP)]
        LOADS = 16 * 6
        block = ctx.enter_context(nc.Block())

        @block.sync
        def _(sp):
            sp.dma_start(gamma[:, :], row(g.w["L0_ffn_gamma"])).then_inc(s["weights"], 16)
            sp.dma_start(beta[:, :], row(g.w["L0_ffn_beta"])).then_inc(s["weights"], 16)
            sp.dma_start(w_r[:, :, :], g.w["L0_ffn_Wr"].rearrange("(c p) n -> p c n", p=P)).then_inc(s["weights"], 16)
            sp.dma_start(b_r[:, :], row(g.w["L0_ffn_br"])).then_inc(s["weights"], 16)
            sp.dma_start(b_2[:, :], g.w["L0_ffn_b2"]).then_inc(s["weights"], 16)
            load_columns(sp, b_1[:, :], g.w["L0_ffn_b1"].rearrange("e n -> (e n)")).then_inc(s["weights"], 16)
            for e in range(NEXP):
                sp.dma_start(w_1[:, e, :, :], g.w["L0_ffn_W1"][e, :, :].rearrange("(c p) n -> p c n", p=P)).then_inc(expert_in[e], 16)
                sp.dma_start(w_2[:, e, :, :], g.w["L0_ffn_W2"][e, :, :].rearrange("(c p) n -> p c n", p=P)).then_inc(expert_in[e], 16)

        def tiles(eng, step):
            step(0, 0, False)
            step(1, 1, False)
            with eng.Fori(0, PAIRS - 1) as i:
                step(i * 2 + 2, 0, False)
                step(i * 2 + 3, 1, False)
            step(T - 1, 0, True)

        @block.scalar
        def _(act):
            def copy_turned(t, b):
                act.wait_ge(s["turned_done"], t + 1)
                act.copy(xe_t[:, b, :, :], turned_ps[:, 0:D].rearrange("p (c n) -> p c n", c=2)).then_inc(s["xet_ready"], 1)

            def exponent(t, b):
                act.wait_ge(s["gap_ready"], t + 1)
                act.activation(ratio[:, :], gap[:, :], ACT.Exp).then_inc(s["ratio_ready"], 1)

            def copy_weights(t, b):
                act.wait_ge(s["weight_turned"], t + 1)
                act.copy(weight_t[:, :], weight_ps[0:NEXP, 0:P]).then_inc(s["weightt_ready"], 1)

            def step(t, b, final):
                for e in range(NEXP):
                    act.wait_ge(s["up_done"], t * NEXP + e + 1)
                    for c in range(HC):
                        last = act.activation(hidden[:, e % 2, c, :], up_ps[e % 2][:, c * P:(c + 1) * P], ACT.Gelu,
                                              bias=b_1[:, e * HC + c:e * HC + c + 1])
                    last.then_inc(s["hidden_ready"], 1)
                    if not final and e == 4:
                        copy_turned(t + 1, 1 - b)
                    if not final and e == 5:
                        exponent(t + 1, 1 - b)
                    if not final and e == 7:
                        copy_weights(t + 1, 1 - b)
            act.wait_ge(s["weights"], LOADS)
            copy_turned(0, 0)
            exponent(0, 0)
            copy_weights(0, 0)
            tiles(act, step)

        @block.vector
        def _(dve):
            def rows(t):
                return g.xn[:, bass.ds(t, 1), :].rearrange("p a n -> p (a n)")

            def first_norm(t, b):
                normalise(dve, work[:, :], rows(t), stats[:, :], mv[:, :], rs[:, :], tmp[:, :])
                dve.drain()

            def second_norm(t, b):
                normalise(dve, work[:, :], work[:, :], stats[:, :], mv[:, :], rs[:, :], tmp[:, :])
                dve.drain()

            def affine(t, b):
                dve.tensor_tensor(work[:, :], work[:, :], gamma[:, :], ALU.mult)
                dve.drain()
                dve.tensor_tensor(xe[:, b, :], work[:, :], beta[:, :], ALU.add).then_inc(s["xe_ready"], 1)

            def choose(t, b):
                dve.wait_ge(s["routed"], t + 1)
                dve.tensor_tensor(logits[:, :], route_ps[:, 0:NEXP], b_r[:, :], ALU.add)
                dve.drain()
                dve.max(top[:, :], logits[:, :])
                dve.drain()
                dve.tensor_tensor(gap[:, :], top[:, 1:2], top[:, 0:1], ALU.subtract).then_inc(s["gap_ready"], 1)
                dve.max_index(best[:, :], top[:, :], logits[:, :])
                dve.drain()
                dve.tensor_copy(best_f[:, :], best[:, :])

            def weigh(t, b):
                dve.wait_ge(s["ratio_ready"], t + 1)
                dve.tensor_scalar(share[:, 0:1], ratio[:, :], 1.0, None, ALU.add)
                dve.drain()
                dve.reciprocal(share[:, 0:1], share[:, 0:1])
                dve.drain()
                dve.tensor_tensor(share[:, 1:2], share[:, 0:1], ratio[:, :], ALU.mult)
                dve.drain()
                dve.tensor_scalar(weight[:, b, :], g.node[:, 0:NEXP], best_f[:, 0:1], share[:, 0:1], ALU.is_equal, ALU.mult)
                dve.tensor_scalar(second[:, :], g.node[:, 0:NEXP], best_f[:, 1:2], share[:, 1:2], ALU.is_equal, ALU.mult)
                dve.drain()
                dve.tensor_tensor(weight[:, b, :], weight[:, b, :], second[:, :], ALU.add).then_inc(s["weight_ready"], 1)

            def add_expert(t, b, e):
                dve.wait_ge(s["down_done"], t * NEXP + e + 1)
                dve.scalar_tensor_tensor(rows(t), down_ps[e % 2][:, 0:D], weight[:, b, e:e + 1], rows(t), ALU.mult, ALU.add).then_inc(s["down_used"], 1)
                dve.drain()

            def step(t, b, final):
                dve.wait_ge(s["bias_done"], t + 1)
                dve.tensor_tensor(rows(t), rows(t), bias_ps[:, 0:D], ALU.add).then_inc(s["bias_used"], 1)
                dve.drain()
                for e in range(NEXP):
                    if not final:
                        if e == 0:
                            first_norm(t + 1, 1 - b)
                        if e == 1:
                            second_norm(t + 1, 1 - b)
                        if e == 2:
                            affine(t + 1, 1 - b)
                        if e == 5:
                            choose(t + 1, 1 - b)
                        if e == 6:
                            weigh(t + 1, 1 - b)
                    add_expert(t, b, e)
                dve.bn_stats(stats[:, :], rows(t))
                dve.drain()
                dve.bn_aggr(mv[:, :], stats[:, :])
                dve.drain()
                dve.tensor_copy(g.x_mean[:, bass.ds(t, 1)], mv[:, 0:1])
                dve.tensor_copy(g.x_var[:, bass.ds(t, 1)], mv[:, 1:2])
            dve.wait_ge(s["weights"], LOADS)
            for part in (first_norm, second_norm, affine, choose, weigh):
                part(0, 0)
            tiles(dve, step)

        @block.tensor
        def _(pe):
            def turn(t, b):
                pe.wait_ge(s["xe_ready"], t + 1)
                for c in range(2):
                    last = pe.transpose(turned_ps[:, c * P:(c + 1) * P], xe[:, b, c * P:(c + 1) * P], g.ident[:, :])
                last.then_inc(s["turned_done"], 1)

            def route(t, b):
                pe.wait_ge(s["xet_ready"], t + 1)
                for c in range(2):
                    last = pe.matmul(route_ps[:, 0:NEXP], xe_t[:, b, c, :], w_r[:, c, :], start=c == 0, stop=c == 1)
                last.then_inc(s["routed"], 1)

            def turn_weights(t, b):
                pe.wait_ge(s["weight_ready"], t + 1)
                pe.transpose(weight_ps[0:NEXP, 0:P], weight[:, b, :], g.ident[:, :]).then_inc(s["weight_turned"], 1)

            def biases(t, b):
                pe.wait_ge(s["weightt_ready"], t + 1)
                pe.wait_ge(s["bias_used"], t)
                pe.matmul(bias_ps[:, 0:D], weight_t[:, :], b_2[:, :], start=True, stop=True).then_inc(s["bias_done"], 1)

            def up(t, b, e):
                if isinstance(t, int) and t == 0:
                    pe.wait_ge(expert_in[e], 32)
                pe.wait_ge(s["hidden_ready"], (t * NEXP + e - 1) if e >= 1 else t * NEXP)
                for c in range(HC):
                    for k in range(2):
                        last = pe.matmul(up_ps[e % 2][:, c * P:(c + 1) * P], w_1[:, e, k, c * P:(c + 1) * P], xe_t[:, b, k, :], start=k == 0, stop=k == 1)
                last.then_inc(s["up_done"], 1)

            def down(t, b, e):
                pe.wait_ge(s["hidden_ready"], t * NEXP + e + 1)
                pe.wait_ge(s["down_used"], (t * NEXP + e - 1) if e >= 1 else t * NEXP)
                for c in range(HC):
                    last = pe.matmul(down_ps[e % 2][:, 0:D], hidden[:, e % 2, c, :], w_2[:, e, c, :], start=c == 0, stop=c == HC - 1)
                last.then_inc(s["down_done"], 1)

            def step(t, b, final):
                for e in range(NEXP):
                    up(t, b, e)
                    if not final:
                        if e == 4:
                            turn(t + 1, 1 - b)
                        if e == 5:
                            route(t + 1, 1 - b)
                        if e == 7:
                            turn_weights(t + 1, 1 - b)
                    if e:
                        down(t, b, e - 1)
                if not final:
                    biases(t + 1, 1 - b)
                down(t, b, NEXP - 1)
            pe.wait_ge(s["weights"], LOADS)
            for part in (turn, route, turn_weights, biases):
                part(0, 0)
            tiles(pe, step)


def layer1_projections(nc, g):
    with ExitStack() as ctx:
        sb = lambda n, s, d=F32: ctx.enter_context(nc.sbuf_tensor(n, s, d))
        sem = lambda n: g.semaphore(nc, ctx, n)
        bank = lambda n: ctx.enter_context(nc.psum_tensor(n, [P, 512], F32))
        w_att = sb("c_watt", [P, 2, D + 8])
        att = sb("c_att", [P, 2, D])
        folded = sb("c_folded", [P, 2, 4, 64])
        w_conv = sb("c_wconv", [P, 2, CQ])
        valid = sb("c_valid", [P, T])
        var, rstd, rstd_log = (sb("c_" + n, [P, T]) for n in ("var", "rstd", "rstdlog"))
        norm2, inv, clipped, sq, series, log_up, log_down, tmp, small = (sb("c_s" + str(i), [P, T]) for i in range(9))
        pair = sb("c_pair", [P, 2, 2, D])
        pair_t = sb("c_pairt", [P, 2, 4, P])
        table = sb("c_table", [P, 2, TBL])
        own_score = sb("c_own", [P, 2, 4])
        conv = sb("c_conv", [P, 2, 6, P])
        turned_ps = bank("c_turn")
        att_banks, conv_banks0, conv_banks1 = ([bank("c_" + n + str(b)) for b in range(2)] for n in ("attps", "conv0", "conv1"))
        names = ("weights valid_made clipped_ready logs_ready pair_ready turned_done pairt_ready projected dst_taken "
                 "table_ready conv_ready stats_taken").split()
        s = {n: sem("c_" + n) for n in names}
        table_out = [sem("c_table_out0"), sem("c_table_out1")]
        conv_out = [sem("c_conv_out0"), sem("c_conv_out1")]
        LOADS = 16 * 4
        block = ctx.enter_context(nc.Block())

        @block.sync
        def _(sp):
            sp.dma_start(w_att[:, :, 0:D], g.w["L1_gnn_W"].rearrange("(c p) n -> p c n", p=P)).then_inc(s["weights"], 16)
            sp.dma_start(att[:, 0, :], row(g.w["L1_gnn_att_src"].rearrange("h c -> (h c)"))).then_inc(s["weights"], 16)
            sp.dma_start(att[:, 1, :], row(g.w["L1_gnn_att_dst"].rearrange("h c -> (h c)"))).then_inc(s["weights"], 16)
            sp.dma_start(w_conv[:, :, :], g.w["L1_mix_w_qkv"][:, 2, :].rearrange("(c p) n -> p c n", p=P)).then_inc(s["weights"], 16)

            def step(t, b):
                sp.wait_ge(s["table_ready"], t + 1)
                sp.dma_start(g.att_table[bass.ds(t * P, P), :], table[:, b, :]).then_inc(table_out[b], 16)
                sp.wait_ge(s["conv_ready"], t + 1)
                sp.dma_start(g.conv[bass.ds(t, 1), :, :].rearrange("a (c p) n -> p (a c) n", p=P), conv[:, b, :, :]).then_inc(conv_out[b], 16)
            over_pairs(sp, step)
            for done in (table_out, conv_out):
                sp.wait_ge(done[0], 16 * ((T + 1) // 2))
                sp.wait_ge(done[1], 16 * (T // 2))

        @block.gpsimd
        def _(pool):
            pool.memset(valid[:, :], 1.0)
            pool.drain()
            pool.affine_select(out=valid[:, :], in_=valid[:, :], compare_op=ALU.is_gt, fill=0.0,
                               base=N, pattern=[[-P, T]], channel_multiplier=-1).then_inc(s["valid_made"], 1)

        @block.scalar
        def _(act):
            act.wait_ge(s["clipped_ready"], 1)
            act.activation(log_up[:, :], clipped[:, :], ACT.Ln, bias=1.0)
            act.activation(log_down[:, :], small[:, :], ACT.Ln).then_inc(s["logs_ready"], 1)

            def copy_turned(t, b):
                act.wait_ge(s["turned_done"], t + 1)
                act.copy(pair_t[:, b, :, :], turned_ps[:, :].rearrange("p (c n) -> p c n", c=4)).then_inc(s["pairt_ready"], 1)

            def step(t, b):
                att_ps, conv_ps0, conv_ps1 = att_banks[b], conv_banks0[b], conv_banks1[b]
                if not at_least(t, T - 1):
                    act.wait_ge(s["projected"], t)
                    copy_turned(t + 1, 1 - b)
                act.wait_ge(s["projected"], t + 1)
                act.wait_ge(s["dst_taken"], t + 1)
                act.copy(table[:, b, 0:D + 4], att_ps[:, 0:D + 4]).then_inc(s["table_ready"], 1)
                act.wait_ge(conv_out[b], uses_before(t, b))
                if not at_most(t, 1):
                    act.wait_ge(s["stats_taken"], t - 1)
                act.copy(conv[:, b, 0:4, :], conv_ps0[:, :].rearrange("p (c n) -> p c n", c=4))
                act.copy(conv[:, b, 4:6, :], conv_ps1[:, 0:2 * P].rearrange("p (c n) -> p c n", c=2)).then_inc(s["conv_ready"], 1)
            copy_turned(0, 0)
            over_tiles(act, step)

        @block.vector
        def _(dve):
            dve.tensor_scalar(var[:, :], g.x_var[:, :], EPS, None, ALU.add)
            dve.drain()
            newton_rsqrt(dve, rstd[:, :], var[:, :], tmp[:, :])
            dve.tensor_tensor(norm2[:, :], rstd[:, :], rstd[:, :], ALU.mult)
            dve.drain()
            dve.scalar_tensor_tensor(norm2[:, :], g.x_var[:, :], float(D), norm2[:, :], ALU.mult, ALU.mult)
            dve.drain()
            dve.tensor_scalar(norm2[:, :], norm2[:, :], 1e-30, None, ALU.max)
            dve.drain()
            newton_rsqrt(dve, inv[:, :], norm2[:, :], tmp[:, :])
            dve.tensor_tensor(clipped[:, :], norm2[:, :], inv[:, :], ALU.mult)
            dve.drain()
            dve.tensor_scalar(clipped[:, :], clipped[:, :], MAXNORM, None, ALU.min)
            dve.drain()
            dve.tensor_scalar(small[:, :], clipped[:, :], -1.0, 1.0, ALU.mult, ALU.add)
            dve.drain()
            dve.tensor_tensor(sq[:, :], clipped[:, :], clipped[:, :], ALU.mult).then_inc(s["clipped_ready"], 1)
            dve.drain()
            dve.tensor_scalar(series[:, :], sq[:, :], 1.0 / 11, 1.0 / 9, ALU.mult, ALU.add)
            dve.drain()
            for c in (7, 5, 3, 1):
                dve.tensor_tensor(series[:, :], series[:, :], sq[:, :], ALU.mult)
                dve.drain()
                dve.tensor_scalar(series[:, :], series[:, :], 1.0 / c, None, ALU.add)
                dve.drain()
            dve.tensor_tensor(series[:, :], series[:, :], clipped[:, :], ALU.mult)
            dve.wait_ge(s["logs_ready"], 1)
            dve.tensor_tensor(log_up[:, :], log_up[:, :], log_down[:, :], ALU.subtract)
            dve.drain()
            dve.tensor_scalar(log_up[:, :], log_up[:, :], 0.5, None, ALU.mult)
            dve.tensor_scalar(small[:, :], clipped[:, :], 0.25, None, ALU.is_lt)
            dve.drain()
            dve.tensor_tensor(series[:, :], series[:, :], log_up[:, :], ALU.subtract)
            dve.drain()
            dve.tensor_tensor(series[:, :], series[:, :], small[:, :], ALU.mult)
            dve.drain()
            dve.tensor_tensor(series[:, :], series[:, :], log_up[:, :], ALU.add)
            dve.drain()
            dve.tensor_tensor(series[:, :], series[:, :], inv[:, :], ALU.mult)
            dve.wait_ge(s["valid_made"], 1)
            dve.drain()
            dve.tensor_tensor(series[:, :], series[:, :], valid[:, :], ALU.mult)
            dve.drain()
            dve.tensor_tensor(rstd_log[:, :], series[:, :], rstd[:, :], ALU.mult)
            dve.wait_ge(s["weights"], LOADS)
            for c in range(2):
                for k in range(2):
                    dve.tensor_tensor(folded[:, k, :, :], w_att[:, c, 0:D].rearrange("p (h n) -> p h n", h=4), att[:, k, :].rearrange("p (h n) -> p h n", h=4), ALU.mult)
                dve.drain()
                dve.reduce_sum(w_att[:, c, D:D + 8].rearrange("p (k h) -> p k h", k=2), folded[:, :, :, :], axis=AX.X)
                dve.drain()

            def rows(t, b):
                if not at_most(t, 1):
                    dve.wait_ge(s["turned_done"], t - 1)
                x2 = g.xn[:, bass.ds(t, 1), :].rearrange("p a n -> p (a n)")
                at = bass.ds(t, 1)
                dve.tensor_scalar(pair[:, b, 0, :], x2, g.x_mean[:, at], rstd[:, at], ALU.subtract, ALU.mult)
                dve.tensor_scalar(pair[:, b, 1, :], x2, g.x_mean[:, at], rstd_log[:, at], ALU.subtract, ALU.mult).then_inc(s["pair_ready"], 1)

            def step(t, b):
                att_ps = att_banks[b]
                if not at_least(t, T - 2):
                    rows(t + 2, b)
                dve.wait_ge(s["projected"], t + 1)
                dve.tensor_copy(own_score[:, :, :].rearrange("p k h -> p (k h)"), att_ps[:, D:D + 8])
                dve.tensor_copy(g.a_dst[:, bass.ds(t, 1), :].rearrange("p a n -> p (a n)"), att_ps[:, D + 4:D + 8])
                dve.drain()
                dve.wait_ge(table_out[b], uses_before(t, b))
                own = table[:, b, D + 4:D + 8]
                dve.tensor_tensor(own, own_score[:, 0, :], own_score[:, 1, :], ALU.add)
                dve.drain()
                dve.scalar_tensor_tensor(own, own, 0.2, own, ALU.mult, ALU.max).then_inc(s["dst_taken"], 1)
                dve.wait_ge(s["conv_ready"], t + 1)
                for c in range(6):
                    last = dve.bn_stats(g.conv_stats[:, c, bass.ds(t, 1), :].rearrange("p a n -> p (a n)"), conv[:, b, c, :])
                last.then_inc(s["stats_taken"], 1)
            dve.memset(table[:, :, D + 8:D + 12], 1.0)
            rows(0, 0)
            rows(1, 1)
            over_tiles(dve, step)

        @block.tensor
        def _(pe):
            pe.wait_ge(s["weights"], LOADS)

            def turn(t, b):
                pe.wait_ge(s["pair_ready"], t + 1)
                pe.wait_ge(s["pairt_ready"], t)
                for k in range(2):
                    for c in range(2):
                        last = pe.transpose(turned_ps[:, (k * 2 + c) * P:(k * 2 + c + 1) * P], pair[:, b, k, c * P:(c + 1) * P], g.ident[:, :])
                last.then_inc(s["turned_done"], 1)

            def step(t, b):
                att_ps, conv_ps0, conv_ps1 = att_banks[b], conv_banks0[b], conv_banks1[b]
                if not at_least(t, T - 1):
                    turn(t + 1, 1 - b)
                pe.wait_ge(s["pairt_ready"], t + 1)
                if not at_most(t, 1):
                    pe.wait_ge(s["conv_ready"], t - 1)
                for c in range(2):
                    pe.matmul(att_ps[:, 0:D + 8], pair_t[:, b, c, :], w_att[:, c, :], start=c == 0, stop=c == 1)
                for o in range(6):
                    out = (conv_ps0 if o < 4 else conv_ps1)[:, (o % 4) * P:(o % 4 + 1) * P]
                    for c in range(2):
                        last = pe.matmul(out, w_conv[:, c, o * P:(o + 1) * P], pair_t[:, b, 2 + c, :], start=c == 0, stop=c == 1)
                last.then_inc(s["projected"], 1)
            turn(0, 0)
            over_tiles(pe, step)


def split_bf16(dve, parts, x, rest):
    dve.tensor_copy(parts[0], x)
    dve.drain()
    dve.tensor_tensor(rest, x, parts[0], ALU.subtract)
    dve.drain()
    dve.tensor_copy(parts[1], rest)
    dve.drain()
    dve.tensor_tensor(rest, rest, parts[1], ALU.subtract)
    dve.drain()
    dve.tensor_copy(parts[2], rest)


def layer1_outputs(nc, g):
    with ExitStack() as ctx:
        sb = lambda n, s, d=F32: ctx.enter_context(nc.sbuf_tensor(n, s, d))
        sem = lambda n: g.semaphore(nc, ctx, n)
        bank = lambda n, d=F32: ctx.enter_context(nc.psum_tensor(n, [P, 2048 // (4 if d == F32 else 2)], d))
        S4 = STEPS * 4
        sources = sb("e_sources", [P, 2, STEPS], I32)
        messages = sb("e_messages", [P, 2, STEPS, TBL])
        own = sb("e_own", [P, 2, TBL])
        spread, spread_h, spread_t = sb("e_spread", [P, STEPS, P]), sb("e_spreadh", [P, STEPS, P], BF16), sb("e_spreadt", [P, STEPS, P], BF16)
        ident_h = sb("e_identh", [P, P], BF16)
        score, first = sb("e_score", [P, STEPS, 4]), sb("e_first4", [P, STEPS, 4])
        rows_t, run = sb("e_rowst", [S4, 2 * P]), sb("e_run", [S4, P])
        run_last, rest = sb("e_runlast", [P, STEPS, 4]), sb("e_rest", [P, STEPS, 4])
        run_h = sb("e_runh", [P, STEPS, 13], BF16)
        picked, picked_sum, absent = sb("e_picked", [P, STEPS, 13]), sb("e_pickedsum", [P, STEPS, 4]), sb("e_absent", [P, STEPS, 1])
        per_node, node_rest, node_h = sb("e_pernode", [P, 8]), sb("e_noderest", [P, 8]), sb("e_nodeh", [P, 3, 8], BF16)
        top_src = sb("e_topsrc", [P, 4])
        own_den = sb("e_ownden", [P, 4])
        fetched, fetched_sum = sb("e_fetched", [P, STEPS, 24]), sb("e_fetchedsum", [P, STEPS, 8])
        z = sb("e_z", [P, S4 + 4])
        ex = sb("e_ex", [P, 2, S4 + 4])
        agg, den = sb("e_agg", [P, D]), sb("e_den", [P, 4])
        b_gat = sb("e_bgat", [P, D])
        gat_neg, gat = sb("e_gatneg", [P, D]), sb("e_gat", [P, 2, D])
        conv_in = sb("e_conv", [P, 2, 6, P])
        bn_mv, bn_a, bn_b, bn_t, gamma, beta = sb("e_bnmv", [P, 6, 2]), sb("e_bna", [P, 6]), sb("e_bnb", [P, 6]), sb("e_bnt", [P, 6]), sb("e_gamma", [P, 6]), sb("e_beta", [P, 6])
        w_dw, w_pw = sb("e_wdw", [P, 6]), sb("e_wpw", [P, 6, P])
        cat = sb("e_cat", [P, 16, 96])
        squares = sb("e_squares", [P, 2 * CQ])
        norm2, exponent, scale1 = (sb("e_" + n, [P, 1]) for n in ("norm2", "exponent", "scale1"))
        root_in = [sb("e_rootin" + str(i), [P, 1]) for i in range(5)]
        r1 = sb("e_r1", [P, 2])
        k_sum, mixed, divisor = sb("e_ksum", [P, 16]), sb("e_mixed", [P, 16, 32]), sb("e_divisor", [P, 16, 32])
        norm3, scale3 = sb("e_norm3", [P, 1]), sb("e_scale3", [P, 1])
        mixed_t, w_res, b_res = sb("e_mixedt", [P, 4, P]), sb("e_wres", [P, 4, D]), sb("e_bres", [P, D])
        ft, norm4, r4, tanh4, length4 = sb("e_ft", [P, D]), sb("e_norm4", [P, 1]), sb("e_r4", [P, 1]), sb("e_tanh4", [P, 1]), sb("e_length4", [P, 1])
        radius4 = sb("e_radius4", [P, 1])
        xf, xf_t = sb("e_xf", [P, D]), sb("e_xft", [P, 2, P])
        stats, mv, rs = sb("e_stats", [P, 6]), sb("e_mv", [P, 2]), sb("e_rs", [P, 1])
        s_w1, s_w2, s_w3 = sb("e_sw1", [P, 2, D]), sb("e_sw2", [P, 2, P]), sb("e_sw3", [P, D])
        x_w1, x_w2, x_w3 = sb("e_xw1", [P, 4, 2, P]), sb("e_xw2", [P, 4, 64]), sb("e_xw3", [64, 4, D])
        s_b1, s_b2, x_b1, x_b2 = sb("e_sb1", [P, 2]), sb("e_sb2", [P, 1]), sb("e_xb1", [P, 4]), sb("e_xb2", [64, 4])
        out_b = sb("e_outb", [5, D])
        g_w, g_b = sb("e_gw", [P, 2, 4]), sb("e_gb", [P, 4])
        hid_s, hid_x, hid_s2, hid_x2 = sb("e_hids", [P, 2, P]), sb("e_hidx", [P, 4, P]), sb("e_hids2", [P, P]), sb("e_hidx2", [64, 4, P])
        gate, gate_e, gate_m, gate_s = sb("e_gate", [P, 8]), sb("e_gatee", [P, 4]), sb("e_gatem", [P, 1]), sb("e_gates", [P, 1])
        top, best, best_f, gap, ratio, share = sb("e_top", [P, 8]), sb("e_best", [P, 8], U32), sb("e_bestf", [P, 8]), sb("e_gap", [P, 1]), sb("e_ratio", [P, 1]), sb("e_share", [P, 2])
        weight, second, weight_t = sb("e_weightx", [P, 5]), sb("e_second", [P, 4]), sb("e_weightt", [5, P])
        result = sb("e_result", [P, 2, D])
        st_ps = [bank("e_st0", BF16), bank("e_st1", BF16)]
        sc_ps, agg_ps, m_ps, f_ps = bank("e_sc"), bank("e_aggps"), [bank("e_m0"), bank("e_m1")], [bank("e_f0"), bank("e_f1")]
        names = ("weights identh sources_ready gathers_begun messages_free own_free spread_ready spreadh_ready scores_ready turned_rows rows_ready "
                 "run_ready run_turned st_done st_copied runh_ready picked_done picked_ready nodeh_ready fetched_done fetched_ready "
                 "z_ready ex_ready scaled agg_done gat_neg gat_exp "
                 "bn_ready h_in lifted m_done m_copied norm2_ready scale1_ready scaled_cat mixed_ready norm3_ready mixed_turned mixedt_ready res_done "
                 "ft_ready norm4_ready length_ready tanh_ready x3_ready "
                 "roots_begun bounded_1 bounded_3 bounded_4 bounded_f rooted_1 rooted_3 rooted_4 scale3_ready moments_ready rs_ready xf_ready xf_turned xft_ready gates_done hidden1 hidden1_ready hidden2 hidden2_ready gate_max gate_exp gap_ready ratio_ready weight_ready weight_turned weightt_ready "
                 "expert_done expert_used result_ready").split()
        s = {n: sem("e_" + n) for n in names}
        messages_in = g.messages_in[2:4]
        own_in = [sem("e_own_in0"), sem("e_own_in1")]
        conv_loaded = [sem("e_conv_in0"), sem("e_conv_in1")]
        result_out = [sem("e_result_out0"), sem("e_result_out1")]
        LOADS = 16 * 28
        block = ctx.enter_context(nc.Block())

        def expert_ps(e):
            return (f_ps[0], m_ps[0])[e // 2][:, e % 2 * D:(e % 2 + 1) * D]

        def one_turn(order, chains, t, b, on):
            G, X, F = chains
            parts = {"G": G(t + 1, 1 - b) if on[0] else {}, "Y": X(t + 1, 1 - b) if on[0] else {},
                     "Z": G(t, b) if on[1] else {}, "X": X(t, b) if on[1] else {}, "F": F(t - 1, 1 - b) if on[2] else {}}
            for name in order:
                chain, part = name.split(".")
                if part in parts[chain]:
                    parts[chain][part]()

        def turns(eng, turn):
            turn(-1, 1, True, False, False)
            turn(0, 0, True, True, False)
            turn(1, 1, True, True, True)
            turn(2, 0, True, True, True)
            with eng.Fori(0, PAIRS - 2) as i:
                turn(i * 2 + 3, 1, True, True, True)
                turn(i * 2 + 4, 0, True, True, True)
            turn(T - 2, 1, True, True, True)
            turn(T - 1, 0, False, True, True)
            turn(T, 1, False, False, True)

        @block.sync
        def _(sp):
            def load(out, src):
                sp.dma_start(out, src).then_inc(s["weights"], 16)
            load(w_res[:, :, :], g.w["L1_mix_w_res"][:, 0, :].rearrange("(c p) n -> p c n", p=P))
            load(s_w1[:, :, :], g.w["L1_ffn_sW1"].rearrange("(c p) n -> p c n", p=P))
            load(s_w2[:, :, :], g.w["L1_ffn_sW2"].rearrange("(c p) n -> p c n", p=P))
            load(s_w3[:, :], g.w["L1_ffn_sW3"])
            load(x_w1[:, :, :, :], g.w["L1_ffn_eW1"].rearrange("e (c p) n -> p e c n", p=P))
            load(x_w2[:, :, :], g.w["L1_ffn_eW2"].rearrange("e p n -> p e n"))
            load(x_w3[:, :, :], g.w["L1_ffn_eW3"].rearrange("e p n -> p e n"))
            load(out_b[0:4, :], g.w["L1_ffn_eb3"])
            load(out_b[4:5, :], row(g.w["L1_ffn_sb3"], 1))
            load(g_w[:, :, :], g.w["L1_ffn_gW"].rearrange("(c p) n -> p c n", p=P))
            load(g_b[:, :], row(g.w["L1_ffn_gb"]))
            load(b_gat[:, :], row(g.w["L1_gnn_bias"]))
            load(b_res[:, :], row(g.w["L1_mix_b_res"]))
            for out, vector in ((gamma, g.w["L1_mix_bn_gamma"]), (beta, g.w["L1_mix_bn_beta"]), (w_dw, g.w["L1_mix_w_dw"][0, 2, :]),
                                (s_b1, g.w["L1_ffn_sb1"]), (s_b2, g.w["L1_ffn_sb2"]), (x_b1, g.w["L1_ffn_eb1"].rearrange("e n -> (e n)"))):
                load_columns(sp, out[:, :], vector).then_inc(s["weights"], 16)
            sp.dma_start(x_b2[:, :], g.w["L1_ffn_eb2"].rearrange("e n -> n e"), allow_slow_non_contiguous=True).then_inc(s["weights"], 16)
            sp.wait_ge(s["identh"], 1)
            for r in range(4):
                part = slice(32 * r, 32 * r + 32)
                load(w_pw[part, :, part], g.w["L1_mix_w_pw"][:, 0, :].rearrange("p (c r n) -> p c r n", r=4, n=32)[:, :, r, :])
            load(own[:, 0, :], g.att_table[0:P, :])
            load(own[:, 1, :], g.att_table[P:2 * P, :])
            load(conv_in[:, 0, :, :], g.conv[0, :, :].rearrange("(c p) n -> p c n", p=P))
            load(conv_in[:, 1, :, :], g.conv[1, :, :].rearrange("(c p) n -> p c n", p=P))

            def store(t, b):
                sp.wait_ge(s["result_ready"], t + 1)
                sp.dma_start(g.out[bass.ds(t * P, P), :], result[:, b, :]).then_inc(result_out[b], 16)

            def refill(t, b):
                sp.wait_ge(s["own_free"], t - 1)
                sp.dma_start(own[:, b, :], g.att_table[bass.ds(t * P, P), :]).then_inc(own_in[b], 16)
                sp.wait_ge(s["lifted"], t - 1)
                sp.dma_start(conv_in[:, b, :, :], g.conv[bass.ds(t, 1), :, :].rearrange("a (c p) n -> p (a c) n", p=P)).then_inc(conv_loaded[b], 16)

            refill(2, 0)
            with sp.Fori(0, PAIRS - 1) as i:
                refill(i * 2 + 3, 1)
                store(i * 2, 0)
                refill(i * 2 + 4, 0)
                store(i * 2 + 1, 1)
            store(T - 3, 0)
            store(T - 2, 1)
            store(T - 1, 0)
            sp.wait_ge(result_out[0], 16 * ((T + 1) // 2))
            sp.wait_ge(result_out[1], 16 * (T // 2))

        @block.gpsimd
        def _(pool):
            pool.memset(w_pw[:, :, :], 0.0)
            pool.drain()
            pool.memset(exponent[:, :], -0.5)
            pool.tensor_copy(ident_h[:, :], g.ident[:, :]).then_inc(s["identh"], 1)

            def inverse_root(t, out, root_in, x, low, op, bounded, rooted):
                pool.sem_inc(s["roots_begun"], 1)
                pool.tensor_scalar(root_in[:, :], x, low, None, op).then_inc(s[bounded], 1)
                pool.wait_ge(s[bounded], t + 1)
                pool.sem_inc(s["roots_begun"], 1)
                last = pool.tensor_tensor(out, root_in[:, :], exponent[:, :], ALU.pow)
                last.then_inc(s[rooted], 1)
                if rooted != "rs_ready":
                    pool.wait_ge(s[rooted], t + 1)
                    pool.sem_inc(s["roots_begun"], 1)

            def gather(t, b, part):
                if part == 0:
                    pool.wait_ge(s["messages_free"], t + 1)
                    pool.tensor_copy(sources[:, b, :], g.e_src[:, bass.ds(t * STEPS, STEPS)]).then_inc(s["sources_ready"], 1)
                    pool.wait_ge(s["sources_ready"], t + 1)
                    pool.sem_inc(s["gathers_begun"], 1)
                for j in range(part * STEPS // 3, (part + 1) * STEPS // 3):
                    pool.indirect_dma_start(messages[:, b, j, :], None, g.att_table[:, :],
                                            bass.IndirectOffsetOnAxis(ap=sources[:, b, j:j + 1], axis=0)).then_inc(messages_in[b], 16)

            def X(t, b):
                def cut(out, r1, root_in, norm, bounded, rooted):
                    inverse_root(t, r1, root_in, norm, 1e-30, ALU.max, bounded, rooted)
                    return pool.tensor_scalar(out, r1, ATANH_MAX, 1.0, ALU.mult, ALU.min)

                def scale_1():
                    pool.wait_ge(s["norm2_ready"], t + 1)
                    cut(scale1[:, :], r1[:, 0:1], root_in[1], norm2[:, :], "bounded_1", "rooted_1").then_inc(s["scale1_ready"], 1)

                def scale_3():
                    pool.wait_ge(s["norm3_ready"], t + 1)
                    pool.wait_ge(s["ft_ready"], t)
                    cut(scale3[:, :], r1[:, 1:2], root_in[3], norm3[:, :], "bounded_3", "rooted_3").then_inc(s["scale3_ready"], 1)

                def length():
                    pool.wait_ge(s["norm4_ready"], t + 1)
                    inverse_root(t, r4[:, :], root_in[4], norm4[:, :], 1e-30, ALU.max, "bounded_4", "rooted_4")
                    pool.tensor_tensor(length4[:, :], root_in[4][:, :], r4[:, :], ALU.mult).then_inc(s["length_ready"], 1)
                return {"scale_1": scale_1, "scale_3": scale_3, "length": length}

            def F(t, b):
                def root():
                    pool.wait_ge(s["moments_ready"], t + 1)
                    inverse_root(t, rs[:, :], root_in[0], mv[:, 1:2], EPS, ALU.add, "bounded_f", "rs_ready")
                return {"root": root}

            def G(t, b):
                if isinstance(t, int) and t >= T - 1:
                    return {}
                return {"first": lambda: gather(t + 1, 1 - b, 0), "second": lambda: gather(t + 1, 1 - b, 1), "third": lambda: gather(t + 1, 1 - b, 2)}

            ORDER = "F.root X.scale_3 G.first X.length G.second Y.scale_1 G.third".split()

            def turn(t, b, *on):
                one_turn(ORDER, (G, X, F), t, b, on)
            for part in range(3):
                gather(0, 0, part)
            turns(pool, turn)

        @block.scalar
        def _(act):
            def G(t, b):
                def halves():
                    act.wait_ge(s["agg_done"], t)
                    act.wait_ge(s["spread_ready"], t + 1)
                    act.copy(spread_h[:, :, :], spread[:, :, :]).then_inc(s["spreadh_ready"], 1)

                def rows_():
                    act.wait_ge(s["turned_rows"], t + 1)
                    act.copy(rows_t[:, :], sc_ps[0:S4, 0:2 * P]).then_inc(s["rows_ready"], 1)

                def turned():
                    for r in range(3):
                        act.wait_ge(s["st_done"], t * 3 + r + 1)
                        act.copy(spread_t[:, r * 6:r * 6 + 6, :], st_ps[r % 2][:, 0:6 * P].rearrange("p (j n) -> p j n", j=6)).then_inc(s["st_copied"], 1)

                def picks():
                    act.wait_ge(s["picked_done"], t + 1)
                    act.copy(picked[:, :, :], sc_ps[:, 0:STEPS * 13].rearrange("p (j n) -> p j n", j=STEPS)).then_inc(s["picked_ready"], 1)

                def fetches():
                    act.wait_ge(s["fetched_done"], t + 1)
                    act.copy(fetched[:, :, :], sc_ps[:, 0:STEPS * 24].rearrange("p (j n) -> p j n", j=STEPS)).then_inc(s["fetched_ready"], 1)

                def exps():
                    act.wait_ge(s["z_ready"], t + 1)
                    act.activation(ex[:, b, :], z[:, :], ACT.Exp).then_inc(s["ex_ready"], 1)

                def elu():
                    act.wait_ge(s["gat_neg"], t + 1)
                    act.activation(gat_neg[:, :], gat_neg[:, :], ACT.Exp).then_inc(s["gat_exp"], 1)
                return {"halves": halves, "rows": rows_, "turned": turned, "picks": picks, "fetches": fetches, "exps": exps, "elu": elu}

            def X(t, b):
                def relu():
                    act.wait_ge(conv_loaded[b], uses_before(t, b))
                    for c in range(6):
                        last = act.activation(conv_in[:, b, c, :], conv_in[:, b, c, :], ACT.Relu, bias=bn_b[:, c:c + 1], scale=bn_a[:, c:c + 1])
                    last.then_inc(s["h_in"], 1)

                def copies():
                    flat = cat[:, :, :].rearrange("p a n -> p (a n)")
                    act.wait_ge(s["mixed_ready"], t)
                    for r in range(2):
                        act.wait_ge(s["m_done"], t * 2 + r + 1)
                        act.copy(flat[:, r * 384:r * 384 + 384], m_ps[0][:, 0:384])
                        act.copy(flat[:, CQ + r * 384:CQ + r * 384 + 384], m_ps[1][:, 0:384]).then_inc(s["m_copied"], 1)
                    act.drain()
                    act.activation(squares[:, :], flat, ACT.Square, accum_out=norm2[:, :]).then_inc(s["norm2_ready"], 1)

                def scale():
                    act.wait_ge(s["scale1_ready"], t + 1)
                    act.activation(cat[:, :, 0:64], cat[:, :, 0:64], ACT.Relu, scale=scale1[:, :])
                    act.activation(cat[:, :, 64:96], cat[:, :, 64:96], ACT.Copy, scale=scale1[:, :]).then_inc(s["scaled_cat"], 1)

                def square3():
                    act.wait_ge(s["mixed_ready"], t + 1)
                    act.activation(squares[:, 0:512], mixed[:, :, :].rearrange("p a n -> p (a n)"), ACT.Square, accum_out=norm3[:, :]).then_inc(s["norm3_ready"], 1)

                def turned():
                    act.wait_ge(s["mixed_turned"], t + 1)
                    act.copy(mixed_t[:, :, :], f_ps[0][:, :].rearrange("p (c n) -> p c n", c=4)).then_inc(s["mixedt_ready"], 1)

                def square4():
                    act.drain()
                    act.wait_ge(s["ft_ready"], t + 1)
                    act.activation(squares[:, 0:D], ft[:, :], ACT.Square, accum_out=norm4[:, :]).then_inc(s["norm4_ready"], 1)

                def tanh():
                    act.wait_ge(s["length_ready"], t + 1)
                    act.activation(tanh4[:, :], length4[:, :], ACT.Tanh).then_inc(s["tanh_ready"], 1)
                return {"relu": relu, "copies": copies, "scale": scale, "square3": square3, "turned": turned, "square4": square4, "tanh": tanh}

            def F(t, b):
                def turned():
                    act.wait_ge(s["xf_turned"], t + 1)
                    act.copy(xf_t[:, :, :], m_ps[0][:, 0:D].rearrange("p (c n) -> p c n", c=2)).then_inc(s["xft_ready"], 1)

                def layer_1():
                    act.wait_ge(s["hidden1"], t + 1)
                    for c in range(2):
                        act.activation(hid_s[:, c, :], f_ps[1][:, c * P:(c + 1) * P], ACT.Relu, bias=s_b1[:, c:c + 1])
                    for e in range(4):
                        last = act.activation(hid_x[:, e, :], f_ps[0][:, e * P:(e + 1) * P], ACT.Relu, bias=x_b1[:, e:e + 1])
                    last.then_inc(s["hidden1_ready"], 1)

                def gates():
                    act.wait_ge(s["gate_max"], t + 1)
                    act.activation(gate_e[:, :], gate[:, 0:4], ACT.Exp, bias=gate_m[:, :], accum_out=gate_s[:, :]).then_inc(s["gate_exp"], 1)

                def layer_2():
                    act.wait_ge(s["hidden2"], t + 1)
                    act.activation(hid_s2[:, :], f_ps[1][:, 0:P], ACT.Relu, bias=s_b2[:, :])
                    for e in range(4):
                        last = act.activation(hid_x2[:, e, :], f_ps[0][0:64, e * P:(e + 1) * P], ACT.Relu, bias=x_b2[:, e:e + 1])
                    last.then_inc(s["hidden2_ready"], 1)

                def ratios():
                    act.wait_ge(s["gap_ready"], t + 1)
                    act.activation(ratio[:, :], gap[:, :], ACT.Exp).then_inc(s["ratio_ready"], 1)

                def weights():
                    act.wait_ge(s["weight_turned"], t + 1)
                    act.copy(weight_t[:, :], m_ps[0][0:5, 0:P]).then_inc(s["weightt_ready"], 1)
                return {"turned": turned, "layer_1": layer_1, "gates": gates, "layer_2": layer_2, "ratios": ratios, "weights": weights}

            ORDER = ("X.square3 X.turned G.rows F.turned G.halves Z.elu G.turned G.picks X.square4 X.tanh F.gates Y.relu F.ratios "
                     "F.layer_1 G.fetches Y.copies G.exps F.layer_2 F.weights Y.scale").split()
            act.wait_ge(s["weights"], LOADS)
            act.wait_ge(s["bn_ready"], 1)

            def turn(t, b, *on):
                one_turn(ORDER, (G, X, F), t, b, on)
            turns(act, turn)

        @block.vector
        def _(dve):
            def rows(t):
                return g.xn[:, bass.ds(t, 1), :].rearrange("p a n -> p (a n)")

            def heads(x):
                return x.rearrange("p (h n) -> p h n", h=4)

            def wide(x, n):
                return x.unsqueeze(2).broadcast_to([P, x.shape[1], n])

            def G(t, b):
                at = bass.ds(t * STEPS, STEPS)

                def build():
                    dve.wait_ge(s["agg_done"], t)
                    dve.wait_ge(s["spreadh_ready"], t)
                    dve.tensor_tensor(spread[:, :, :], g.node[:, :].unsqueeze(1).broadcast_to([P, STEPS, P]), wide(g.e_dst[:, at], P), ALU.is_equal).then_inc(s["spread_ready"], 1)
                    dve.wait_ge(messages_in[b], uses_before(t, b) * STEPS + 16 * STEPS)
                    dve.tensor_copy(score[:, :, :], messages[:, b, :, D:D + 4])
                    dve.tensor_copy(first[:, :, :], wide(g.e_first[:, at], 4)).then_inc(s["scores_ready"], 1)

                def scan():
                    dve.wait_ge(s["rows_ready"], t + 1)
                    dve.tensor_tensor_scan(run[:, :], rows_t[:, P:2 * P], rows_t[:, 0:P], -BIG, ALU.add, ALU.max).then_inc(s["run_ready"], 1)

                def last_of_run():
                    dve.wait_ge(s["run_turned"], t + 1)
                    dve.tensor_tensor(run_last[:, :, :], sc_ps[:, 2 * P:2 * P + S4].rearrange("p (j n) -> p j n", j=STEPS), wide(g.e_last[:, at], 4), ALU.mult)
                    dve.tensor_copy(run_h[:, :, 12:13], wide(g.e_last[:, at], 1))
                    dve.drain()
                    split_bf16(dve, [run_h[:, :, 4 * k:4 * k + 4] for k in range(3)], run_last[:, :, :], rest[:, :, :])
                    dve.drain()
                    dve.sem_inc(s["runh_ready"], 1)

                def node_max():
                    dve.wait_ge(s["picked_ready"], t + 1)
                    dve.tensor_tensor(picked_sum[:, :, :], picked[:, :, 0:4], picked[:, :, 4:8], ALU.add)
                    dve.tensor_scalar(absent[:, :, :], picked[:, :, 12:13], -1.0, BIG, ALU.add, ALU.mult)
                    dve.drain()
                    dve.tensor_tensor(picked_sum[:, :, :], picked_sum[:, :, :], picked[:, :, 8:12], ALU.add)
                    dve.drain()
                    dve.tensor_tensor(picked_sum[:, :, :], picked_sum[:, :, :], absent[:, :, :].broadcast_to([P, STEPS, 4]), ALU.add)
                    dve.drain()
                    dve.tensor_reduce(top_src[:, :], picked_sum[:, :, :].rearrange("p j h -> p h j"), AX.X, ALU.max)
                    dve.drain()
                    dve.wait_ge(own_in[b], uses_before(t, b))
                    a_dst = g.a_dst[:, bass.ds(t, 1), :].rearrange("p a n -> p (a n)")
                    dve.tensor_copy(per_node[:, 0:4], a_dst)
                    dve.drain()
                    dve.tensor_tensor(top_src[:, :], top_src[:, :], a_dst, ALU.add)
                    dve.drain()
                    dve.scalar_tensor_tensor(top_src[:, :], top_src[:, :], 0.2, top_src[:, :], ALU.mult, ALU.max)
                    dve.drain()
                    dve.tensor_tensor(per_node[:, 4:8], top_src[:, :], own[:, b, D + 4:D + 8], ALU.max)
                    dve.drain()
                    dve.tensor_tensor(z[:, S4:S4 + 4], own[:, b, D + 4:D + 8], per_node[:, 4:8], ALU.subtract)
                    split_bf16(dve, [node_h[:, k, :] for k in range(3)], per_node[:, :], node_rest[:, :])
                    dve.drain()
                    dve.sem_inc(s["nodeh_ready"], 1)

                def exponents():
                    dve.wait_ge(s["fetched_ready"], t + 1)
                    dve.tensor_tensor(fetched_sum[:, :, :], fetched[:, :, 0:8], fetched[:, :, 8:16], ALU.add)
                    dve.drain()
                    dve.tensor_tensor(fetched_sum[:, :, :], fetched_sum[:, :, :], fetched[:, :, 16:24], ALU.add)
                    dve.drain()
                    dve.tensor_tensor(score[:, :, :], score[:, :, :], fetched_sum[:, :, 0:4], ALU.add)
                    dve.drain()
                    dve.scalar_tensor_tensor(score[:, :, :], score[:, :, :], 0.2, score[:, :, :], ALU.mult, ALU.max)
                    dve.drain()
                    dve.tensor_tensor(score[:, :, :], score[:, :, :], fetched_sum[:, :, 4:8], ALU.subtract)
                    dve.drain()
                    dve.tensor_scalar(z[:, 0:S4], score[:, :, :].rearrange("p j h -> p (j h)"), 0.0, None, ALU.min).then_inc(s["z_ready"], 1)

                def scale():
                    dve.wait_ge(s["ex_ready"], t + 1)
                    for half in range(2):
                        part = slice(half * HALF, half * HALF + HALF)
                        e = ex[:, b, half * HALF * 4:(half + 1) * HALF * 4]
                        features = messages[:, b, part, 0:D].rearrange("p j (h n) -> p j h n", h=4)
                        dve.tensor_tensor(features, features, e.rearrange("p (j h) -> p j h", h=4).unsqueeze(3).broadcast_to([P, HALF, 4, 64]), ALU.mult)
                        dve.tensor_copy(messages[:, b, part, D:D + 4], e.rearrange("p (j h) -> p j h", h=4)).then_inc(s["scaled"], 1)

                def finish():
                    dve.wait_ge(s["agg_done"], t + 1)
                    own_ex = ex[:, b, S4:S4 + 4]
                    dve.tensor_tensor(heads(own[:, b, 0:D]), heads(own[:, b, 0:D]), wide(own_ex, 64), ALU.mult)
                    dve.tensor_tensor(own_den[:, :], own[:, b, D + 8:D + 12], own_ex, ALU.mult)
                    dve.drain()
                    dve.tensor_tensor(den[:, :], agg_ps[:, D:D + 4], own_den[:, :], ALU.add)
                    dve.drain()
                    dve.reciprocal(den[:, :], den[:, :])
                    dve.tensor_tensor(agg[:, :], agg_ps[:, 0:D], own[:, b, 0:D], ALU.add)
                    dve.drain()
                    dve.tensor_tensor(heads(agg[:, :]), heads(agg[:, :]), wide(den[:, :], 64), ALU.mult)
                    dve.drain()
                    dve.tensor_tensor(agg[:, :], agg[:, :], b_gat[:, :], ALU.add)
                    dve.drain()
                    dve.tensor_scalar(gat_neg[:, :], agg[:, :], 0.0, None, ALU.min).then_inc(s["gat_neg"], 1)
                    dve.sem_inc(s["own_free"], 1)

                def elu():
                    dve.wait_ge(s["gat_exp"], t + 1)
                    dve.scalar_tensor_tensor(gat[:, b, :], agg[:, :], 0.0, gat_neg[:, :], ALU.max, ALU.add)
                    dve.drain()
                    dve.tensor_scalar(gat[:, b, :], gat[:, b, :], -1.0, None, ALU.add)
                    dve.drain()
                return {"build": build, "scan": scan, "last_of_run": last_of_run, "node_max": node_max, "exponents": exponents, "scale": scale, "finish": finish, "elu": elu}

            def X(t, b):
                def attend():
                    dve.wait_ge(s["scaled_cat"], t + 1)
                    dve.wait_ge(s["mixedt_ready"], t)
                    dve.wait_ge(s["norm3_ready"], t)
                    q, k, v = cat[:, :, 0:32], cat[:, :, 32:64], cat[:, :, 64:96]
                    dve.tensor_scalar(divisor[:, :, :], v, 1e-15, None, ALU.add)
                    dve.reduce_sum(k_sum[:, :], k, axis=AX.X)
                    dve.drain()
                    dve.reciprocal(divisor[:, :, :], divisor[:, :, :])
                    dve.tensor_tensor(mixed[:, :, :], v, wide(k_sum[:, :], 32), ALU.mult)
                    dve.drain()
                    dve.tensor_tensor(mixed[:, :, :], mixed[:, :, :], q, ALU.mult)
                    dve.drain()
                    dve.tensor_tensor(mixed[:, :, :], mixed[:, :, :], divisor[:, :, :], ALU.mult).then_inc(s["mixed_ready"], 1)

                def tangent():
                    dve.wait_ge(s["res_done"], t + 1)
                    dve.wait_ge(s["scale3_ready"], t + 1)
                    dve.scalar_tensor_tensor(ft[:, :], f_ps[1][:, 0:D], scale3[:, :], b_res[:, :], ALU.mult, ALU.add).then_inc(s["ft_ready"], 1)

                def sum_up():
                    dve.wait_ge(s["tanh_ready"], t + 1)
                    dve.scalar_tensor_tensor(radius4[:, :], tanh4[:, :], MAXNORM, r4[:, :], ALU.min, ALU.mult)
                    dve.tensor_tensor(gat[:, b, :], gat[:, b, :], rows(t), ALU.add)
                    dve.drain()
                    dve.scalar_tensor_tensor(rows(t), ft[:, :], radius4[:, :], gat[:, b, :], ALU.mult, ALU.add)
                    dve.drain()
                    dve.sem_inc(s["x3_ready"], 1)
                return {"attend": attend, "tangent": tangent, "sum_up": sum_up}

            def F(t, b):
                def moments():
                    dve.bn_stats(stats[:, :], rows(t))
                    dve.drain()
                    dve.bn_aggr(mv[:, :], stats[:, :]).then_inc(s["moments_ready"], 1)

                def norm():
                    dve.wait_ge(s["rs_ready"], t + 1)
                    dve.wait_ge(s["xf_turned"], t)
                    dve.tensor_scalar(xf[:, :], rows(t), mv[:, 0:1], rs[:, :], ALU.subtract, ALU.mult)
                    dve.drain()
                    dve.sem_inc(s["xf_ready"], 1)

                def gate_1():
                    dve.wait_ge(s["gates_done"], t + 1)
                    dve.tensor_tensor(gate[:, 0:4], agg_ps[:, 264:268], g_b[:, :], ALU.add)
                    dve.drain()
                    dve.tensor_reduce(gate_m[:, :], gate[:, 0:4], AX.X, ALU.max)
                    dve.drain()
                    dve.tensor_scalar(gate_m[:, :], gate_m[:, :], -1.0, None, ALU.mult).then_inc(s["gate_max"], 1)

                def gate_2():
                    dve.wait_ge(s["gate_exp"], t + 1)
                    dve.reciprocal(gate_s[:, :], gate_s[:, :])
                    dve.drain()
                    dve.tensor_scalar(gate[:, 0:4], gate_e[:, :], gate_s[:, :], None, ALU.mult)
                    dve.drain()
                    dve.max(top[:, :], gate[:, :])
                    dve.drain()
                    dve.tensor_tensor(gap[:, :], top[:, 1:2], top[:, 0:1], ALU.subtract).then_inc(s["gap_ready"], 1)
                    dve.max_index(best[:, :], top[:, :], gate[:, :])
                    dve.drain()
                    dve.tensor_copy(best_f[:, :], best[:, :])

                def gate_3():
                    dve.wait_ge(s["ratio_ready"], t + 1)
                    dve.tensor_scalar(share[:, 0:1], ratio[:, :], 1.0, None, ALU.add)
                    dve.drain()
                    dve.reciprocal(share[:, 0:1], share[:, 0:1])
                    dve.drain()
                    dve.tensor_tensor(share[:, 1:2], share[:, 0:1], ratio[:, :], ALU.mult)
                    dve.drain()
                    dve.tensor_scalar(weight[:, 0:4], g.node[:, 0:4], best_f[:, 0:1], share[:, 0:1], ALU.is_equal, ALU.mult)
                    dve.tensor_scalar(second[:, :], g.node[:, 0:4], best_f[:, 1:2], share[:, 1:2], ALU.is_equal, ALU.mult)
                    dve.drain()
                    dve.tensor_tensor(weight[:, 0:4], weight[:, 0:4], second[:, :], ALU.add).then_inc(s["weight_ready"], 1)

                def outputs():
                    dve.wait_ge(s["expert_done"], t + 1)
                    dve.wait_ge(result_out[b], uses_before(t, b))
                    res = result[:, b, :]
                    dve.tensor_tensor(res, rows(t), f_ps[1][:, 0:D], ALU.add)
                    for e in range(4):
                        dve.drain()
                        dve.scalar_tensor_tensor(res, expert_ps(e), weight[:, e:e + 1], res, ALU.mult, ALU.add)
                    dve.drain()
                    dve.sem_inc(s["expert_used"], 1)
                    dve.sem_inc(s["result_ready"], 1)
                return {"moments": moments, "norm": norm, "gate_1": gate_1, "gate_2": gate_2, "gate_3": gate_3, "outputs": outputs}

            ORDER = ("F.moments X.attend G.build F.norm Z.finish G.scan X.tangent G.last_of_run Z.elu F.gate_1 G.node_max F.gate_2 G.exponents "
                     "F.gate_3 X.sum_up G.scale F.outputs").split()

            def turn(t, b, *on):
                one_turn(ORDER, (G, X, F), t, b, on)
            dve.memset(gate[:, :], -1.0)
            dve.memset(weight[:, 4:5], 1.0)
            dve.sem_inc(s["messages_free"], 2)
            dve.wait_ge(s["weights"], LOADS)
            for c in range(6):
                dve.bn_aggr(bn_mv[:, c, :], g.conv_stats[:, c, :, :].rearrange("p a n -> p (a n)"))
            dve.drain()
            ma, va = bn_mv[:, :, 0], bn_mv[:, :, 1]
            dve.tensor_tensor(bn_t[:, :], ma, ma, ALU.mult)
            dve.drain()
            dve.tensor_scalar(bn_t[:, :], bn_t[:, :], -float(NP) * (NP - N) / float(N) ** 2, EPS, ALU.mult, ALU.add)
            dve.tensor_scalar(va, va, float(NP) / N, None, ALU.mult)
            dve.tensor_scalar(ma, ma, float(NP) / N, None, ALU.mult)
            dve.drain()
            dve.tensor_tensor(bn_t[:, :], bn_t[:, :], va, ALU.add)
            dve.drain()
            newton_rsqrt(dve, bn_a[:, :], bn_t[:, :], bn_b[:, :])
            dve.tensor_tensor(bn_a[:, :], bn_a[:, :], gamma[:, :], ALU.mult)
            dve.drain()
            dve.tensor_tensor(bn_t[:, :], ma, bn_a[:, :], ALU.mult)
            dve.tensor_tensor(w_pw[:, :, :], w_pw[:, :, :], wide(w_dw[:, :], P), ALU.mult)
            dve.drain()
            dve.tensor_tensor(bn_b[:, :], beta[:, :], bn_t[:, :], ALU.subtract)
            dve.drain()
            dve.sem_inc(s["bn_ready"], 1)
            turns(dve, turn)

        @block.tensor
        def _(pe):
            def G(t, b):
                def scores():
                    pe.wait_ge(s["scores_ready"], t + 1)
                    pe.wait_ge(s["fetched_ready"], t)
                    pe.transpose(sc_ps[0:S4, 0:P], score[:, :, :].rearrange("p j h -> p (j h)"), g.ident[:, :])
                    pe.transpose(sc_ps[0:S4, P:2 * P], first[:, :, :].rearrange("p j h -> p (j h)"), g.ident[:, :]).then_inc(s["turned_rows"], 1)

                def turn_spread():
                    pe.wait_ge(s["spreadh_ready"], t + 1)
                    for r in range(3):
                        if r == 0:
                            pe.wait_ge(s["st_copied"], t * 3)
                        if r == 2:
                            pe.wait_ge(s["st_copied"], t * 3 + 1)
                        for j in range(6):
                            last = pe.transpose(st_ps[r % 2][:, j * P:(j + 1) * P], spread_h[:, r * 6 + j, :], ident_h[:, :])
                        last.then_inc(s["st_done"], 1)

                def turn_run():
                    pe.wait_ge(s["run_ready"], t + 1)
                    pe.transpose(sc_ps[:, 2 * P:2 * P + S4], run[:, :], g.ident[0:S4, 0:S4]).then_inc(s["run_turned"], 1)

                def pick():
                    pe.wait_ge(s["spreadh_ready"], t + 1)
                    pe.wait_ge(s["runh_ready"], t + 1)
                    for j in range(STEPS):
                        last = pe.matmul(sc_ps[:, j * 13:(j + 1) * 13], spread_h[:, j, :], run_h[:, j, :], start=True, stop=True)
                    last.then_inc(s["picked_done"], 1)

                def fetch():
                    pe.wait_ge(s["nodeh_ready"], t + 1)
                    pe.wait_ge(s["st_copied"], t * 3 + 3)
                    for j in range(STEPS):
                        last = pe.matmul(sc_ps[:, j * 24:(j + 1) * 24], spread_t[:, j, :], node_h[:, :, :].rearrange("p k n -> p (k n)"), start=True, stop=True)
                    last.then_inc(s["fetched_done"], 1)

                def sums():
                    for half in range(2):
                        pe.wait_ge(s["scaled"], t * 2 + half + 1)
                        if half == 0:
                            pe.wait_ge(s["gat_neg"], t)
                        for j in range(half * HALF, half * HALF + HALF):
                            last = pe.matmul(agg_ps[:, 0:D + 4], spread[:, j, :], messages[:, b, j, 0:D + 4], start=j == 0, stop=j == STEPS - 1)
                    last.then_inc(s["agg_done"], 1)
                    pe.wait_ge(s["agg_done"], t + 1)
                    pe.sem_inc(s["messages_free"], 1)
                return {"scores": scores, "turn_spread": turn_spread, "turn_run": turn_run, "pick": pick, "fetch": fetch, "sums": sums}

            def X(t, b):
                def lift():
                    pe.wait_ge(s["h_in"], t + 1)
                    if not (isinstance(t, int) and t < 2):
                        pe.wait_ge(s["expert_used"], t - 2)
                        pe.wait_ge(s["xft_ready"], t - 1)
                    for r in range(2):
                        pe.wait_ge(s["m_copied"], t * 2 + r)
                        for c in range(3):
                            pe.transpose(m_ps[0][:, c * P:(c + 1) * P], conv_in[:, b, r * 3 + c, :], g.ident[:, :])
                        for c in range(3):
                            last = pe.matmul(m_ps[1][:, c * P:(c + 1) * P], conv_in[:, b, r * 3 + c, :], w_pw[:, r * 3 + c, :], start=True, stop=True)
                        last.then_inc(s["m_done"], 1)
                    pe.wait_ge(s["m_done"], t * 2 + 2)
                    pe.sem_inc(s["lifted"], 1)

                def turn_mixed():
                    pe.wait_ge(s["mixed_ready"], t + 1)
                    if not (isinstance(t, int) and t < 1):
                        pe.wait_ge(s["expert_used"], t - 1)
                    for c in range(4):
                        last = pe.transpose(f_ps[0][:, c * P:(c + 1) * P], mixed[:, c * 4:c * 4 + 4, :].rearrange("p a n -> p (a n)"), g.ident[:, :])
                    last.then_inc(s["mixed_turned"], 1)

                def residual():
                    pe.wait_ge(s["mixedt_ready"], t + 1)
                    for c in range(4):
                        last = pe.matmul(f_ps[1][:, 0:D], mixed_t[:, c, :], w_res[:, c, :], start=c == 0, stop=c == 3)
                    last.then_inc(s["res_done"], 1)
                return {"lift": lift, "turn_mixed": turn_mixed, "residual": residual}

            def F(t, b):
                def of_next(value, most):
                    return min(value, most) if isinstance(t, int) else value

                def turned():
                    pe.wait_ge(s["xf_ready"], t + 1)
                    pe.wait_ge(s["m_copied"], of_next(2 * t + 4, 2 * T))
                    for c in range(2):
                        last = pe.transpose(m_ps[0][:, c * P:(c + 1) * P], xf[:, c * P:(c + 1) * P], g.ident[:, :])
                    last.then_inc(s["xf_turned"], 1)

                def layer_1():
                    pe.wait_ge(s["xft_ready"], t + 1)
                    pe.wait_ge(s["mixedt_ready"], of_next(t + 2, T))
                    pe.wait_ge(s["ft_ready"], of_next(t + 2, T))
                    pe.wait_ge(s["gat_neg"], of_next(t + 2, T))
                    for c in range(2):
                        last = pe.matmul(agg_ps[:, 264:268], xf_t[:, c, :], g_w[:, c, :], start=c == 0, stop=c == 1)
                    last.then_inc(s["gates_done"], 1)
                    for o in range(2):
                        for c in range(2):
                            pe.matmul(f_ps[1][:, o * P:(o + 1) * P], s_w1[:, c, o * P:(o + 1) * P], xf_t[:, c, :], start=c == 0, stop=c == 1)
                    for e in range(4):
                        for c in range(2):
                            last = pe.matmul(f_ps[0][:, e * P:(e + 1) * P], x_w1[:, e, c, :], xf_t[:, c, :], start=c == 0, stop=c == 1)
                    last.then_inc(s["hidden1"], 1)

                def layer_2():
                    pe.wait_ge(s["hidden1_ready"], t + 1)
                    for c in range(2):
                        pe.matmul(f_ps[1][:, 0:P], s_w2[:, c, :], hid_s[:, c, :], start=c == 0, stop=c == 1)
                    for e in range(4):
                        last = pe.matmul(f_ps[0][0:64, e * P:(e + 1) * P], x_w2[:, e, :], hid_x[:, e, :], start=True, stop=True)
                    last.then_inc(s["hidden2"], 1)

                def weights():
                    pe.wait_ge(s["m_copied"], of_next(2 * t + 6, 2 * T))
                    pe.wait_ge(s["weight_ready"], t + 1)
                    pe.transpose(m_ps[0][0:5, 0:P], weight[:, :], g.ident[:, :]).then_inc(s["weight_turned"], 1)

                def outputs():
                    pe.wait_ge(s["hidden2_ready"], t + 1)
                    pe.wait_ge(s["weightt_ready"], t + 1)
                    pe.matmul(f_ps[1][:, 0:D], hid_s2[:, :], s_w3[:, :], start=True, stop=False)
                    pe.matmul(f_ps[1][:, 0:D], weight_t[:, :], out_b[:, :], start=False, stop=True)
                    for e in range(4):
                        last = pe.matmul(expert_ps(e), hid_x2[:, e, :], x_w3[:, e, :], start=True, stop=True)
                    last.then_inc(s["expert_done"], 1)
                return {"turned": turned, "layer_1": layer_1, "layer_2": layer_2, "weights": weights, "outputs": outputs}

            ORDER = ("X.turn_mixed X.residual G.scores F.turned G.turn_run G.turn_spread G.pick F.layer_1 G.fetch Y.lift F.layer_2 F.weights "
                     "F.outputs G.sums").split()

            def turn(t, b, *on):
                one_turn(ORDER, (G, X, F), t, b, on)
            pe.wait_ge(s["weights"], LOADS)
            turns(pe, turn)


WEIGHTS = ['L0_gnn_weight', 'L0_gnn_bias', 'L0_mix_Wq', 'L0_mix_bq', 'L0_mix_Wk', 'L0_mix_bk', 'L0_mix_Wv', 'L0_mix_bv',
           'L0_mix_Wo', 'L0_mix_bo', 'L0_mix_W1', 'L0_mix_b1', 'L0_mix_W2', 'L0_mix_b2', 'L0_mix_ln1_g', 'L0_mix_ln1_b',
           'L0_mix_ln2_g', 'L0_mix_ln2_b', 'L0_ffn_gamma', 'L0_ffn_beta', 'L0_ffn_Wr', 'L0_ffn_br', 'L0_ffn_W1',
           'L0_ffn_b1', 'L0_ffn_W2', 'L0_ffn_b2', 'L1_gnn_W', 'L1_gnn_att_src', 'L1_gnn_att_dst', 'L1_gnn_bias',
           'L1_mix_w_qkv', 'L1_mix_bn_gamma', 'L1_mix_bn_beta', 'L1_mix_w_dw', 'L1_mix_w_pw', 'L1_mix_w_res',
           'L1_mix_b_res', 'L1_ffn_sW1', 'L1_ffn_sb1', 'L1_ffn_sW2', 'L1_ffn_sb2', 'L1_ffn_sW3', 'L1_ffn_sb3',
           'L1_ffn_eW1', 'L1_ffn_eb1', 'L1_ffn_eW2', 'L1_ffn_eb2', 'L1_ffn_eW3', 'L1_ffn_eb3', 'L1_ffn_gW', 'L1_ffn_gb']
TURNED = {'L1_mix_w_qkv': (1, 2, 0), 'L1_mix_w_dw': (1, 2, 0), 'L1_mix_w_pw': (1, 2, 0), 'L1_mix_w_res': (1, 2, 0)}


def build(nc, g):
    with ExitStack() as ctx:
        sb = lambda n, s, d=F32: ctx.enter_context(nc.sbuf_tensor(n, s, d))
        g.messages_in = [ctx.enter_context(nc.semaphore("messages_in" + str(i))) for i in range(6)]
        g.ident = sb("ident", [P, P])
        g.node = sb("node", [P, P])
        g.starts = sb("starts", [P, T + 1], I32)
        g.general = sb("general", [P, 1], I32)
        g.marker = sb("marker", [P, 1])
        g.e_src = sb("e_src", [P, T * STEPS], I32)
        g.e_dst, g.e_weight, g.e_last, g.e_first = (sb("e_" + n, [P, T * STEPS]) for n in ("dst", "weight", "last", "first"))
        g.xn = sb("nodes", [P, T, D])
        g.sup_table = nc.dram_tensor("sup_table", [NP, D], F32).ap()
        g.x_mean, g.x_rstd, g.x_var = sb("x_mean", [P, T]), sb("x_rstd", [P, T]), sb("x_var", [P, T])
        g.x_plus = nc.dram_tensor("x_plus", [NP, D], F32).ap()
        g.att_table = nc.dram_tensor("att_table", [NP, TBL], F32).ap()
        g.conv = nc.dram_tensor("conv", [T, CQ, P], F32).ap()
        build_edge_tables(nc, g)
        with ExitStack() as c2:
            sb2 = lambda n, s, d=F32: c2.enter_context(nc.sbuf_tensor(n, s, d))
            g.q_phi = sb2("q_phi", [P, 2, NP])
            g.kv, g.ksum = sb2("kv", [P, 2, P]), sb2("ksum", [P, 2, P])
            layer0_projections(nc, g)
            g.clear_semaphores(nc)
            layer0_edges_of_any_order(nc, g)
            layer0_graph_and_attention(nc, g)
        layer0_experts(nc, g)
        g.a_dst = sb("a_dst", [P, T, 4])
        g.conv_stats = sb("conv_stats", [P, 6, T, 6])
        layer1_projections(nc, g)
        g.clear_semaphores(nc)
        layer1_edges_of_any_order(nc, g)
        layer1_outputs(nc, g)


def declare(nc, g, arrays):
    g.w = {name: nc.dram_tensor(name, a.shape, mybir.dt.from_np(a.dtype), kind="ExternalInput").ap() for name, a in arrays.items()}
    g.x, g.src, g.dst, g.ew = g.w["x"], g.w["src"], g.w["dst"], g.w["ew"]
    g.out = nc.dram_tensor("out", (NP, D), F32, kind="ExternalOutput").ap()


def lay_out(inputs):
    arrays = {}
    x = np.zeros((NP, D), np.float32)
    x[:N] = inputs["x"]
    src = np.zeros((EPAD,), np.int32)
    src[:EDGES] = inputs["src"]
    dst = np.full((EPAD,), NODES_OF_EDGES_PAD, np.int32)
    dst[:EDGES] = inputs["dst"]
    ew = np.zeros((EPAD,), np.float32)
    ew[:EDGES] = inputs["edge_weight"]
    arrays.update(x=x, src=src, dst=dst, ew=ew)
    for name in WEIGHTS:
        a = np.asarray(inputs[name])
        arrays[name] = np.ascontiguousarray(a.transpose(TURNED[name]) if name in TURNED else a)
    return arrays


def kernel(**inputs):
    import concourse.bacc as bacc
    from concourse.bass_utils import run_bass_kernel_spmd

    nc = bacc.Bacc("TRN2", target_bir_lowering=False, num_devices=1)
    arrays = lay_out(inputs)
    g = Ctx()
    declare(nc, g, arrays)
    build(nc, g)
    r = run_bass_kernel_spmd(nc, [arrays], core_ids=[0])
    return r.results[0]["out"][:N]
```
